# Optimizing a Trainium2 kernel written in Bass

```python
import numpy as np
import jax
import jax.numpy as jnp

def _softmax(x, axis=-1):
    return jax.nn.softmax(x, axis=axis)

def _gelu(x):
    return jax.nn.gelu(x, approximate=True)

def _silu(x):
    return jax.nn.silu(x)

def _sigmoid(x):
    return jax.nn.sigmoid(x)

def _layernorm(x, axis=-1, eps=1e-05):
    m = jnp.mean(x, axis=axis, keepdims=True)
    v = jnp.var(x, axis=axis, keepdims=True)
    return (x - m) / jnp.sqrt(v + eps)

def _scatter_add(tgt, idx, src, axis=0):
    return tgt.at[idx].add(src)

def _segment_sum(src, seg, n):
    return jax.ops.segment_sum(src, seg, n)
kernel_name = 'mk_gnn_resnorm_d2_gnn_r8_074746'

def setup_inputs(seed: int=0):
    np.random.seed(seed)
    _w = jnp.asarray

    def _rec_inputs():
        import jax
        import jax.numpy as jnp
        _gk = jax.random.key(seed)
        x = -0.0006008 + 1.001 * jax.random.normal(jax.random.fold_in(_gk, 1), (6250, 128), jnp.float32)
        src = jax.random.randint(jax.random.fold_in(_gk, 2), (200000,), 0, 6250, jnp.int32)
        dst = jax.random.randint(jax.random.fold_in(_gk, 3), (200000,), 0, 6250, jnp.int32)
        _o = jnp.argsort(dst, stable=True)
        src = src[_o]
        dst = dst[_o]
        return (x, src, dst)
    x, src, dst = _rec_inputs()

    def _L0_gnn_setup():
        import jax, jax.numpy as jnp
        import numpy as np
        N_NODES = 2500
        N_EDGES = 80000
        CHANNEL = 128
        LEAKY_ALPHA = 0.2
        key = jax.random.key(seed)
        k_h, k_w, k_a, k_s, k_d = jax.random.split(key, 5)
        C = CHANNEL
        h = jax.random.normal(k_h, (N_NODES, C), dtype=jnp.float32)
        w = jax.random.normal(k_w, (2 * C, C), dtype=jnp.float32) * np.sqrt(2.0 / (3 * C))
        a = jax.random.normal(k_a, (C, 1), dtype=jnp.float32) * np.sqrt(2.0 / (C + 1))
        src = jax.random.randint(k_s, (N_EDGES,), 0, N_NODES, dtype=jnp.int32)
        dst = jax.random.randint(k_d, (N_EDGES,), 0, N_NODES, dtype=jnp.int32)
        return {'h': h, 'w': w, 'a': a, 'src': src, 'dst': dst}
    _L0_gnn_all = _L0_gnn_setup()
    _L0_gnn_in = {k: v for k, v in _L0_gnn_all.items() if k in ('w', 'a')}
    del _L0_gnn_all

    def _L1_gnn_setup():
        import jax, jax.numpy as jnp
        import numpy as np
        N = 12500
        E = 200000
        IN_DIM = 128
        HEADS = 4
        OUT_DIM = 32
        ALPHA = 0.2
        EPS = 1e-08
        key = jax.random.key(seed)
        k1, k2, k3, k4, k5, k6 = jax.random.split(key, 6)
        x = jax.random.normal(k1, (N, IN_DIM), dtype=jnp.float32)
        edge_index = jax.random.randint(k2, (2, E), 0, N, dtype=jnp.int64)
        W = jax.random.normal(k3, (IN_DIM, HEADS * OUT_DIM), dtype=jnp.float32) * (2.0 / IN_DIM) ** 0.5
        A_left = jax.random.normal(k4, (HEADS, OUT_DIM, 1), dtype=jnp.float32) * (2.0 / OUT_DIM) ** 0.5
        A_right = jax.random.normal(k5, (HEADS, OUT_DIM, 1), dtype=jnp.float32) * (2.0 / OUT_DIM) ** 0.5
        residual_projection = jax.random.normal(k6, (IN_DIM, HEADS * OUT_DIM), dtype=jnp.float32) * (2.0 / IN_DIM) ** 0.5
        return {'x': x, 'edge_index': edge_index, 'W': W, 'A_left': A_left, 'A_right': A_right, 'residual_projection': residual_projection}
    _L1_gnn_all = _L1_gnn_setup()
    _L1_gnn_in = {k: v for k, v in _L1_gnn_all.items() if k in ('W', 'A_left', 'A_right', 'residual_projection')}
    del _L1_gnn_all
    return {'x': x, 'src': src, 'dst': dst, 'L0_gnn_w': _L0_gnn_in['w'], 'L0_gnn_a': _L0_gnn_in['a'], 'L1_gnn_W': _L1_gnn_in['W'], 'L1_gnn_A_left': _L1_gnn_in['A_left'], 'L1_gnn_A_right': _L1_gnn_in['A_right'], 'L1_gnn_residual_projection': _L1_gnn_in['residual_projection']}

def reference(x, src, dst, L0_gnn_w, L0_gnn_a, L1_gnn_W, L1_gnn_A_left, L1_gnn_A_right, L1_gnn_residual_projection):
    import jax
    import jax.numpy as jnp

    def _L0_gnn_ref(h, w, a, src, dst):
        import jax, jax.numpy as jnp
        import numpy as np
        N_NODES = 2500
        N_EDGES = 80000
        CHANNEL = 128
        LEAKY_ALPHA = 0.2
        N = h.shape[0]
        hi = h[src]
        hj = h[dst]
        hij = jnp.concatenate([hi, hj], axis=-1)
        e = jnp.matmul(jax.nn.leaky_relu(jnp.matmul(hij, w), LEAKY_ALPHA), a)
        exp_e = jnp.exp(e)
        denom = jax.ops.segment_sum(exp_e, src, num_segments=N)
        att = exp_e / denom[src]
        out = jax.ops.segment_sum(hi * att, dst, num_segments=N)
        return out

    def _L1_gnn_ref(x, edge_index, W, A_left, A_right, residual_projection):
        import jax, jax.numpy as jnp
        import numpy as np
        N = 12500
        E = 200000
        IN_DIM = 128
        HEADS = 4
        OUT_DIM = 32
        ALPHA = 0.2
        EPS = 1e-08
        n = x.shape[0]
        H = jnp.matmul(x, W).reshape(n, HEADS, OUT_DIM).transpose(1, 0, 2)
        H_s = jnp.einsum('hnd,hd->hn', H, A_left[..., 0])
        H_t = jnp.einsum('hnd,hd->hn', H, A_right[..., 0])
        src = edge_index[0]
        tgt = edge_index[1]
        s = H_s[:, src] + H_t[:, tgt]
        s = jnp.where(s >= 0, s, ALPHA * s)
        s = jnp.exp(s - jnp.max(s))
        denom = jnp.zeros((HEADS, n), dtype=s.dtype).at[:, src].add(s)
        alpha = s / (denom[:, src] + EPS)
        H_sf = H[:, tgt]
        agg = jnp.zeros((HEADS, n, OUT_DIM), dtype=H.dtype).at[:, src].add(alpha[..., None] * H_sf)
        agg = agg + jnp.matmul(x, residual_projection).reshape(n, HEADS, OUT_DIM).transpose(1, 0, 2)
        res = agg.transpose(1, 0, 2).reshape(n, HEADS * OUT_DIM)
        return jax.nn.elu(res)
    edge_index = jnp.stack([src, dst])
    x = _layernorm(x + _L0_gnn_ref(x, L0_gnn_w, L0_gnn_a, src, dst), axis=-1)
    x = _layernorm(x + _L1_gnn_ref(x, edge_index, L1_gnn_W, L1_gnn_A_left, L1_gnn_A_right, L1_gnn_residual_projection), axis=-1)
    return x

_drawn_inputs = setup_inputs


def setup_inputs(seed=0):
    import zlib

    import numpy as np

    out = dict(_drawn_inputs(seed))
    spreads = {}
    factors = {}
    for name, (base, spread) in spreads.items():
        noise = np.random.default_rng([zlib.crc32(name.encode()), seed]).standard_normal(out[name].shape)
        drawn = base * np.exp(spread * noise) if base else spread * noise
        out[name] = jnp.asarray(drawn.astype(out[name].dtype))
    for name, factor in factors.items():
        out[name] = (out[name] * factor).astype(out[name].dtype)
    return out
```

```python
from contextlib import ExitStack

import concourse.bass as bass
from concourse import mybir

F32 = mybir.dt.float32
I32 = mybir.dt.int32
U32 = mybir.dt.uint32
ALU = mybir.AluOpType
ACT = mybir.ActivationFunctionType
AX = mybir.AxisListType
RMAX = bass.bass_isa.ReduceOp.max

P = 128
C = 128
HEADS = 4
D = C // HEADS
ALPHA = 0.2
LN_EPS = 1e-5
SM_EPS = 1e-8

EP = 125
G = 8
COPIES = 4


def gnn_program(nc, x, src, dst, w0, a0, w1, a_left, a_right, w_res, out):
    N = x.shape[0]
    E = src.shape[0]
    T = E // EP
    ITERS = T // (2 * G)
    assert T * EP == E and ITERS * 2 * G == T
    NB = 2 * (-(-N // (2 * P)))
    NFULL, NREST = N // P, N % P
    NP = NB * P
    DUMMY = NP
    HI = NB

    p_tab = nc.dram_tensor("p_tab", (NP, C), F32, kind="Internal").ap()
    q_tab = nc.dram_tensor("q_tab", (NP, C), F32, kind="Internal").ap()
    xs_tab = nc.dram_tensor("xs_tab", (NP, C), F32, kind="Internal").ap()
    h_tab = nc.dram_tensor("h_tab", (NP, C), F32, kind="Internal").ap()
    st_tab = nc.dram_tensor("st_tab", (NP, 2 * HEADS), F32, kind="Internal").ap()
    acc_tabs = [[nc.dram_tensor(f"acc{l}_{k}", (NP + P, C), F32, kind="Internal").ap() for k in range(COPIES)]
                for l in range(2)]

    def blocks(table):
        return table[0:NP].rearrange("(b p) c -> p b c", p=P)

    with ExitStack() as ctx:
        def sb(name, shape, dt=F32):
            return ctx.enter_context(nc.sbuf_tensor(name, shape, dt))

        def ps(name, shape, dt=F32):
            return ctx.enter_context(nc.psum_tensor(name, shape, dt))

        def sem(name):
            return ctx.enter_context(nc.semaphore(name))

        turns = sem("pool_turns")

        iota_i = sb("iota_i", [P, P], I32)
        part_i = sb("part_i", [P, 1], I32)
        iota = sb("iota", [P, P])
        part = sb("part", [P, 1])
        ident = sb("ident", [P, P])
        below = sb("below", [P, P])
        ones = sb("one_mat", [P, P])
        dummy = sb("dummy_rows", [P, 1])
        a_row = sb("a_row", [P, C])
        w0_sb = sb("w0_sb", [P, 2, C])
        w1_sb = sb("w1_sb", [P, C])
        w1_t = sb("w1_t", [P, C])
        wres_sb = sb("wres_sb", [P, C])
        al_col = sb("al_col", [P, 2])
        headmask = sb("headmask", [P, HEADS])
        hm_i = sb("hm_i", [P, 2], I32)
        hm_f = sb("hm_f", [P, 2])
        al_blk = sb("al_blk", [P, 2 * HEADS])
        w1_all = sb("w1_all", [P, 2 * C + 2 * HEADS])
        X = sb("X", [P, NB, C])
        S = sb("S", [P, NB, C])
        R = sb("R", [P, NB, C])
        den = sb("den", [P, HEADS * HI])
        rden = sb("rden", [P, HEADS * HI])
        stat = sb("stat", [P, NB])
        stat2 = sb("stat2", [P, NB])
        src_i = sb("src_i", [P, T], I32)
        dst_i = sb("dst_i", [P, T], I32)
        lo_i = sb("lo_i", [P, T], I32)
        lo_f = sb("lo_f", [P, T])
        hi_f = sb("hi_f", [P, T])
        e0 = sb("e0", [P, T])
        s1 = sb("s1", [P, T, HEADS])
        gmax = sb("gmax", [P, 2])
        idx_a = sb("idx_a", [P, 2, G], U32)
        idx_b = sb("idx_b", [P, 2, G], U32)
        ga = sb("ga", [P, 2, G, C])
        gb = sb("gb", [P, 2, G, C])
        wk = sb("wk", [P, G, C])
        wk2 = sb("wk2", [P, G, C])
        wk3 = sb("wk3", [P, G, C])
        oh = sb("oh", [P, 2, 4, P])
        ohw = sb("ohw", [P, 2, 4, HEADS * HI])
        key_f = sb("key_f", [P, G])
        dup = sb("dup", [P, G])
        dmy = sb("dmy", [P, G])
        xt = sb("xt", [P, 2, C])
        nstage = sb("nstage", [P, 2, 2 * C + 2 * HEADS])

        bank_a = ps("bank_a", [P, 2, 512])
        bank_b = ps("bank_b", [P, 2, 512])
        bank_c = ps("bank_c", [P, 512])

        ld = sem("loaded")
        zeroed = sem("x_pad_zeroed")
        io = sem("iota_ready")
        cst = sem("constants_chain")
        wt_ready = sem("w1_transposed")
        wt_sb = sem("w1_transposed_in_sbuf")
        wa_ready = sem("w1_attention_product")
        zsem = sem("accumulators_zeroed")
        with nc.Block() as block:
            @block.sync
            def _(sp):
                sp.dma_start(w0_sb[:], w0.rearrange("(t c) o -> c t o", t=2)).then_inc(ld, 16)
                sp.dma_start(w1_sb[:], w1).then_inc(ld, 16)
                sp.dma_start(wres_sb[:], w_res).then_inc(ld, 16)
                sp.dma_start(a_row[:], a0.rearrange("c o -> (c o)").partition_broadcast(P)).then_inc(ld, 16)
                sp.dma_start(al_col[:, 0:1], a_left.rearrange("h d o -> (h d) o")).then_inc(ld, 16)
                sp.dma_start(al_col[:, 1:2], a_right.rearrange("h d o -> (h d) o")).then_inc(ld, 16)
                sp.dma_start(src_i[0:EP, :], src.rearrange("(p t) -> p t", p=EP)).then_inc(ld, 16)
                sp.dma_start(dst_i[0:EP, :], dst.rearrange("(p t) -> p t", p=EP)).then_inc(ld, 16)
                sp.dma_start(X[:, 0:NFULL, :], x[0:NFULL * P].rearrange("(b p) c -> p b c", p=P)).then_inc(ld, 16)
                sp.wait_ge(zeroed, 1)
                sp.dma_start(X[0:NREST, NFULL, :], x[NFULL * P:N]).then_inc(ld, 16)
                sp.wait_ge(ld, 160)

            @block.gpsimd
            def _(pool):
                nc.gpsimd.iota(iota_i[:], [[1, P]], base=0, channel_multiplier=0).then_inc(io, 1)
                nc.gpsimd.iota(part_i[:], [[1, 1]], base=0, channel_multiplier=1).then_inc(io, 1)

            @block.scalar
            def _(act):
                act.wait_ge(zeroed, 2)
                for l in range(2):
                    for k in range(COPIES):
                        act.dma_start(blocks(acc_tabs[l][k]), S[:]).then_inc(zsem, 16)
                act.wait_ge(zsem, 16 * 2 * COPIES)

            @block.vector
            def _(dve):
                count = [0]

                def link(ins):
                    count[0] += 1
                    ins.then_inc(cst, 1)
                    dve.wait_ge(cst, count[0])

                nc.vector.memset(X[:, NFULL:NB, :], 0.0).then_inc(zeroed, 1)
                nc.vector.memset(S[:], 0.0).then_inc(zeroed, 1)
                nc.vector.memset(ones[:], 1.0)
                dve.wait_ge(io, 2)
                nc.vector.tensor_copy(iota[:], iota_i[:])
                link(nc.vector.tensor_copy(part[:], part_i[:]))
                nc.vector.tensor_scalar(ident[:], iota[:], part[:, 0:1], None, ALU.is_equal)
                nc.vector.tensor_scalar(below[:], iota[:], part[:, 0:1], None, ALU.is_lt)
                nc.vector.tensor_scalar(dummy[:], part[:], float(DUMMY), None, ALU.add)
                link(nc.vector.tensor_scalar(hm_i[:, 0:1], part_i[:], D.bit_length() - 1, None,
                                             ALU.logical_shift_right))
                link(nc.vector.tensor_copy(hm_f[:, 0:1], hm_i[:, 0:1]))
                link(nc.vector.tensor_scalar(headmask[:], iota[:, 0:HEADS], hm_f[:, 0:1], None, ALU.is_equal))
                dve.wait_ge(ld, 160)
                nc.vector.tensor_scalar(al_blk[:, 0:HEADS], headmask[:], al_col[:, 0:1], None, ALU.mult)
                nc.vector.tensor_scalar(al_blk[:, HEADS:], headmask[:], al_col[:, 1:2], None, ALU.mult)
                nc.vector.tensor_copy(w1_all[:, 0:C], w1_sb[:])
                link(nc.vector.tensor_copy(w1_all[:, C:2 * C], wres_sb[:]))
                dve.wait_ge(wt_ready, 1)
                nc.vector.tensor_copy(w1_t[:], bank_c[:, 0:C]).then_inc(wt_sb, 1)
                dve.wait_ge(wa_ready, 1)
                nc.vector.tensor_copy(w1_all[:, 2 * C:], bank_c[:, 0:2 * HEADS])

            @block.tensor
            def _(pe):
                pe.wait_ge(cst, 5)
                nc.tensor.transpose(bank_c[:, 0:C], w1_sb[:], ident[:]).then_inc(wt_ready, 1)
                pe.wait_ge(wt_sb, 1)
                nc.tensor.matmul(bank_c[:, 0:2 * HEADS], w1_t[:], al_blk[:], start=True, stop=True).then_inc(wa_ready, 1)

        def project(tag, weights, width, stores):
            x_t, x_sb, prod, staged, stored = (sem(f"{tag}_{n}") for n in
                                               ("transposed", "transposed_in_sbuf", "product", "staged", "stored"))
            stored = [stored, sem(f"{tag}_stored1")]
            nstores = len(stores)
            with nc.Block() as block:
                @block.tensor
                def _(pe):
                    for b in range(NB):
                        h = b % 2
                        if b >= 2:
                            pe.wait_ge(x_sb, b - 1)
                        nc.tensor.transpose(bank_a[:, h, 0:C], X[:, b, :], ident[:]).then_inc(x_t, 1)
                        pe.wait_ge(x_sb, b + 1)
                        if b >= 2:
                            pe.wait_ge(staged, b - 1)
                        nc.tensor.matmul(bank_b[:, h, 0:width], xt[:, h, :], weights, start=True,
                                         stop=True).then_inc(prod, 1)

                @block.vector
                def _(dve):
                    for b in range(NB):
                        h = b % 2
                        dve.wait_ge(x_t, b + 1)
                        if b >= 2:
                            dve.wait_ge(prod, b - 1)
                        nc.vector.tensor_copy(xt[:, h, :], bank_a[:, h, 0:C]).then_inc(x_sb, 1)

                @block.scalar
                def _(act):
                    for b in range(NB):
                        h = b % 2
                        act.wait_ge(prod, b + 1)
                        if b >= 2:
                            act.wait_ge(stored[h], 16 * nstores * (b // 2))
                        nc.scalar.copy(nstage[:, h, 0:width], bank_b[:, h, 0:width]).then_inc(staged, 1)

                @block.sync
                def _(sp):
                    for b in range(NB):
                        h = b % 2
                        sp.wait_ge(staged, b + 1)
                        for dest, lo, hi in stores:
                            sp.dma_start(dest(b), nstage[:, h, lo:hi]).then_inc(stored[h], 16)
                    for h in range(2):
                        sp.wait_ge(stored[h], 16 * nstores * (NB // 2))

        def rows(table):
            return lambda b: table[b * P:(b + 1) * P]

        project("proj0", w0_sb[:].rearrange("c t o -> c (t o)"), 2 * C, [(rows(p_tab), 0, C), (rows(q_tab), C, 2 * C)])

        def scores(tag, tab_a, tab_b, width, lo_b, combine, steps):
            idx_ready = [sem(f"{tag}_idx{h}") for h in range(2)]
            gathered = [sem(f"{tag}_gathered{h}") for h in range(2)]
            used = [sem(f"{tag}_used{h}") for h in range(2)]
            chain = sem(f"{tag}_chain")
            PER = 16 * 2 * G

            with nc.Block() as block:
                @block.scalar
                def _(act):
                    with act.Fori(0, ITERS) as it:
                        for h in range(2):
                            act.wait_ge(used[h], it + 1)
                            t0 = it * (2 * G) + h * G
                            nc.scalar.copy(idx_a[0:EP, h, :], src_i[0:EP, bass.ds(t0, G)]).then_inc(idx_ready[h], 1)
                            nc.scalar.copy(idx_b[0:EP, h, :], dst_i[0:EP, bass.ds(t0, G)]).then_inc(idx_ready[h], 1)

                @block.gpsimd
                def _(pool):
                    with pool.Fori(0, ITERS) as it:
                        for h in range(2):
                            pool.wait_ge(idx_ready[h], it * 2 + 2)
                            pool.wait_ge(used[h], it + 1)
                            pool.sem_inc(turns, 1)
                            for k in range(G):
                                pool.indirect_dma_start(
                                    out=ga[0:EP, h, k, 0:width], out_offset=None, in_=tab_a,
                                    in_offset=bass.IndirectOffsetOnAxis(ap=idx_a[0:EP, h, k:k + 1], axis=0),
                                ).then_inc(gathered[h], 16)
                                pool.indirect_dma_start(
                                    out=gb[0:EP, h, k, 0:width], out_offset=None, in_=tab_b,
                                    in_offset=bass.IndirectOffsetOnAxis(ap=idx_b[0:EP, h, k:k + 1], axis=0),
                                ).then_inc(gathered[h], 16)

                @block.vector
                def _(dve):
                    for h in range(2):
                        dve.sem_inc(used[h], 1)
                    with dve.Fori(0, ITERS) as it:
                        for h in range(2):
                            dve.wait_ge(gathered[h], (it + 1) * PER)
                            dve.wait_ge(used[1 - h], it + h + 1)
                            done = [0]

                            def link(ins):
                                done[0] += 1
                                ins.then_inc(chain, 1)
                                dve.wait_ge(chain, it * (2 * steps) + (h * steps + done[0]))

                            last = combine(link, h, it * (2 * G) + h * G)
                            last.then_inc(used[h], 1)
                            assert done[0] == steps

        def combine0(link, h, t0):
            a, b = ga[0:EP, h], gb[0:EP, h]
            link(nc.vector.tensor_tensor(wk[0:EP], a, b, ALU.add))
            link(nc.vector.scalar_tensor_tensor(out=wk2[0:EP], in0=wk[0:EP], scalar=ALPHA, in1=wk[0:EP],
                                                op0=ALU.mult, op1=ALU.max))
            link(nc.vector.tensor_tensor(wk[0:EP], wk2[0:EP], a_row[0:EP, :].unsqueeze(1).to_broadcast([EP, G, C]),
                                         ALU.mult))
            return nc.vector.tensor_reduce(e0[0:EP, bass.ds(t0, G)], wk[0:EP], AX.X, ALU.add)

        scores("score0", p_tab, q_tab, C, 0, combine0, 3)

        def denominators(tag, weight, heads, prep_act):
            ready = sem(f"{tag}_weights_ready")
            idxf = sem(f"{tag}_index_parts")
            hot = [sem(f"{tag}_onehot{h}") for h in range(2)]
            taken = [sem(f"{tag}_taken{h}") for h in range(2)]
            chain = sem(f"{tag}_chain")
            opened = sem(f"{tag}_opened")
            closed = sem(f"{tag}_closed")
            K = 4
            L = T // (2 * K)
            W = heads * HI
            with nc.Block() as block:
                @block.scalar
                def _(act):
                    prep_act(act).then_inc(ready, 1)

                @block.vector
                def _(dve):
                    nc.vector.tensor_scalar(lo_i[0:EP], src_i[0:EP], P - 1, None, ALU.bitwise_and).then_inc(chain, 1)
                    dve.wait_ge(chain, 1)
                    nc.vector.tensor_copy(lo_f[0:EP], lo_i[0:EP]).then_inc(chain, 1)
                    dve.wait_ge(chain, 2)
                    nc.vector.tensor_scalar(lo_i[0:EP], src_i[0:EP], 7, None, ALU.logical_shift_right).then_inc(chain, 1)
                    dve.wait_ge(chain, 3)
                    nc.vector.tensor_copy(hi_f[0:EP], lo_i[0:EP]).then_inc(chain, 1)
                    dve.wait_ge(chain, 4)
                    dve.wait_ge(ready, 1)
                    for h in range(2):
                        dve.sem_inc(hot[h], 1)
                    with dve.Fori(0, L) as it:
                        for h in range(2):
                            t0 = it * (2 * K) + h * K
                            dve.wait_ge(taken[h], it + 1)
                            dve.wait_ge(hot[1 - h], it + h + 1)
                            nc.vector.tensor_tensor(
                                oh[0:EP, h], iota[0:EP].unsqueeze(1).to_broadcast([EP, K, P]),
                                lo_f[0:EP, bass.ds(t0, K)].unsqueeze(2).to_broadcast([EP, K, P]), ALU.is_equal)
                            v = wk[0:EP].rearrange("p g c -> p (g c)")[:, 0:K * HI].rearrange("p (k n) -> p k n", k=K)
                            nc.vector.tensor_tensor(
                                v, iota[0:EP, 0:HI].unsqueeze(1).to_broadcast([EP, K, HI]),
                                hi_f[0:EP, bass.ds(t0, K)].unsqueeze(2).to_broadcast([EP, K, HI]),
                                ALU.is_equal).then_inc(chain, 1)
                            dve.wait_ge(chain, it * 2 + (5 + h))
                            for q in range(heads):
                                wq = weight(q, t0, K)
                                ins = nc.vector.tensor_tensor(
                                    ohw[0:EP, h, :, q * HI:(q + 1) * HI], v,
                                    wq.unsqueeze(2).to_broadcast([EP, K, HI]), ALU.mult)
                            ins.then_inc(hot[h], 1)
                    dve.wait_ge(closed, 1)
                    nc.vector.tensor_copy(den[:, 0:W], bank_c[:, 0:W])

                @block.tensor
                def _(pe):
                    nc.tensor.matmul(bank_c[:, 0:W], ones[:, :], S[:].rearrange("p b c -> p (b c)")[:, 0:W],
                                     start=True, stop=False).then_inc(opened, 1)
                    for h in range(2):
                        pe.sem_inc(taken[h], 1)
                    with pe.Fori(0, L) as it:
                        for h in range(2):
                            pe.wait_ge(hot[h], it + 2)
                            for k in range(K):
                                ins = nc.tensor.matmul(bank_c[:, 0:W], oh[0:EP, h, k, :], ohw[0:EP, h, k, 0:W],
                                                       start=False, stop=False)
                            ins.then_inc(taken[h], 1)
                    nc.tensor.matmul(bank_c[:, 0:W], ones[:, :], S[:].rearrange("p b c -> p (b c)")[:, 0:W],
                                     start=False, stop=True).then_inc(closed, 1)

        denominators("den0", lambda q, t0, k: e0[0:EP, bass.ds(t0, k)], 1,
                     lambda act: nc.scalar.activation(e0[0:EP], e0[0:EP], ACT.Exp))

        sc = sem("xs_scaled")
        scc = sem("xs_chain")
        sct = sem("xs_stored")
        with nc.Block() as block:
            @block.vector
            def _(dve):
                nc.vector.tensor_scalar(den[:, 0:NB], den[:, 0:NB], 1.1754944e-38, None, ALU.max).then_inc(scc, 1)
                dve.wait_ge(scc, 1)
                nc.vector.reciprocal(rden[:, 0:NB], den[:, 0:NB]).then_inc(scc, 1)
                dve.wait_ge(scc, 2)
                nc.vector.tensor_tensor(R[:], X[:], rden[:, 0:NB].unsqueeze(2).to_broadcast([P, NB, C]),
                                        ALU.mult).then_inc(sc, 1)

            @block.sync
            def _(sp):
                sp.wait_ge(sc, 1)
                sp.dma_start(blocks(xs_tab), R[:]).then_inc(sct, 16)
                sp.wait_ge(sct, 16)

        def aggregate(tag, table, pick, key, weigh, accs):
            idx_ready = [sem(f"{tag}_idx{h}") for h in range(2)]
            gathered = [sem(f"{tag}_gathered{h}") for h in range(2)]
            msg_ready = [sem(f"{tag}_messages{h}") for h in range(2)]
            diag_ready = [sem(f"{tag}_diagonals{h}") for h in range(2)]
            rows_ready = [sem(f"{tag}_keyrows{h}") for h in range(2)]
            same_ready = [sem(f"{tag}_same{h}") for h in range(2)]
            summed = [sem(f"{tag}_summed{h}") for h in range(2)]
            out_ready = [sem(f"{tag}_out{h}") for h in range(2)]
            scattered = [sem(f"{tag}_scattered{k}") for k in range(COPIES)]
            chain = sem(f"{tag}_chain")
            PER = 16 * G
            STEPS = 7
            SPI = 2 * G // COPIES
            key_rows = bank_a[0:EP].rearrange("p b n -> p (b n)").rearrange("p (k n) -> p k n", k=G)[:, :, 0:EP]
            sums = bank_b[0:EP].rearrange("p b n -> p (b n)").rearrange("p (k n) -> p k n", k=G)

            with nc.Block() as block:
                @block.scalar
                def _(act):
                    for h in range(2):
                        act.sem_inc(out_ready[h], 1)
                    with act.Fori(0, ITERS) as it:
                        for h in range(2):
                            act.wait_ge(msg_ready[h], it + 1)
                            nc.scalar.copy(idx_a[0:EP, h, :], pick[0:EP, bass.ds(it * (2 * G) + h * G, G)]
                                           ).then_inc(idx_ready[h], 1)
                        for h in range(2):
                            act.wait_ge(summed[h], it + 2)
                            for k in range(COPIES):
                                act.wait_ge(scattered[k], it * (16 * SPI) + 16)
                            nc.scalar.copy(gb[0:EP, h], sums).then_inc(out_ready[h], 1)

                @block.gpsimd
                def _(pool):
                    for k in range(COPIES):
                        pool.dma_start(accs[k][NP:NP + P], S[:, 0, :]).then_inc(scattered[k], 16)
                    with pool.Fori(0, ITERS) as it:
                        for h in range(2):
                            pool.wait_ge(idx_ready[h], it + 1)
                            pool.wait_ge(msg_ready[h], it + 1)
                            pool.sem_inc(turns, 1)
                            for k in range(G):
                                pool.indirect_dma_start(
                                    out=ga[0:EP, h, k, :], out_offset=None, in_=table,
                                    in_offset=bass.IndirectOffsetOnAxis(ap=idx_a[0:EP, h, k:k + 1], axis=0),
                                ).then_inc(gathered[h], 16)
                        for h in range(2):
                            pool.wait_ge(same_ready[h], it + 2)
                            pool.wait_ge(out_ready[h], it + 2)
                            pool.sem_inc(turns, 1)
                            for k in range(G):
                                n = (h * G + k) // COPIES
                                pool.wait_ge(scattered[k % COPIES], it * (16 * SPI) + 16 * (n + 1))
                                pool.sem_inc(turns, 1)
                                pool.indirect_dma_start(
                                    out=accs[k % COPIES],
                                    out_offset=bass.IndirectOffsetOnAxis(ap=idx_b[0:EP, h, k:k + 1], axis=0),
                                    in_=gb[0:EP, h, k, :], in_offset=None, compute_op=ALU.add,
                                ).then_inc(scattered[k % COPIES], 16)
                    for k in range(COPIES):
                        pool.wait_ge(scattered[k], 16 * (SPI * ITERS + 1))

                @block.vector
                def _(dve):
                    for h in range(2):
                        dve.sem_inc(msg_ready[h], 1)
                        dve.sem_inc(same_ready[h], 1)
                    with dve.Fori(0, ITERS) as it:
                        for h in range(2):
                            t0 = it * (2 * G) + h * G
                            done = [0]

                            def link(ins):
                                done[0] += 1
                                ins.then_inc(chain, 1)
                                dve.wait_ge(chain, it * (2 * STEPS) + (h * STEPS + done[0]))

                            dve.wait_ge(same_ready[1 - h], it + h + 1)
                            link(nc.vector.tensor_copy(key_f[0:EP], key[0:EP, bass.ds(t0, G)]))
                            keys = key_f[0:EP].unsqueeze(2).to_broadcast([EP, G, EP])
                            nc.vector.tensor_tensor(
                                wk[0:EP, :, 0:EP], ident[0:EP, 0:EP].unsqueeze(1).to_broadcast([EP, G, EP]), keys,
                                ALU.mult).then_inc(diag_ready[h], 1)
                            dve.wait_ge(rows_ready[h], it + 1)
                            dve.wait_ge(summed[1 - h], it + h + 1)
                            link(nc.vector.tensor_tensor(wk2[0:EP, :, 0:EP], key_rows, keys, ALU.is_equal))
                            link(nc.vector.tensor_tensor(
                                wk[0:EP, :, 0:EP], wk2[0:EP, :, 0:EP],
                                below[0:EP, 0:EP].unsqueeze(1).to_broadcast([EP, G, EP]), ALU.mult))
                            link(nc.vector.tensor_reduce(dup[0:EP], wk[0:EP, :, 0:EP], AX.X, ALU.add))
                            link(nc.vector.tensor_scalar(dup[0:EP], dup[0:EP], 1.0, None, ALU.min))
                            link(nc.vector.tensor_scalar(dmy[0:EP], key_f[0:EP], -1.0, dummy[0:EP, 0:1], ALU.mult,
                                                         ALU.add))
                            link(nc.vector.tensor_tensor(dmy[0:EP], dmy[0:EP], dup[0:EP], ALU.mult))
                            for k in range(COPIES):
                                dve.wait_ge(scattered[k], it * (16 * SPI) + 16)
                            nc.vector.tensor_tensor(idx_b[0:EP, h, :], dmy[0:EP], key_f[0:EP], ALU.add
                                                    ).then_inc(same_ready[h], 1)
                            dve.wait_ge(gathered[h], (it + 1) * PER)
                            weigh(wk3[0:EP], ga[0:EP, h], t0).then_inc(msg_ready[h], 1)

                @block.tensor
                def _(pe):
                    for h in range(2):
                        pe.sem_inc(summed[h], 1)
                    with pe.Fori(0, ITERS) as it:
                        for h in range(2):
                            pe.wait_ge(diag_ready[h], it + 1)
                            half = G // 2
                            for b in range(2):
                                ins = nc.tensor.matmul(
                                    bank_a[0:EP, b, :].rearrange("p (k n) -> p k n", k=half)[:, :, 0:EP],
                                    ones[0:EP, 0:EP], wk[0:EP, b * half:(b + 1) * half, 0:EP],
                                    start=True, stop=True)
                            ins.then_inc(rows_ready[h], 1)
                            pe.wait_ge(msg_ready[h], it + 2)
                            pe.wait_ge(out_ready[1 - h], it + h + 1)
                            for k in range(G):
                                ins = nc.tensor.matmul(sums[:, k, :], wk2[0:EP, k, 0:EP], wk3[0:EP, k, :],
                                                       start=True, stop=True)
                            ins.then_inc(summed[h], 1)

        def weigh0(dest, rows_, t0):
            return nc.vector.tensor_tensor(dest, rows_, e0[0:EP, bass.ds(t0, G)].unsqueeze(2).to_broadcast([EP, G, C]),
                                           ALU.mult)

        aggregate("agg0", xs_tab, src_i, dst_i, weigh0, acc_tabs[0])

        def load_sums(tag, accs, dest, tmp, after):
            l0, l1, added, chain = sem(f"{tag}_loaded0"), sem(f"{tag}_loaded1"), sem(f"{tag}_added"), sem(f"{tag}_chain")
            a_req, a_done = sem(f"{tag}_act_asked"), sem(f"{tag}_act_done")
            asked = []
            st = sem(f"{tag}_stored")
            fin = sem(f"{tag}_finished")
            with nc.Block() as block:
                @block.sync
                def _(sp):
                    sp.dma_start(dest[:], blocks(accs[0])).then_inc(l0, 16)
                    for k in range(1, COPIES):
                        if k > 1:
                            sp.wait_ge(added, k - 1)
                        sp.dma_start(tmp[:], blocks(accs[k])).then_inc(l1, 16)
                    sp.wait_ge(l0, 16)
                    sp.wait_ge(l1, 16 * (COPIES - 1))
                    if tag == "norm1":
                        sp.wait_ge(fin, 1)
                        sp.dma_start(out[0:NFULL * P].rearrange("(b p) c -> p b c", p=P), X[:, 0:NFULL, :]).then_inc(st, 16)
                        sp.dma_start(out[NFULL * P:N], X[0:NREST, NFULL, :]).then_inc(st, 16)
                        sp.wait_ge(st, 32)

                @block.vector
                def _(dve):
                    count = [0]

                    def link(ins):
                        count[0] += 1
                        ins.then_inc(chain, 1)
                        dve.wait_ge(chain, count[0])

                    def on_act(emit):
                        asked.append(emit)
                        nc.vector.tensor_copy(stat2[:, 0:1], part[:, 0:1]).then_inc(a_req, 1)
                        dve.wait_ge(a_done, len(asked))

                    dve.wait_ge(l0, 16)
                    for k in range(1, COPIES):
                        dve.wait_ge(l1, 16 * k)
                        count[0] += 1
                        ins = nc.vector.tensor_tensor(dest[:], dest[:], tmp[:], ALU.add)
                        ins.then_inc(added, 1)
                        dve.wait_ge(added, k)
                        count[0] -= 1
                    after(link, on_act)
                    link(nc.vector.tensor_tensor(X[:], X[:], dest[:], ALU.add))
                    link(nc.vector.tensor_reduce(stat[:], X[:], AX.X, ALU.add))
                    link(nc.vector.tensor_scalar(stat[:], stat[:], 1.0 / C, None, ALU.mult))
                    link(nc.vector.tensor_tensor(X[:], X[:], stat[:].unsqueeze(2).to_broadcast([P, NB, C]),
                                                 ALU.subtract))
                    link(nc.vector.tensor_tensor(dest[:], X[:], X[:], ALU.mult))
                    link(nc.vector.tensor_reduce(stat[:], dest[:], AX.X, ALU.add))
                    link(nc.vector.tensor_scalar(stat[:], stat[:], 1.0 / C, LN_EPS, ALU.mult, ALU.add))
                    on_act(lambda: nc.scalar.activation(stat[:], stat[:], ACT.Sqrt))
                    link(nc.vector.reciprocal(stat[:], stat[:]))
                    nc.vector.tensor_tensor(X[:], X[:], stat[:].unsqueeze(2).to_broadcast([P, NB, C]),
                                            ALU.mult).then_inc(fin, 1)

                @block.scalar
                def _(act):
                    for n, emit in enumerate(asked):
                        act.wait_ge(a_req, n + 1)
                        emit().then_inc(a_done, 1)

        load_sums("norm0", acc_tabs[0], S, R, lambda link, on_act: None)

        def res_rows(b):
            return r_tab[b * P:(b + 1) * P]

        r_tab = nc.dram_tensor("r_tab", (NP, C), F32, kind="Internal").ap()
        project("proj1", w1_all[:], 2 * C + 2 * HEADS,
                [(rows(h_tab), 0, C), (res_rows, C, 2 * C), (rows(st_tab), 2 * C, 2 * C + 2 * HEADS)])

        def combine1(link, h, t0):
            a, b = ga[0:EP, h, :, 0:HEADS], gb[0:EP, h, :, HEADS:2 * HEADS]
            link(nc.vector.tensor_tensor(wk[0:EP, :, 0:HEADS], a, b, ALU.add))
            return nc.vector.scalar_tensor_tensor(out=s1[0:EP, bass.ds(t0, G), :], in0=wk[0:EP, :, 0:HEADS],
                                                  scalar=ALPHA, in1=wk[0:EP, :, 0:HEADS], op0=ALU.mult, op1=ALU.max)

        scores("score1", st_tab, st_tab, 2 * HEADS, HEADS, combine1, 1)

        mx = sem("max_steps")
        with nc.Block() as block:
            @block.vector
            def _(dve):
                nc.vector.tensor_reduce(gmax[0:EP, 0:1], s1[0:EP].rearrange("p t h -> p (t h)"), AX.X,
                                        ALU.max).then_inc(mx, 1)
                nc.vector.memset(S[:], 0.0)
                dve.wait_ge(mx, 2)
                nc.vector.tensor_scalar(gmax[0:EP, 1:2], gmax[0:EP, 1:2], -1.0, None, ALU.mult)

            @block.gpsimd
            def _(pool):
                pool.wait_ge(mx, 1)
                nc.gpsimd.partition_all_reduce(gmax[0:EP, 1:2], gmax[0:EP, 0:1], EP, RMAX).then_inc(mx, 1)

        denominators("den1", lambda q, t0, k: s1[0:EP, bass.ds(t0, k), q], HEADS,
                     lambda act: nc.scalar.activation(s1[0:EP].rearrange("p t h -> p (t h)"),
                                                      s1[0:EP].rearrange("p t h -> p (t h)"), ACT.Exp,
                                                      bias=gmax[0:EP, 1:2]))

        def weigh1(dest, rows_, t0):
            w = s1[0:EP, bass.ds(t0, G), :].rearrange("p g h -> p (g h)").unsqueeze(2).to_broadcast([EP, G * HEADS, D])
            return nc.vector.tensor_tensor(dest.rearrange("p g (h d) -> p (g h) d", h=HEADS),
                                           rows_.rearrange("p g (h d) -> p (g h) d", h=HEADS), w, ALU.mult)

        aggregate("agg1", h_tab, dst_i, src_i, weigh1, acc_tabs[1])

        rl = sem("residual_loaded")

        def finish1(link, on_act):
            link(nc.vector.tensor_scalar(den[:, 0:HEADS * HI], den[:, 0:HEADS * HI], SM_EPS, None, ALU.add))
            link(nc.vector.reciprocal(rden[:, 0:HEADS * HI], den[:, 0:HEADS * HI]))
            for q in range(HEADS):
                r = rden[:, q * HI:q * HI + NB].unsqueeze(2).to_broadcast([P, NB, D])
                v = S[:, :, q * D:(q + 1) * D]
                link(nc.vector.tensor_tensor(v, v, r, ALU.mult))
            res_chunks(link)
            link(nc.vector.tensor_scalar(R[:], S[:], 0.0, None, ALU.min))
            on_act(lambda: nc.scalar.activation(R[:], R[:], ACT.Exp))
            link(nc.vector.tensor_scalar(R[:], R[:], -1.0, None, ALU.add))
            link(nc.vector.scalar_tensor_tensor(out=S[:], in0=S[:], scalar=0.0, in1=R[:], op0=ALU.max, op1=ALU.add))

        def res_chunks(link):
            link(nc.vector.tensor_tensor(S[:], S[:], RES[:], ALU.add))

        assert T * HEADS >= NB * C
        RES = s1[:].rearrange("p t h -> p (t h)")[:, 0:NB * C].rearrange("p (b c) -> p b c", c=C)
        with nc.Block() as block:
            @block.sync
            def _(sp):
                sp.dma_start(RES[:], blocks(r_tab)).then_inc(rl, 16)
                sp.wait_ge(rl, 16)
        load_sums("norm1", acc_tabs[1], S, R, finish1)


_INS = ["x", "src", "dst", "L0_gnn_w", "L0_gnn_a", "L1_gnn_W", "L1_gnn_A_left", "L1_gnn_A_right",
        "L1_gnn_residual_projection"]


def kernel(**inputs):
    import numpy as _np
    import concourse.bacc as _bacc
    from concourse import mybir as _mybir
    from concourse.bass_utils import run_bass_kernel_spmd as _run

    nc = _bacc.Bacc("TRN2", target_bir_lowering=False, num_devices=1)
    arrays, args = {}, []
    for name in _INS:
        a = _np.ascontiguousarray(inputs[name])
        arrays[f"in_{name}_dram"] = a
        args.append(nc.dram_tensor(f"in_{name}_dram", a.shape, _mybir.dt.from_np(a.dtype), kind="ExternalInput").ap())
    n, c = inputs["x"].shape
    args.append(nc.dram_tensor("out_0_dram", (n, c), _mybir.dt.float32, kind="ExternalOutput").ap())
    gnn_program(nc, *args)
    r = _run(nc, [arrays], core_ids=[0])
    return r.results[0]["out_0_dram"]
```

```python
from contextlib import ExitStack

import concourse.bass as bass
from concourse import mybir

F32 = mybir.dt.float32
BF16 = mybir.dt.bfloat16
I32 = mybir.dt.int32
U32 = mybir.dt.uint32
ALU = mybir.AluOpType
ACT = mybir.ActivationFunctionType
AX = mybir.AxisListType
RMAX = bass.bass_isa.ReduceOp.max

P = 128
C = 128
HEADS = 4
D = C // HEADS
ALPHA = 0.2
LN_EPS = 1e-5
SM_EPS = 1e-8
NEVER = -1e30
ENGINES = mybir.ALL_ENGINES
EP = 125



CZ = C + 2
W_T = 36
WIN = P * W_T
GT = 4
STEP = 16


class Stage(ExitStack):

    def __init__(self, nc):
        super().__init__()
        self.nc, self.semaphores = nc, []

    def semaphore(self, name):
        self.semaphores.append(self.nc.alloc_semaphore(name))
        return self.semaphores[-1]

    def __exit__(self, *error):
        closed = super().__exit__(*error)
        if error[0] is None and self.semaphores:
            self.nc.clear_and_free_semaphores(self.semaphores)
            self.nc.all_engine_barrier()
        return closed


def groups_of(n):
    return [(a, min(GT, n - a)) for a in range(0, n, GT)]


class Chain:

    def __init__(self, eng, sem, per=0):
        self.eng, self.sem, self.per, self.n, self.base, self.it = eng, sem, per, 0, 0, None

    def enter(self, it):
        self.base, self.n, self.it = self.n, 0, it

    def leave(self, iters):
        assert self.n == self.per, (self.n, self.per)
        self.n, self.it, self.base = self.base + self.per * iters, None, 0

    def mark(self, ins):
        self.n += 1
        ins.then_inc(self.sem, 1)
        return self.n

    def wait(self, n):
        self.eng.wait_ge(self.sem, n if self.it is None else self.it * self.per + (self.base + n))

    def link(self, ins):
        self.wait(self.mark(ins))


def split3(nc, chain, value, hi, mid, lo, rest):
    chain.link(nc.vector.tensor_copy(hi, value))
    chain.link(nc.vector.tensor_tensor(rest, value, hi, ALU.subtract))
    chain.link(nc.vector.tensor_copy(mid, rest))
    return nc.vector.tensor_tensor(lo, rest, mid, ALU.subtract)


def place_windows(nc, k, src, dst):
    E = dst.shape[0]
    T, NS = E // EP, E // EP // STEP
    NW = k.NW
    with Stage(nc) as ctx:
        def sb(name, shape, dt=F32):
            return ctx.enter_context(nc.sbuf_tensor(name, shape, dt))

        dst_i = sb("win_dst_all", [P, T], I32)
        dst_f = sb("win_dst_sample", [P, NS])
        less = sb("win_less", [P, k.NW, NS], BF16)
        count = sb("win_count", [P, k.NW])
        thr = k.thr
        off_f = sb("win_off_f", [P, NW])
        off_i = sb("win_off_i", [P, NW], I32)
        ws = sb("win_src", [P, NW, W_T], I32)
        wd = sb("win_dst", [P, NW, W_T], I32)
        wi = sb("win_int", [P, NW, W_T], I32)
        f1 = sb("win_f1", [P, NW, W_T])
        f2 = sb("win_f2", [P, NW, W_T])
        f3 = sb("win_f3", [P, NW, W_T])
        psum = ctx.enter_context(nc.psum_tensor("win_psum", [P, NW], F32))
        s = {n: ctx.semaphore("win_" + n) for n in
             ("loaded", "chain", "counted", "summed", "offsets", "src_read", "dst_read", "padded")}
        with nc.Block() as block:
            @block.sync
            def _(sp):
                sp.dma_start(dst_i[0:EP, :], dst.rearrange("(p t) -> p t", p=EP)).then_inc(s["loaded"], 16)
                sp.wait_ge(s["offsets"], 1)
                sp.wait_ge(s["padded"], 1)
                with sp.Fori(0, k.NI) as j:
                    o = sp.value_load(off_i[0:1, bass.ds(j, 1)], min_val=0, max_val=E - WIN)
                    sp.dma_start(ws[:, bass.ds(j, 1), :], src[bass.ds(o, WIN)].rearrange("(p a t) -> p a t", p=P, a=1)
                                 ).then_inc(s["src_read"], 16)
                sp.wait_ge(s["src_read"], 16 * k.NI)

            @block.scalar
            def _(act):
                act.wait_ge(s["offsets"], 1)
                act.wait_ge(s["padded"], 1)
                with act.Fori(0, k.NI) as j:
                    o = act.value_load(off_i[0:1, bass.ds(j, 1)], min_val=0, max_val=E - WIN)
                    act.dma_start(wd[:, bass.ds(j, 1), :], dst[bass.ds(o, WIN)].rearrange("(p a t) -> p a t", p=P, a=1)
                                  ).then_inc(s["dst_read"], 16)
                act.wait_ge(s["dst_read"], 16 * k.NI)

            @block.tensor
            def _(pe):
                pe.wait_ge(s["counted"], 1)
                nc.tensor.matmul(psum[:], k.ones[0:EP, :], count[0:EP, :], start=True, stop=True).then_inc(s["summed"], 1)

            @block.vector
            def _(dve):
                ch = Chain(dve, s["chain"])
                nc.vector.memset(ws[:, k.NI:NW, :], 0)
                nc.vector.memset(wd[:, k.NI:NW, :], 0).then_inc(s["padded"], 1)
                dve.wait_ge(s["loaded"], 16)
                ch.link(nc.vector.tensor_copy(dst_f[0:EP], dst_i[0:EP, 0:T:STEP]))
                ch.link(nc.vector.tensor_tensor(less[0:EP], dst_f[0:EP].unsqueeze(1).to_broadcast([EP, NW, NS]),
                                                thr[0:EP].unsqueeze(2).to_broadcast([EP, NW, NS]), ALU.is_lt))
                nc.vector.tensor_reduce(count[0:EP], less[0:EP], AX.X, ALU.add).then_inc(s["counted"], 1)
                dve.wait_ge(s["summed"], 1)
                ch.link(nc.vector.tensor_scalar(off_f[:], psum[:], float(STEP), -float(STEP), ALU.mult, ALU.add))
                ch.link(nc.vector.tensor_scalar(off_f[:], off_f[:], 0.0, float(E - WIN), ALU.max, ALU.min))
                nc.vector.tensor_copy(off_i[:], off_f[:]).then_inc(s["offsets"], 1)
                dve.wait_ge(s["src_read"], 16 * k.NI)
                dve.wait_ge(s["dst_read"], 16 * k.NI)
                ch.link(nc.vector.tensor_copy(f1[:], wd[:]))
                ch.link(nc.vector.tensor_tensor(f1[:], f1[:], thr[:].unsqueeze(2).to_broadcast([P, NW, W_T]),
                                                ALU.subtract))
                nc.vector.tensor_scalar(k.dlo[:], f1[:], 1.0, None, ALU.add)
                ch.link(nc.vector.tensor_scalar(f2[:], f1[:], 0.0, None, ALU.is_ge))
                ch.link(nc.vector.tensor_scalar(f3[:], f1[:], float(P), None, ALU.is_lt))
                ch.link(nc.vector.tensor_tensor(f2[:], f2[:], f3[:], ALU.mult))
                ch.link(nc.vector.tensor_scalar(f2[:], f2[:], -200.0, 200.0, ALU.mult, ALU.add))
                ch.link(nc.vector.tensor_scalar(wi[:], ws[:], P - 1, None, ALU.bitwise_and))
                ch.link(nc.vector.tensor_copy(f3[:], wi[:]))
                nc.vector.tensor_scalar(k.slo[:], f3[:], 1.0, None, ALU.add)
                ch.link(nc.vector.tensor_scalar(wi[:], ws[:], 7, None, ALU.logical_shift_right))
                ch.link(nc.vector.tensor_copy(f1[:], wi[:]))
                nc.vector.tensor_tensor(k.key[:], f1[:], f2[:], ALU.add)


def project_parts(nc, k, tag, X, weights, split, NB, parts, plain):
    width = weights.shape[1]
    with Stage(nc) as ctx:
        def sb(name, shape, dt=F32):
            return ctx.enter_context(nc.sbuf_tensor(f"{tag}_{name}", shape, dt))

        def pair(name):
            return [ctx.semaphore(f"{tag}_{name}{h}") for h in range(2)]

        xb, xt, rest = sb("block", [P, 2, C]), sb("turned", [P, 2, C]), sb("rest", [P, 2, split])
        tps = ctx.enter_context(nc.psum_tensor(f"{tag}_tps", [P, 2, 512], F32))
        prod = ctx.enter_context(nc.psum_tensor(f"{tag}_prod", [P, 2, 512], F32))
        picked, turned, xt_ok, mul, hi_ok, rest_ok, mid_ok, lo_ok = (
            pair(n) for n in ("picked", "turned", "turned_in_sbuf", "product", "hi", "rest", "mid", "lo"))

        def part(b, q):
            return parts[:, bass.ds(b, 1), q, :]

        with nc.Block() as block:
            @block.vector
            def _(dve):
                for h in range(2):
                    dve.sem_inc(rest_ok[h], 1)
                    dve.sem_inc(lo_ok[h], 1)
                with dve.Fori(0, NB // 2) as it:
                    for h in range(2):
                        dve.wait_ge(turned[h], it + 1)
                        nc.vector.tensor_copy(xb[:, h:h + 1, :], X[:, bass.ds(it * 2 + h, 1), :]
                                              ).then_inc(picked[h], 1)
                    for h in range(2):
                        dve.wait_ge(hi_ok[h], it + 1)
                        nc.vector.tensor_tensor(rest[:, h:h + 1, :], prod[:, h:h + 1, 0:split], part(it * 2 + h, 0),
                                                ALU.subtract).then_inc(rest_ok[h], 1)
                    for h in range(2):
                        dve.wait_ge(mid_ok[h], it + 1)
                        nc.vector.tensor_tensor(part(it * 2 + h, 2), rest[:, h:h + 1, :], part(it * 2 + h, 1),
                                                ALU.subtract).then_inc(lo_ok[h], 1)
                        dve.wait_ge(lo_ok[h], it + 2)

            @block.tensor
            def _(pe):
                for h in range(2):
                    pe.sem_inc(turned[h], 1)
                with pe.Fori(0, NB // 2) as it:
                    for h in range(2):
                        pe.wait_ge(picked[h], it + 1)
                        pe.wait_ge(xt_ok[h], it + 1)
                        nc.tensor.transpose(tps[:, h, 0:C], xb[:, h, :], k.ident[:]).then_inc(turned[h], 1)
                    for h in range(2):
                        pe.wait_ge(xt_ok[h], it + 2)
                        pe.wait_ge(rest_ok[h], it + 1)
                        nc.tensor.matmul(prod[:, h, 0:width], xt[:, h, :], weights, start=True, stop=True
                                         ).then_inc(mul[h], 1)

            @block.scalar
            def _(act):
                for h in range(2):
                    act.sem_inc(xt_ok[h], 1)
                with act.Fori(0, NB // 2) as it:
                    for h in range(2):
                        act.wait_ge(turned[h], it + 2)
                        act.wait_ge(lo_ok[h], it + 1)
                        nc.scalar.copy(xt[:, h, :], tps[:, h, 0:C]).then_inc(xt_ok[h], 1)
                    for h in range(2):
                        act.wait_ge(mul[h], it + 1)
                        if plain is not None:
                            nc.scalar.copy(plain[:, bass.ds(it * 2 + h, 1), :], prod[:, h:h + 1, split:width])
                        nc.scalar.copy(part(it * 2 + h, 0), prod[:, h:h + 1, 0:split]).then_inc(hi_ok[h], 1)
                    for h in range(2):
                        act.wait_ge(rest_ok[h], it + 2)
                        nc.scalar.copy(part(it * 2 + h, 1), rest[:, h:h + 1, :]).then_inc(mid_ok[h], 1)


def one(ap):
    return ap.squeeze(1)


def bin_and_score(nc, k, pq, e0, den_out):
    NI, NW = k.NI - 1, k.NW
    grp = groups_of(NI)
    NG = len(grp)
    K2 = 2 * NG
    PER = K2 // 2
    L = k.NI // 2
    W2 = W_T + 2
    with Stage(nc) as ctx:
        def sb(name, shape, dt=F32):
            return ctx.enter_context(nc.sbuf_tensor(f"p1_{name}", shape, dt))

        def ps(name, shape, dt=F32):
            return ctx.enter_context(nc.psum_tensor(f"p1_{name}", shape, dt))

        def sem(name):
            return ctx.semaphore(f"p1_{name}")

        def pair(name):
            return [sem(f"{name}{h}") for h in range(2)]

        binrow = sb("binrow", [P, NI, W_T], BF16)
        keep = sb("keep", [P, NI, W2], BF16)
        ohb = sb("ohb", [P, NI, W2], BF16)
        scan = sb("scan", [P, NI, W2], BF16)
        rank = sb("rank", [P, W_T])
        rank_b = sb("rank_b", [P, W_T], BF16)
        lanes = sb("lanes", [P, P, W_T], BF16)
        pay = sb("pay", [P, 2, NI, W_T], BF16)
        picked = pay[:, 0]
        slot = sb("slot", [P, 2, 2, NI], BF16)
        ohs = sb("ohs", [P, 2, NG, P, GT], BF16)
        ohd = sb("ohd", [P, 2, P, GT], BF16)
        oht = sb("oht", [P, 2, 2, GT, P], BF16)
        qst = sb("qst", [P, 2, 3, CZ], BF16)
        rz = sb("rz", [P, 2, GT, CZ])
        score = sb("score", [P, 2, NI])
        rest = sb("rest", [P, NI])
        ep = sb("ep", [P, 2, NI, 3], BF16)
        zeros = keep[:, :, 0:1].to_broadcast([P, NI, 3])

        tp = ps("tp", [P, 2, 2, GT * P], BF16)
        z = ps("z", [P, 2, 2, 512])
        base_slots = ps("base_slots", [P, 512])
        base, slots = base_slots[:, 0:NI], base_slots[:, 256:256 + 2 * NI]
        dps = ps("dps", [P, 512])

        gen, tr, ev, zz, rl, dt = (pair(n) for n in ("onehot", "turned", "turned_in_sbuf", "z", "relu", "scored"))
        qs, ex, pt, dn = (pair(n) for n in ("q_block", "exp", "exp_parts", "den"))
        b_oh, b_base, b_scan, b_pick, b_rank, b_lane, b_pay, b_slot = (sem(n) for n in (
            "bin_onehot", "bin_base", "bin_scan", "bin_picked", "bin_rank", "bin_lanes", "bin_payload", "bin_slots"))
        b_init, opened, closed, chain = sem("const"), sem("opened"), sem("closed"), sem("chain")

        def bins_of(banks, w):
            pairs = banks[:, :, 0:2 * CZ].rearrange("p b (i c) -> p b i c", c=CZ)
            return pairs if w == GT else pairs[:, 0, 0:w]

        def key_at(arr, n):
            return one(arr[:, bass.ds(n, 1), :]) if not isinstance(n, int) else arr[:, n, :]

        oh_part = ohb[:, :, 2:W2]

        LANE_PIECES = (4, 5, 7, 8)

        def dve_bin(ch, dve, piece, n, m, h):
            first = isinstance(n, int)
            if piece == 0:
                if not first:
                    dve.wait_ge(b_base, m)
                    dve.wait_ge(b_slot, m)
                nc.vector.tensor_tensor(oh_part, binrow[:], key_at(k.key, n).unsqueeze(1).to_broadcast([P, NI, W_T]),
                                        ALU.is_equal).then_inc(b_oh, 1)
            if piece == 1:
                dve.wait_ge(b_base, m + 1)
                ch.link(nc.vector.tensor_scalar(ohb[:, :, 1], base, 200.0, None, ALU.min))
                nc.vector.tensor_tensor_scan(scan[:].rearrange("p b t -> p (b t)"), keep[:].rearrange("p b t -> p (b t)"),
                                             ohb[:].rearrange("p b t -> p (b t)"), 0.0, ALU.mult, ALU.add
                                             ).then_inc(b_scan, 1)
            if piece == 3:
                dve.wait_ge(b_pick, m + 1)
                nc.vector.tensor_reduce(rank[:], picked.rearrange("p b t -> p t b"), AX.X, ALU.add).then_inc(b_rank, 1)
                dve.wait_ge(b_rank, m + 1)
                ch.link(nc.vector.tensor_scalar(rank_b[:], rank[:], -1.0, None, ALU.add))
            if piece in LANE_PIECES:
                part = LANE_PIECES.index(piece)
                a, b = part * P // 4, (part + 1) * P // 4
                by4 = [P, b - a, W_T // GT, GT]
                ins = nc.vector.tensor_tensor(
                    lanes[:, a:b, :].rearrange("p n (u v) -> p n u v", v=GT), k.iota_x[:, a:b, :].unsqueeze(2).to_broadcast(by4),
                    rank_b[:].rearrange("p (u v) -> p u v", v=GT).unsqueeze(1).to_broadcast(by4), ALU.is_equal)
                if part == 3:
                    ins.then_inc(b_lane, 1)
            if piece == 6:
                dve.wait_ge(b_slot, m + 1)
                ch.link(nc.vector.tensor_scalar(slot[:, h].rearrange("p a b -> p (a b)"), slots, -1.0, None, ALU.add))
                for a, arr in ((0, k.SLs), (1, k.SLd)):
                    out = arr[:, bass.ds(n, 1), 0:NI] if not first else arr[:, n:n + 1, 0:NI]
                    ins = nc.vector.tensor_copy(out, slot[:, h, a].unsqueeze(1))
                ch.link(ins)

        def pe_base(pe, m):
            pe.wait_ge(b_oh, m + 1)
            for t in range(W_T):
                ins = nc.tensor.matmul(base, k.above_b[:], ohb[:, :, 2 + t], start=(t == 0), stop=(t == W_T - 1))
            ins.then_inc(b_base, 1)

        def pe_slots(pe, m):
            pe.wait_ge(b_lane, m + 1)
            pe.wait_ge(b_pay, m + 1)
            for t in range(W_T):
                ins = nc.tensor.matmul(slots.rearrange("p (a b) -> p a b", a=2), lanes[:, :, t], pay[:, :, :, t],
                                       start=(t == 0), stop=(t == W_T - 1))
            ins.then_inc(b_slot, 1)

        def pool_bin(pool, n, m):
            if not isinstance(n, int):
                pool.wait_ge(b_slot, m)
            pool.wait_ge(b_scan, m + 1)
            nc.gpsimd.tensor_tensor(picked, oh_part, scan[:, :, 2:W2], ALU.mult).then_inc(b_pick, 1)
            pool.wait_ge(b_rank, m + 1)
            for q, arr in enumerate((k.slo, k.dlo)):
                ins = nc.gpsimd.tensor_tensor(pay[:, q], oh_part, key_at(arr, n).unsqueeze(1).to_broadcast([P, NI, W_T]),
                                              ALU.mult)
            ins.then_inc(b_pay, 1)

        PIECES = {0: 0, 2: 1, 5: 3, 6: 4, 7: 5, 8: 7, 9: 8, 12: 6}
        CH = 2 * (1 + 1 + 2) + 2 * 3

        with nc.Block() as block:
            @block.vector
            def _(dve):
                ch = Chain(dve, chain, CH)
                nc.vector.tensor_copy(binrow[:], k.iota[:, 0:NI].unsqueeze(2).to_broadcast([P, NI, W_T]))
                ch.link(nc.vector.memset(keep[:], 1.0))
                nc.vector.memset(keep[:, :, 0:1], 0.0)
                nc.vector.memset(ohb[:, :, 0:2], 0.0)
                nc.vector.memset(k.SLs[:], -1.0)
                nc.vector.memset(k.SLd[:], -1.0)
                nc.vector.memset(e0[:], 0.0)
                nc.vector.memset(den_out[:, NI:], 1.0).then_inc(b_init, 1)
                dve.wait_ge(b_init, 1)
                for piece in (0, 1, 3, 4, 5, 7, 8, 6):
                    dve_bin(ch, dve, piece, 0, 0, 0)
                for h in range(2):
                    dve.sem_inc(gen[h], 1)
                    dve.sem_inc(dt[h], 1)
                    dve.sem_inc(pt[h], 1)

                def weigh(it, r):
                    h, g = divmod(r, NG)
                    i0, w = grp[g]
                    gp, c = r % 2, it * PER + (r // 2 + 1)
                    if g == 0:
                        dve.wait_ge(ex[h], it + 1)
                    dve.wait_ge(rl[gp], c + 1)
                    for i in range(w):
                        ins = nc.vector.tensor_tensor_reduce(
                            out=rz[:, gp, i, :], in0=rz[:, gp, i, :], in1=k.a_pos[:], scale=1.0, scalar=0.0,
                            op0=ALU.mult, op1=ALU.add, accum_out=score[:, h, i0 + i:i0 + i + 1])
                    ins.then_inc(dt[gp], 1)

                with dve.Fori(0, L) as it:
                    ch.enter(it)
                    for s in range(K2 + 5):
                        if s < K2:
                            h, g = divmod(s, NG)
                            i0, w = grp[g]
                            gp, c = s % 2, it * PER + (s // 2 + 1)
                            if g == 0:
                                dve.wait_ge(dn[h], it + 1)
                            dve.wait_ge(tr[gp], c)
                            nc.vector.tensor_tensor(ohs[:, h, g, :, 0:w], k.iota_x[:, :, 0:w],
                                                    slot[:, h, 0, i0:i0 + w].unsqueeze(1).to_broadcast([P, P, w]),
                                                    ALU.is_equal)
                            nc.vector.tensor_tensor(ohd[:, gp, :, 0:w], k.iota_x[:, :, 0:w],
                                                    slot[:, h, 1, i0:i0 + w].unsqueeze(1).to_broadcast([P, P, w]),
                                                    ALU.is_equal).then_inc(gen[gp], 1)
                            if g in PIECES:
                                dve_bin(ch, dve, PIECES[g], it * 2 + (h + 1), it * 2 + (h + 1), 1 - h)
                        if 0 <= s - 3 < K2:
                            weigh(it, s - 3)
                        if s == NG + 5 or s == K2 + 4:
                            h = 0 if s == NG + 5 else 1
                            dve.wait_ge(ex[h], it + 2)
                            dve.wait_ge(dn[h], it + 1)
                            split3(nc, ch, one(e0[:, bass.ds(it * 2 + h, 1), 0:NI]), ep[:, h, :, 0], ep[:, h, :, 1],
                                   ep[:, h, :, 2], rest[:]).then_inc(pt[h], 1)
                    ch.leave(L)
                dve.wait_ge(closed, 1)
                nc.vector.tensor_reduce(den_out[:, 0:NI], dps[:, 0:3 * NI].rearrange("p (i q) -> p i q", q=3), AX.X, ALU.add)

            @block.tensor
            def _(pe):
                pe.wait_ge(b_init, 1)
                nc.tensor.matmul(dps[:, 0:3 * NI].rearrange("p (i q) -> p i q", q=3), k.ident_b[:], zeros, start=True, stop=False).then_inc(opened, 1)
                pe_base(pe, 0)
                pe_slots(pe, 0)
                for h in range(2):
                    pe.sem_inc(tr[h], 1)
                    pe.sem_inc(dn[h], 1)
                    pe.sem_inc(zz[h], 1)
                with pe.Fori(0, L) as it:
                    for s in range(K2 + 6):
                        if s < K2:
                            h, g = divmod(s, NG)
                            i0, w = grp[g]
                            gp, c = s % 2, it * PER + (s // 2 + 1)
                            pe.wait_ge(gen[gp], c + 1)
                            pe.wait_ge(ev[gp], c)
                            for q in range(w):
                                nc.tensor.transpose(tp[:, gp, 0, q * P:(q + 1) * P], ohs[:, h, g, :, q], k.ident_b[:])
                                ins = nc.tensor.transpose(tp[:, gp, 1, q * P:(q + 1) * P], ohd[:, gp, :, q], k.ident_b[:])
                            ins.then_inc(tr[gp], 1)
                            if g == 1:
                                pe_base(pe, it * 2 + (h + 1))
                            if g == 11:
                                pe_slots(pe, it * 2 + (h + 1))
                        if 0 <= s - 1 < K2:
                            r = s - 1
                            h, g = divmod(r, NG)
                            i0, w = grp[g]
                            gp, c = r % 2, it * PER + (r // 2 + 1)
                            pe.wait_ge(ev[gp], c + 1)
                            pe.wait_ge(rl[gp], c)
                            if g == 0:
                                pe.wait_ge(qs[h], it + 2)
                            for i in range(w):
                                at = z[:, gp, i // 2, i % 2 * CZ:(i % 2 + 1) * CZ]
                                for q in range(3):
                                    nc.tensor.matmul(at, oht[:, gp, 1, i, :], qst[:, h, q, :], start=(q == 0), stop=False)
                                for q in range(3):
                                    ins = nc.tensor.matmul(at, oht[:, gp, 0, i, :], pq[:, i0 + i, q, 0:CZ],
                                                           start=False, stop=(q == 2))
                            ins.then_inc(zz[gp], 1)
                        if s == NG + 6 or s == K2 + 5:
                            h = 0 if s == NG + 6 else 1
                            pe.wait_ge(pt[h], it + 2)
                            for i in range(NI):
                                ins = nc.tensor.matmul(dps[:, 3 * i:3 * i + 3], ohs[:, h, i // GT, :, i % GT], ep[:, h, i, :],
                                                       start=False, stop=False, skip_group_check=True)
                            ins.then_inc(dn[h], 1)
                nc.tensor.matmul(dps[:, 0:3 * NI].rearrange("p (i q) -> p i q", q=3), k.ident_b[:], zeros, start=False, stop=True).then_inc(closed, 1)

            @block.scalar
            def _(act):
                for h in range(2):
                    act.sem_inc(ev[h], 1)
                    act.sem_inc(rl[h], 1)
                    act.sem_inc(ex[h], 1)
                    act.sem_inc(qs[h], 1)
                with act.Fori(0, L) as it:
                    for s in range(K2 + 4):
                        if s < K2:
                            h, g = divmod(s, NG)
                            w = grp[g][1]
                            gp, c = s % 2, it * PER + (s // 2 + 1)
                            if g == 0:
                                act.wait_ge(dn[h], it + 1)
                                nc.scalar.copy(qst[:, h], one(pq[:, bass.ds(it * 2 + h, 1), :, CZ:2 * CZ])).then_inc(qs[h], 1)
                            act.wait_ge(tr[gp], c + 1)
                            act.wait_ge(zz[gp], c)
                            nc.scalar.copy(oht[:, gp, :, 0:w, :].rearrange("p a w n -> p a (w n)"), tp[:, gp, :, 0:w * P]
                                           ).then_inc(ev[gp], 1)
                        if 0 <= s - 1 < K2:
                            r = s - 1
                            w = grp[r % NG][1]
                            gp, c = r % 2, it * PER + (r // 2 + 1)
                            act.wait_ge(zz[gp], c + 1)
                            act.wait_ge(dt[gp], c)
                            out = rz[:, gp].rearrange("p (b i) c -> p b i c", b=2) if w == GT else rz[:, gp, 0:w]
                            nc.scalar.activation(out, bins_of(z[:, gp], w), ACT.Relu).then_inc(rl[gp], 1)
                        if s == NG + 3 or s == K2 + 3:
                            h = 0 if s == NG + 3 else 1
                            r = NG - 1 if h == 0 else K2 - 1
                            act.wait_ge(dt[r % 2], it * PER + (r // 2 + 2))
                            nc.scalar.activation(one(e0[:, bass.ds(it * 2 + h, 1), 0:NI]), score[:, h, :], ACT.Exp
                                                 ).then_inc(ex[h], 1)

            @block.gpsimd
            def _(pool):
                pool_bin(pool, 0, 0)
                with pool.Fori(0, L) as it:
                    for h in range(2):
                        pool_bin(pool, it * 2 + (h + 1), it * 2 + (h + 1))


STAGE = {0: 0, 8: 1}


def layer0_sums(nc, k, xs, e0, S):
    NI = k.NI - 1
    grp = groups_of(NI)
    NG = len(grp)
    K2, PER, L = 2 * NG, NG, k.NI // 2
    with Stage(nc) as ctx:
        def sb(name, shape, dt=F32):
            return ctx.enter_context(nc.sbuf_tensor(f"p2_{name}", shape, dt))

        def ps(name, shape, dt=F32):
            return ctx.enter_context(nc.psum_tensor(f"p2_{name}", shape, dt))

        def pair(name):
            return [ctx.semaphore(f"p2_{name}{h}") for h in range(2)]

        win = sb("window", [P, 2, 3, NI])
        ohs = sb("ohs", [P, 2, GT, P])
        ohd = sb("ohd", [P, 2, GT, P])
        wsb = sb("wsb", [P, 2, GT, P])
        wps = ps("wps", [P, 2, GT * P])
        acc = ps("acc", [P, 2, 512])
        staged, gen, wm, wc, used, kept = (pair(n) for n in (
            "staged", "onehot", "weights", "weights_in_sbuf", "weights_used", "kept"))
        with nc.Block() as block:
            @block.vector
            def _(dve):
                for h in range(2):
                    dve.sem_inc(gen[h], 1)
                    dve.sem_inc(kept[h], 1)
                with dve.Fori(0, L) as it:
                    for s in range(K2 + 3):
                        if s < K2:
                            h, g = divmod(s, NG)
                            i0, w = grp[g]
                            gp, c = s % 2, it * PER + (s // 2 + 1)
                            dve.wait_ge(staged[h], it + 2)
                            dve.wait_ge(wm[gp], c)
                            nc.vector.tensor_tensor(ohs[:, gp, 0:w, :], k.iota[:].unsqueeze(1).to_broadcast([P, w, P]),
                                                    win[:, h, 0, i0:i0 + w].unsqueeze(2).to_broadcast([P, w, P]),
                                                    ALU.is_equal)
                            for i in range(w):
                                ins = nc.vector.tensor_scalar(ohd[:, gp, i, :], k.iota[:], win[:, h, 1, i0 + i:i0 + i + 1],
                                                              win[:, h, 2, i0 + i:i0 + i + 1], ALU.is_equal, ALU.mult)
                            ins.then_inc(gen[gp], 1)
                        if s == NG + 2 or s == K2 + 2:
                            h = 0 if s == NG + 2 else 1
                            r = (h + 1) * NG - 1
                            dve.wait_ge(used[r % 2], it * PER + (r // 2 + 2))
                            nc.vector.tensor_copy(S[:, bass.ds(it * 2 + h, 1), :], acc[:, h, 0:C].unsqueeze(1)
                                                  ).then_inc(kept[h], 1)

            @block.tensor
            def _(pe):
                for h in range(2):
                    pe.sem_inc(wm[h], 1)
                    pe.sem_inc(used[h], 1)
                with pe.Fori(0, L) as it:
                    for s in range(K2 + 1):
                        if s < K2:
                            w = grp[s % NG][1]
                            gp, c = s % 2, it * PER + (s // 2 + 1)
                            pe.wait_ge(gen[gp], c + 1)
                            pe.wait_ge(wc[gp], c)
                            for i in range(w):
                                ins = nc.tensor.matmul(wps[:, gp, i * P:(i + 1) * P], ohs[:, gp, i, :], ohd[:, gp, i, :],
                                                       start=True, stop=True)
                            ins.then_inc(wm[gp], 1)
                        if s >= 1:
                            r = s - 1
                            h, g = divmod(r, NG)
                            i0, w = grp[g]
                            gp, c = r % 2, it * PER + (r // 2 + 1)
                            pe.wait_ge(wc[gp], c + 1)
                            if g == 0:
                                pe.wait_ge(kept[h], it + 1)
                            for i in range(w):
                                ins = nc.tensor.matmul(acc[:, h, 0:C], wsb[:, gp, i, :], xs[:, i0 + i, :],
                                                       start=(i0 + i == 0), stop=(i0 + i == NI - 1))
                            ins.then_inc(used[gp], 1)

            @block.scalar
            def _(act):
                for h in range(2):
                    act.sem_inc(wc[h], 1)
                    act.sem_inc(staged[h], 1)
                with act.Fori(0, L) as it:
                    for s in range(K2):
                        h, g = divmod(s, NG)
                        w = grp[g][1] * P
                        gp, c = s % 2, it * PER + (s // 2 + 1)
                        if s in STAGE:
                            v = STAGE[s]
                            for q in range(2):
                                act.wait_ge(gen[q], it * PER + 1)
                            n = it * 2 + v
                            nc.scalar.copy(win[:, v, 0, :], one(k.SLs[:, bass.ds(n, 1), 0:NI]))
                            nc.scalar.copy(win[:, v, 1, :], one(k.SLd[:, bass.ds(n, 1), 0:NI]))
                            nc.scalar.copy(win[:, v, 2, :], one(e0[:, bass.ds(n, 1), 0:NI])).then_inc(staged[v], 1)
                        act.wait_ge(wm[gp], c + 1)
                        act.wait_ge(used[gp], c)
                        nc.scalar.copy(wsb[:, gp].rearrange("p a b -> p (a b)")[:, 0:w], wps[:, gp, 0:w]
                                       ).then_inc(wc[gp], 1)


def layer1_scores(nc, k, hp, s1):
    NI = k.NI - 1
    grp = groups_of(NI)
    NG = len(grp)
    K2, PER, L = 2 * NG, NG, k.NI // 2
    HP = 3 * HEADS
    with Stage(nc) as ctx:
        def sb(name, shape, dt=F32):
            return ctx.enter_context(nc.sbuf_tensor(f"p3_{name}", shape, dt))

        def ps(name, shape, dt=F32):
            return ctx.enter_context(nc.psum_tensor(f"p3_{name}", shape, dt))

        def sem(name):
            return ctx.semaphore(f"p3_{name}")

        def pair(name):
            return [sem(f"{name}{h}") for h in range(2)]

        win = sb("window", [P, 2, 2, NI], BF16)
        htw = sb("htw", [P, 2, 3, HEADS], BF16)
        oht = sb("oht", [P, 2, 2, GT, P], BF16)
        sm = sb("sm", [P, NI, HEADS])
        tp = ps("tp", [P, 2, 2, GT * P], BF16)
        FIRST = 40
        sp_ = ps("scores", [P, 2, 2, 512])
        staged, tr, ev, gt, kept = (pair(n) for n in ("staged", "turned", "onehot", "gathered", "kept"))
        chain, padded = sem("chain"), sem("padded")
        with nc.Block() as block:
            @block.vector
            def _(dve):
                ch = Chain(dve, chain, 2 * 2)
                nc.vector.memset(s1[:, :, NI:, :], 0.0)
                for h in range(2):
                    dve.sem_inc(ev[h], 1)
                    dve.sem_inc(kept[h], 1)
                with dve.Fori(0, L) as it:
                    ch.enter(it)
                    for s in range(K2 + 3):
                        if s < K2:
                            h, g = divmod(s, NG)
                            i0, w = grp[g]
                            gp, c = s % 2, it * PER + (s // 2 + 1)
                            dve.wait_ge(tr[gp], c + 1)
                            dve.wait_ge(gt[gp], c)
                            nc.vector.tensor_scalar(oht[:, gp, :, 0:w, :].rearrange("p a w n -> p a (w n)"),
                                                    tp[:, gp, :, 0:w * P], k.part[:, 0:1], None, ALU.is_equal
                                                    ).then_inc(ev[gp], 1)
                        if s == NG + 2 or s == K2 + 2:
                            h = 0 if s == NG + 2 else 1
                            r = (h + 1) * NG - 1
                            dve.wait_ge(gt[r % 2], it * PER + (r // 2 + 2))
                            for bank, a, b in ((0, 0, FIRST), (1, FIRST, NI)):
                                ins = nc.vector.tensor_reduce(
                                    sm[:, a:b, :], sp_[:, h, bank, 0:(b - a) * HP].rearrange(
                                        "p (i q e) -> p i e q", q=3, e=HEADS), AX.X, ALU.add)
                            ch.link(ins)
                            ch.link(nc.vector.scalar_tensor_tensor(
                                out=s1[:, bass.ds(it * 2 + h, 1), 0:NI, :].rearrange("p a i e -> p (a i e)"),
                                in0=sm[:].rearrange("p i e -> p (i e)"), scalar=ALPHA,
                                in1=sm[:].rearrange("p i e -> p (i e)"), op0=ALU.mult, op1=ALU.max))
                            dve.sem_inc(kept[h], 1)
                    ch.leave(L)

            @block.tensor
            def _(pe):
                for h in range(2):
                    pe.sem_inc(tr[h], 1)
                    pe.sem_inc(gt[h], 1)
                with pe.Fori(0, L) as it:
                    for s in range(K2 + 2):
                        if s < K2:
                            h, g = divmod(s, NG)
                            i0, w = grp[g]
                            gp, c = s % 2, it * PER + (s // 2 + 1)
                            if g == 0:
                                pe.wait_ge(staged[h], it + 1)
                            pe.wait_ge(ev[gp], c)
                            for a in range(2):
                                for q in range(w):
                                    ins = nc.tensor.transpose(tp[:, gp, a, q * P:(q + 1) * P],
                                                              win[:, h, a, i0 + q:i0 + q + 1].to_broadcast([P, P]),
                                                              k.ident_b[:])
                            ins.then_inc(tr[gp], 1)
                        if s >= 2:
                            r = s - 2
                            h, g = divmod(r, NG)
                            i0, w = grp[g]
                            gp, c = r % 2, it * PER + (r // 2 + 1)
                            pe.wait_ge(ev[gp], c + 1)
                            if g == 0:
                                pe.wait_ge(kept[h], it + 1)
                            for q in range(w):
                                i = i0 + q
                                bank, at = (0, i) if i < FIRST else (1, i - FIRST)
                                o = sp_[:, h, bank, at * HP:(at + 1) * HP]
                                nc.tensor.matmul(o, oht[:, gp, 0, q, :], hp[:, i, :, C:C + HEADS], start=True, stop=False)
                                ins = nc.tensor.matmul(o, oht[:, gp, 1, q, :], htw[:, h], start=False, stop=True)
                            ins.then_inc(gt[gp], 1)

            @block.scalar
            def _(act):
                def stage(n, v):
                    row = slice(n, n + 1) if isinstance(n, int) else bass.ds(n, 1)
                    nc.scalar.copy(win[:, v, 0, :], one(k.SLs[:, row, 0:NI]))
                    nc.scalar.copy(win[:, v, 1, :], one(k.SLd[:, row, 0:NI]))
                    nc.scalar.copy(htw[:, v], one(hp[:, row, :, C + HEADS:C + 2 * HEADS])).then_inc(staged[v], 1)

                act.wait_ge(padded, 1)
                stage(0, 0)
                with act.Fori(0, L) as it:
                    for q in range(2):
                        act.wait_ge(tr[q], it * PER + 1)
                        act.wait_ge(gt[q], it * PER + 1)
                    stage(it * 2 + 1, 1)
                    for r in (NG - 2, NG - 1):
                        act.wait_ge(tr[r % 2], it * PER + (r // 2 + 2))
                        act.wait_ge(gt[r % 2], it * PER + (r // 2 + 2))
                    stage(it * 2 + 2, 0)

            @block.gpsimd
            def _(pool):
                nc.gpsimd.memset(hp[:, k.NI:, :, :], 0.0).then_inc(padded, 1)


def layer1_weights(nc, k, s1, pen):
    with Stage(nc) as ctx:
        s = {n: ctx.semaphore("p3b_" + n) for n in ("chain", "top", "all", "neg")}
        top = ctx.enter_context(nc.sbuf_tensor("p3b_top", [P, 2], F32))
        A = k.NI
        flat = s1[:, 0:A].rearrange("p a i e -> p (a i e)")
        with nc.Block() as block:
            @block.vector
            def _(dve):
                ch = Chain(dve, s["chain"])
                ch.link(nc.vector.tensor_scalar(pen[:, 0:A], k.SLs[:, 0:A], 0.0, NEVER, ALU.is_lt, ALU.mult))
                v = s1[:, 0:A].rearrange("p a i e -> p (a i) e")
                ch.link(nc.vector.tensor_tensor(v, v, pen[:, 0:A].rearrange("p a i -> p (a i)").unsqueeze(2)
                                                .to_broadcast([P, A * k.NI, HEADS]), ALU.add))
                nc.vector.tensor_reduce(top[:, 0:1], flat, AX.X, ALU.max).then_inc(s["top"], 1)
                dve.wait_ge(s["all"], 1)
                nc.vector.tensor_scalar(top[:, 1:2], top[:, 1:2], -1.0, None, ALU.mult).then_inc(s["neg"], 1)

            @block.gpsimd
            def _(pool):
                pool.wait_ge(s["top"], 1)
                nc.gpsimd.partition_all_reduce(top[:, 1:2], top[:, 0:1], P, RMAX).then_inc(s["all"], 1)

            @block.scalar
            def _(act):
                act.wait_ge(s["neg"], 1)
                nc.scalar.activation(flat, flat, ACT.Exp, bias=top[:, 1:2])


def layer1_sums(nc, k, hp, s1, S, den4):
    NI = k.NI - 1
    grp = groups_of(NI)
    NG = len(grp)
    K2, PER, L = 2 * NG, NG, k.NI // 2
    CW = C + HEADS
    with Stage(nc) as ctx:
        def sb(name, shape, dt=F32):
            return ctx.enter_context(nc.sbuf_tensor(f"p4_{name}", shape, dt))

        def ps(name, shape, dt=F32):
            return ctx.enter_context(nc.psum_tensor(f"p4_{name}", shape, dt))

        def pair(name):
            return [ctx.semaphore(f"p4_{name}{h}") for h in range(2)]

        win = sb("window", [P, 2, 2, NI], BF16)
        wgt = sb("weights", [P, 2, NI, HEADS])
        ohd = sb("ohd", [P, 2, P, GT], BF16)
        oht = sb("oht", [P, 2, GT, P], BF16)
        ohs = sb("ohs", [P, 2, GT, P])
        msg = sb("msg", [P, 2, GT, CW])
        tp = ps("tp", [P, 2, 2 * GT * P], BF16)
        gps = ps("gathered", [P, 2, GT * P])
        acc = ps("acc", [P, 2, 512])
        staged, gen, tr, ev, gt, ms, ag, kept = (pair(n) for n in (
            "staged", "onehot", "turned", "turned_in_sbuf", "gathered", "messages", "added", "kept"))
        wcp = pair("weights_copied")
        with nc.Block() as block:
            @block.vector
            def _(dve):
                for h in range(2):
                    dve.sem_inc(gen[h], 1)
                    dve.sem_inc(ms[h], 1)
                    dve.sem_inc(kept[h], 1)
                with dve.Fori(0, L) as it:
                    for s in range(K2 + 4):
                        if s < K2:
                            h, g = divmod(s, NG)
                            i0, w = grp[g]
                            gp, c = s % 2, it * PER + (s // 2 + 1)
                            dve.wait_ge(staged[h], it + 2)
                            dve.wait_ge(tr[gp], c)
                            nc.vector.tensor_tensor(ohd[:, gp, :, 0:w], k.iota_x[:, :, 0:w],
                                                    win[:, h, 1, i0:i0 + w].unsqueeze(1).to_broadcast([P, P, w]),
                                                    ALU.is_equal).then_inc(gen[gp], 1)
                        if 0 <= s - 2 < K2:
                            r = s - 2
                            h, g = divmod(r, NG)
                            i0, w = grp[g]
                            gp, c = r % 2, it * PER + (r // 2 + 1)
                            dve.wait_ge(gt[gp], c + 1)
                            dve.wait_ge(ag[gp], c)
                            nc.vector.tensor_tensor(ohs[:, gp, 0:w, :], k.iota[:].unsqueeze(1).to_broadcast([P, w, P]),
                                                    win[:, h, 0, i0:i0 + w].unsqueeze(2).to_broadcast([P, w, P]),
                                                    ALU.is_equal)
                            nc.vector.tensor_tensor(
                                msg[:, gp, 0:w, 0:C].rearrange("p w (e d) -> p w e d", e=HEADS),
                                gps[:, gp, 0:w * P].rearrange("p (w e d) -> p w e d", w=w, e=HEADS),
                                wgt[:, h, i0:i0 + w, :].unsqueeze(3).to_broadcast([P, w, HEADS, D]),
                                ALU.mult).then_inc(ms[gp], 1)
                        if s == NG + 3 or s == K2 + 3:
                            h = 0 if s == NG + 3 else 1
                            r = (h + 1) * NG - 1
                            dve.wait_ge(ag[r % 2], it * PER + (r // 2 + 2))
                            nc.vector.tensor_copy(S[:, bass.ds(it * 2 + h, 1), :], acc[:, h, 0:C].unsqueeze(1))
                            nc.vector.tensor_copy(den4[:, bass.ds(it * 2 + h, 1), :], acc[:, h, C:CW].unsqueeze(1)
                                                  ).then_inc(kept[h], 1)

            @block.tensor
            def _(pe):
                for h in range(2):
                    pe.sem_inc(tr[h], 1)
                    pe.sem_inc(gt[h], 1)
                    pe.sem_inc(ag[h], 1)
                with pe.Fori(0, L) as it:
                    for s in range(K2 + 2):
                        if s < K2:
                            w = grp[s % NG][1]
                            gp, c = s % 2, it * PER + (s // 2 + 1)
                            pe.wait_ge(gen[gp], c + 1)
                            pe.wait_ge(ev[gp], c)
                            for q in range(w):
                                ins = nc.tensor.transpose(tp[:, gp, q * P:(q + 1) * P], ohd[:, gp, :, q], k.ident_b[:])
                            ins.then_inc(tr[gp], 1)
                        if 0 <= s - 1 < K2:
                            r = s - 1
                            h, g = divmod(r, NG)
                            i0, w = grp[g]
                            gp, c = r % 2, it * PER + (r // 2 + 1)
                            pe.wait_ge(ev[gp], c + 1)
                            pe.wait_ge(ms[gp], c)
                            for i in range(w):
                                for q in range(3):
                                    ins = nc.tensor.matmul(gps[:, gp, i * P:(i + 1) * P], oht[:, gp, i, :],
                                                           hp[:, i0 + i, q, 0:C], start=(q == 0), stop=(q == 2))
                            ins.then_inc(gt[gp], 1)
                        if 0 <= s - 2 < K2:
                            r = s - 2
                            h, g = divmod(r, NG)
                            i0, w = grp[g]
                            gp, c = r % 2, it * PER + (r // 2 + 1)
                            pe.wait_ge(ms[gp], c + 1)
                            pe.wait_ge(wcp[gp], c + 1)
                            if g == 0:
                                pe.wait_ge(kept[h], it + 1)
                            for i in range(w):
                                ins = nc.tensor.matmul(acc[:, h, 0:CW], ohs[:, gp, i, :], msg[:, gp, i, :],
                                                       start=(i0 + i == 0), stop=(i0 + i == NI - 1))
                            ins.then_inc(ag[gp], 1)

            @block.scalar
            def _(act):
                for h in range(2):
                    act.sem_inc(ev[h], 1)
                    act.sem_inc(staged[h], 1)
                    act.sem_inc(wcp[h], 1)
                with act.Fori(0, L) as it:
                    for s in range(K2 + 1):
                        if s < K2:
                            h, g = divmod(s, NG)
                            w = grp[g][1] * P
                            gp, c = s % 2, it * PER + (s // 2 + 1)
                            if s in STAGE:
                                v = STAGE[s]
                                for q in range(2):
                                    act.wait_ge(ms[q], it * PER + 1)
                                n = it * 2 + v
                                nc.scalar.copy(win[:, v, 0, :], k.SLs[:, 0:NI, bass.ds(n, 1)].rearrange("p a b -> p (a b)"))
                                nc.scalar.copy(win[:, v, 1, :], k.SLd[:, 0:NI, bass.ds(n, 1)].rearrange("p a b -> p (a b)"))
                                nc.scalar.copy(wgt[:, v], s1[:, 0:NI, bass.ds(n, 1), :].rearrange("p a b e -> p a (b e)")
                                               ).then_inc(staged[v], 1)
                            act.wait_ge(tr[gp], c + 1)
                            act.wait_ge(gt[gp], c)
                            nc.scalar.copy(oht[:, gp].rearrange("p a b -> p (a b)")[:, 0:w], tp[:, gp, 0:w]
                                           ).then_inc(ev[gp], 1)
                        if s >= 1:
                            r = s - 1
                            h, g = divmod(r, NG)
                            i0, w = grp[g]
                            gp, c = r % 2, it * PER + (r // 2 + 1)
                            act.wait_ge(ag[gp], c)
                            act.wait_ge(staged[h], it + 2)
                            nc.scalar.copy(msg[:, gp, 0:w, C:CW], wgt[:, h, i0:i0 + w, :]).then_inc(wcp[gp], 1)



G = 8
COPIES = 4


class General:

    def __init__(self, nc, k, ctx, tag, src, dst):
        self.tag = tag
        self.T = src.shape[0] // EP
        self.ITERS = self.T // (2 * G)
        assert self.ITERS * 2 * G == self.T
        self.NP = k.NI * P

        def sb(name, shape, dt=F32):
            return ctx.enter_context(nc.sbuf_tensor(f"{tag}_{name}", shape, dt))

        self.src, self.dst = sb("src", [P, self.T], I32), sb("dst", [P, self.T], I32)
        self.below = sb("below", [P, P])
        self.dummy = sb("own_row", [P, 1])
        self.idx_a, self.idx_b = sb("idx_a", [P, 2, G], U32), sb("idx_b", [P, 2, G], U32)
        self.ga, self.gb = sb("rows_a", [P, 2, G, C]), sb("rows_b", [P, 2, G, C])
        self.wk, self.wk2, self.wk3 = (sb(n, [P, G, C]) for n in ("work1", "work2", "work3"))
        self.bank_a = ctx.enter_context(nc.psum_tensor(f"{tag}_bank_a", [P, 2, 512], F32))
        self.bank_b = ctx.enter_context(nc.psum_tensor(f"{tag}_bank_b", [P, 2, 512], F32))
        self.bank_c = ctx.enter_context(nc.psum_tensor(f"{tag}_bank_c", [P, 512], F32))
        self.turns = ctx.semaphore(f"{tag}_pool_turns")
        self.accs = [nc.dram_tensor(f"{tag}_acc{c}", (self.NP + P, C), F32, kind="Internal").ap()
                     for c in range(COPIES)]
        self.prepare(nc, k, ctx, src, dst)

    def table(self, nc, name, width):
        return nc.dram_tensor(f"{self.tag}_{name}", (self.NP, width), F32, kind="Internal").ap()

    def blocks(self, table):
        return table[0:self.NP].rearrange("(b p) c -> p b c", p=P)

    def prepare(self, nc, k, ctx, src, dst):
        tag = self.tag
        zero = k.S_zero
        ld, zs, ready, io, chain = (ctx.semaphore(f"{tag}_{n}") for n in (
            "loaded", "cleared", "zeros_ready", "part_ready", "part_chain"))
        part_i = ctx.enter_context(nc.sbuf_tensor(f"{tag}_part_i", [P, 1], I32))
        part = ctx.enter_context(nc.sbuf_tensor(f"{tag}_part", [P, 1], F32))
        with nc.Block() as block:
            @block.sync
            def _(sp):
                sp.dma_start(self.src[0:EP, :], src.rearrange("(p t) -> p t", p=EP)).then_inc(ld, 16)
                sp.dma_start(self.dst[0:EP, :], dst.rearrange("(p t) -> p t", p=EP)).then_inc(ld, 16)
                sp.wait_ge(ld, 32)

            @block.scalar
            def _(act):
                act.wait_ge(ready, 1)
                for acc in self.accs:
                    act.dma_start(self.blocks(acc), zero[:]).then_inc(zs, 16)
                act.wait_ge(zs, 16 * COPIES)

            @block.gpsimd
            def _(pool):
                nc.gpsimd.iota(part_i[:], [[1, 1]], base=0, channel_multiplier=1).then_inc(io, 1)

            @block.vector
            def _(dve):
                nc.vector.memset(zero[:], 0.0).then_inc(ready, 1)
                dve.wait_ge(io, 1)
                nc.vector.tensor_copy(part[:], part_i[:]).then_inc(chain, 1)
                dve.wait_ge(chain, 1)
                nc.vector.tensor_scalar(self.dummy[:], part[:], float(self.NP), None, ALU.add)
                nc.vector.tensor_scalar(self.below[:], k.iota[:], part[:, 0:1], None, ALU.is_lt)


def general_project(nc, k, g, name, X, weights, stores):
    width = weights.shape[1]
    tag = f"{g.tag}_{name}"
    with Stage(nc) as ctx:
        def pair(n):
            return [ctx.semaphore(f"{tag}_{n}{h}") for h in range(2)]

        xb, xt = (ctx.enter_context(nc.sbuf_tensor(f"{tag}_{n}", [P, 2, C], F32)) for n in ("block", "turned"))
        stage = ctx.enter_context(nc.sbuf_tensor(f"{tag}_stage", [P, 2, width], F32))
        picked, turned, xt_ok, mul, staged, stored = (pair(n) for n in (
            "picked", "turned_ok", "turned_in_sbuf", "product", "staged", "stored"))
        PER = 16 * len(stores)
        with nc.Block() as block:
            @block.vector
            def _(dve):
                with dve.Fori(0, k.NI // 2) as it:
                    for h in range(2):
                        dve.wait_ge(turned[h], it + 1)
                        nc.vector.tensor_copy(xb[:, h:h + 1, :], X[:, bass.ds(it * 2 + h, 1), :]
                                              ).then_inc(picked[h], 1)

            @block.tensor
            def _(pe):
                for h in range(2):
                    pe.sem_inc(turned[h], 1)
                    pe.sem_inc(mul[h], 1)
                with pe.Fori(0, k.NI // 2) as it:
                    for h in range(2):
                        pe.wait_ge(picked[h], it + 1)
                        pe.wait_ge(xt_ok[h], it + 1)
                        nc.tensor.transpose(g.bank_a[:, h, 0:C], xb[:, h, :], k.ident[:]).then_inc(turned[h], 1)
                        pe.wait_ge(xt_ok[h], it + 2)
                        pe.wait_ge(staged[h], it + 1)
                        nc.tensor.matmul(g.bank_b[:, h, 0:width], xt[:, h, :], weights, start=True, stop=True
                                         ).then_inc(mul[h], 1)

            @block.scalar
            def _(act):
                for h in range(2):
                    act.sem_inc(xt_ok[h], 1)
                    act.sem_inc(staged[h], 1)
                with act.Fori(0, k.NI // 2) as it:
                    for h in range(2):
                        act.wait_ge(turned[h], it + 2)
                        act.wait_ge(mul[h], it + 1)
                        nc.scalar.copy(xt[:, h, :], g.bank_a[:, h, 0:C]).then_inc(xt_ok[h], 1)
                        act.wait_ge(mul[h], it + 2)
                        nc.scalar.copy(stage[:, h, :], g.bank_b[:, h, 0:width]).then_inc(staged[h], 1)
                        act.wait_ge(staged[h], it + 2)
                        for tab, a, b in stores:
                            act.dma_start(tab[bass.ds((it * 2 + h) * P, P)], stage[:, h, a:b]).then_inc(stored[h], 16)
                        act.wait_ge(stored[h], (it + 1) * PER)


def general_scores(nc, k, g, tab_a, tab_b, width, combine, steps):
    with Stage(nc) as ctx:
        def pair(n):
            return [ctx.semaphore(f"{g.tag}_score_{n}{h}") for h in range(2)]

        idx_ready, gathered, used = (pair(n) for n in ("indices", "gathered", "used"))
        chain = ctx.semaphore(f"{g.tag}_score_chain")
        PER = 16 * 2 * G
        with nc.Block() as block:
            @block.scalar
            def _(act):
                with act.Fori(0, g.ITERS) as it:
                    for h in range(2):
                        act.wait_ge(used[h], it + 1)
                        for idx, edges in ((g.idx_a, g.src), (g.idx_b, g.dst)):
                            nc.scalar.copy(idx[0:EP, h, :], edges[0:EP, bass.ds(it * (2 * G) + h * G, G)]
                                           ).then_inc(idx_ready[h], 1)

            @block.gpsimd
            def _(pool):
                with pool.Fori(0, g.ITERS) as it:
                    for h in range(2):
                        pool.wait_ge(idx_ready[h], it * 2 + 2)
                        pool.wait_ge(used[h], it + 1)
                        pool.sem_inc(g.turns, 1)
                        for q in range(G):
                            for rows, idx, tab in ((g.ga, g.idx_a, tab_a), (g.gb, g.idx_b, tab_b)):
                                pool.indirect_dma_start(
                                    out=rows[0:EP, h, q, 0:width], out_offset=None, in_=tab,
                                    in_offset=bass.IndirectOffsetOnAxis(ap=idx[0:EP, h, q:q + 1], axis=0),
                                ).then_inc(gathered[h], 16)

            @block.vector
            def _(dve):
                ch = Chain(dve, chain, 2 * steps)
                for h in range(2):
                    dve.sem_inc(used[h], 1)
                with dve.Fori(0, g.ITERS) as it:
                    ch.enter(it)
                    for h in range(2):
                        dve.wait_ge(gathered[h], (it + 1) * PER)
                        dve.wait_ge(used[1 - h], it + h + 1)
                        combine(ch.link, h, it * (2 * G) + h * G).then_inc(used[h], 1)
                    ch.leave(g.ITERS)


def general_denominators(nc, k, g, weight, heads, prepare_weights, den):
    HI, K = k.NI, 4
    L, W = g.T // (2 * K), heads * HI
    with Stage(nc) as ctx:
        def sb(name, shape, dt=F32):
            return ctx.enter_context(nc.sbuf_tensor(f"{g.tag}_den_{name}", shape, dt))

        def sem(name):
            return ctx.semaphore(f"{g.tag}_den_{name}")

        part_i, lo_f, hi_f = sb("part_i", [P, g.T], I32), sb("lo", [P, g.T]), sb("hi", [P, g.T])
        oh, ohw = sb("oh", [P, 2, K, P]), sb("ohw", [P, 2, K, heads * HI])
        zero = sb("zero", [P, W])
        ready, chain, opened, closed, zeros = (sem(n) for n in ("weights", "chain", "opened", "closed", "zeros"))
        hot, taken = ([sem(f"{n}{h}") for h in range(2)] for n in ("onehot", "taken"))
        with nc.Block() as block:
            @block.scalar
            def _(act):
                prepare_weights().then_inc(ready, 1)

            @block.vector
            def _(dve):
                ch = Chain(dve, chain, 2)
                nc.vector.memset(zero[:], 0.0).then_inc(zeros, 1)
                ch.link(nc.vector.tensor_scalar(part_i[0:EP], g.src[0:EP], P - 1, None, ALU.bitwise_and))
                ch.link(nc.vector.tensor_copy(lo_f[0:EP], part_i[0:EP]))
                ch.link(nc.vector.tensor_scalar(part_i[0:EP], g.src[0:EP], 7, None, ALU.logical_shift_right))
                ch.link(nc.vector.tensor_copy(hi_f[0:EP], part_i[0:EP]))
                dve.wait_ge(ready, 1)
                for h in range(2):
                    dve.sem_inc(hot[h], 1)
                with dve.Fori(0, L) as it:
                    ch.enter(it)
                    for h in range(2):
                        t0 = it * (2 * K) + h * K
                        dve.wait_ge(taken[h], it + 1)
                        dve.wait_ge(hot[1 - h], it + h + 1)
                        nc.vector.tensor_tensor(
                            oh[0:EP, h], k.iota[0:EP].unsqueeze(1).to_broadcast([EP, K, P]),
                            lo_f[0:EP, bass.ds(t0, K)].unsqueeze(2).to_broadcast([EP, K, P]), ALU.is_equal)
                        v = g.wk[0:EP].rearrange("p g c -> p (g c)")[:, 0:K * HI].rearrange("p (k n) -> p k n", k=K)
                        ch.link(nc.vector.tensor_tensor(
                            v, k.iota[0:EP, 0:HI].unsqueeze(1).to_broadcast([EP, K, HI]),
                            hi_f[0:EP, bass.ds(t0, K)].unsqueeze(2).to_broadcast([EP, K, HI]), ALU.is_equal))
                        for q in range(heads):
                            ins = nc.vector.tensor_tensor(
                                ohw[0:EP, h, :, q * HI:(q + 1) * HI], v,
                                weight(q, t0, K).unsqueeze(2).to_broadcast([EP, K, HI]), ALU.mult)
                        ins.then_inc(hot[h], 1)
                    ch.leave(L)
                dve.wait_ge(closed, 1)
                nc.vector.tensor_copy(den[:, 0:W], g.bank_c[:, 0:W])

            @block.tensor
            def _(pe):
                pe.wait_ge(zeros, 1)
                nc.tensor.matmul(g.bank_c[:, 0:W], k.ones[:], zero[:], start=True, stop=False).then_inc(opened, 1)
                for h in range(2):
                    pe.sem_inc(taken[h], 1)
                with pe.Fori(0, L) as it:
                    for h in range(2):
                        pe.wait_ge(hot[h], it + 2)
                        for q in range(K):
                            ins = nc.tensor.matmul(g.bank_c[:, 0:W], oh[0:EP, h, q, :], ohw[0:EP, h, q, 0:W],
                                                   start=False, stop=False)
                        ins.then_inc(taken[h], 1)
                nc.tensor.matmul(g.bank_c[:, 0:W], k.ones[:], zero[:], start=False, stop=True).then_inc(closed, 1)


def general_sums(nc, k, g, table, pick, key, weigh, S, R):
    with Stage(nc) as ctx:
        def sb(name, shape, dt=F32):
            return ctx.enter_context(nc.sbuf_tensor(f"{g.tag}_sum_{name}", shape, dt))

        def sem(name):
            return ctx.semaphore(f"{g.tag}_sum_{name}")

        def pair(name):
            return [sem(f"{name}{h}") for h in range(2)]

        key_f, dup, dmy = sb("key", [P, G]), sb("dup", [P, G]), sb("target", [P, G])
        idx_ready, gathered, msg_ready, diag_ready, rows_ready, same_ready, summed, out_ready = (pair(n) for n in (
            "indices", "gathered", "messages", "diagonals", "key_rows", "targets", "tile_sums", "sums_in_sbuf"))
        scattered = [sem(f"scattered{c}") for c in range(COPIES)]
        chain = sem("chain")
        PER, STEPS = 16 * G, 7
        SPI = 2 * G // COPIES
        key_rows = g.bank_a[0:EP].rearrange("p b n -> p (b n)").rearrange("p (k n) -> p k n", k=G)[:, :, 0:EP]
        sums = g.bank_b[0:EP].rearrange("p b n -> p (b n)").rearrange("p (k n) -> p k n", k=G)

        with nc.Block() as block:
            @block.scalar
            def _(act):
                for h in range(2):
                    act.sem_inc(out_ready[h], 1)
                with act.Fori(0, g.ITERS) as it:
                    for h in range(2):
                        act.wait_ge(msg_ready[h], it + 1)
                        nc.scalar.copy(g.idx_a[0:EP, h, :], pick[0:EP, bass.ds(it * (2 * G) + h * G, G)]
                                       ).then_inc(idx_ready[h], 1)
                    for h in range(2):
                        act.wait_ge(summed[h], it + 2)
                        for c in range(COPIES):
                            act.wait_ge(scattered[c], it * (16 * SPI) + 16)
                        nc.scalar.copy(g.gb[0:EP, h], sums).then_inc(out_ready[h], 1)

            @block.gpsimd
            def _(pool):
                for c in range(COPIES):
                    pool.dma_start(g.accs[c][g.NP:g.NP + P], k.S_zero[:, 0, :]).then_inc(scattered[c], 16)
                with pool.Fori(0, g.ITERS) as it:
                    for h in range(2):
                        pool.wait_ge(idx_ready[h], it + 1)
                        pool.wait_ge(msg_ready[h], it + 1)
                        pool.sem_inc(g.turns, 1)
                        for q in range(G):
                            pool.indirect_dma_start(
                                out=g.ga[0:EP, h, q, :], out_offset=None, in_=table,
                                in_offset=bass.IndirectOffsetOnAxis(ap=g.idx_a[0:EP, h, q:q + 1], axis=0),
                            ).then_inc(gathered[h], 16)
                    for h in range(2):
                        pool.wait_ge(same_ready[h], it + 2)
                        pool.wait_ge(out_ready[h], it + 2)
                        pool.sem_inc(g.turns, 1)
                        for q in range(G):
                            c, n = q % COPIES, (h * G + q) // COPIES
                            pool.wait_ge(scattered[c], it * (16 * SPI) + 16 * (n + 1))
                            pool.sem_inc(g.turns, 1)
                            pool.indirect_dma_start(
                                out=g.accs[c], out_offset=bass.IndirectOffsetOnAxis(ap=g.idx_b[0:EP, h, q:q + 1], axis=0),
                                in_=g.gb[0:EP, h, q, :], in_offset=None, compute_op=ALU.add,
                            ).then_inc(scattered[c], 16)
                for c in range(COPIES):
                    pool.wait_ge(scattered[c], 16 * (SPI * g.ITERS + 1))

            @block.vector
            def _(dve):
                ch = Chain(dve, chain, 2 * STEPS - 2)
                for h in range(2):
                    dve.sem_inc(msg_ready[h], 1)
                    dve.sem_inc(same_ready[h], 1)
                with dve.Fori(0, g.ITERS) as it:
                    ch.enter(it)
                    for h in range(2):
                        t0 = it * (2 * G) + h * G
                        dve.wait_ge(same_ready[1 - h], it + h + 1)
                        ch.link(nc.vector.tensor_copy(key_f[0:EP], key[0:EP, bass.ds(t0, G)]))
                        keys = key_f[0:EP].unsqueeze(2).to_broadcast([EP, G, EP])
                        nc.vector.tensor_tensor(
                            g.wk[0:EP, :, 0:EP], k.ident[0:EP, 0:EP].unsqueeze(1).to_broadcast([EP, G, EP]), keys,
                            ALU.mult).then_inc(diag_ready[h], 1)
                        dve.wait_ge(rows_ready[h], it + 1)
                        dve.wait_ge(summed[1 - h], it + h + 1)
                        ch.link(nc.vector.tensor_tensor(g.wk2[0:EP, :, 0:EP], key_rows, keys, ALU.is_equal))
                        ch.link(nc.vector.tensor_tensor(
                            g.wk[0:EP, :, 0:EP], g.wk2[0:EP, :, 0:EP],
                            g.below[0:EP, 0:EP].unsqueeze(1).to_broadcast([EP, G, EP]), ALU.mult))
                        ch.link(nc.vector.tensor_reduce(dup[0:EP], g.wk[0:EP, :, 0:EP], AX.X, ALU.add))
                        ch.link(nc.vector.tensor_scalar(dmy[0:EP], key_f[0:EP], -1.0, g.dummy[0:EP, 0:1], ALU.mult,
                                                        ALU.add))
                        ch.link(nc.vector.scalar_tensor_tensor(out=dmy[0:EP], in0=dup[0:EP], scalar=1.0, in1=dmy[0:EP],
                                                               op0=ALU.min, op1=ALU.mult))
                        for c in range(COPIES):
                            dve.wait_ge(scattered[c], it * (16 * SPI) + 16)
                        nc.vector.tensor_tensor(g.idx_b[0:EP, h, :], dmy[0:EP], key_f[0:EP], ALU.add
                                                ).then_inc(same_ready[h], 1)
                        dve.wait_ge(gathered[h], (it + 1) * PER)
                        weigh(g.wk3[0:EP], g.ga[0:EP, h], t0).then_inc(msg_ready[h], 1)
                    ch.leave(g.ITERS)

            @block.tensor
            def _(pe):
                for h in range(2):
                    pe.sem_inc(summed[h], 1)
                with pe.Fori(0, g.ITERS) as it:
                    for h in range(2):
                        pe.wait_ge(diag_ready[h], it + 1)
                        half = G // 2
                        for b in range(2):
                            ins = nc.tensor.matmul(
                                g.bank_a[0:EP, b, :].rearrange("p (k n) -> p k n", k=half)[:, :, 0:EP],
                                k.ones[0:EP, 0:EP], g.wk[0:EP, b * half:(b + 1) * half, 0:EP],
                                start=True, stop=True)
                        ins.then_inc(rows_ready[h], 1)
                        pe.wait_ge(msg_ready[h], it + 2)
                        pe.wait_ge(out_ready[1 - h], it + h + 1)
                        for q in range(G):
                            ins = nc.tensor.matmul(sums[:, q, :], g.wk2[0:EP, q, 0:EP], g.wk3[0:EP, q, :],
                                                   start=True, stop=True)
                        ins.then_inc(summed[h], 1)

        first, others, added = sem("first_loaded"), sem("others_loaded"), sem("added")
        with nc.Block() as block:
            @block.sync
            def _(sp):
                sp.dma_start(S[:], g.blocks(g.accs[0])).then_inc(first, 16)
                for c in range(1, COPIES):
                    if c > 1:
                        sp.wait_ge(added, c - 1)
                    sp.dma_start(R[:], g.blocks(g.accs[c])).then_inc(others, 16)
                sp.wait_ge(others, 16 * (COPIES - 1))

            @block.vector
            def _(dve):
                dve.wait_ge(first, 16)
                for c in range(1, COPIES):
                    dve.wait_ge(others, 16 * c)
                    nc.vector.tensor_tensor(S[:], S[:], R[:], ALU.add).then_inc(added, 1)
                    dve.wait_ge(added, c)


def general_layer0(nc, k, src, dst, X, a0, S, R, e0):
    e = e0[:].rearrange("p a b -> p (a b)")
    with Stage(nc) as ctx:
        k.S_zero = S
        g = General(nc, k, ctx, "g0", src, dst)
        p_tab, q_tab, xs_tab = (g.table(nc, n, C) for n in ("p_tab", "q_tab", "xs_tab"))
        a_row = ctx.enter_context(nc.sbuf_tensor("g0_a_row", [P, C], F32))
        den = ctx.enter_context(nc.sbuf_tensor("g0_den", [P, k.NI], F32))
        al, xs_st = ctx.semaphore("g0_a_loaded"), ctx.semaphore("g0_xs_stored")
        with nc.Block() as block:
            @block.sync
            def _(sp):
                sp.dma_start(a_row[:], a0.rearrange("c o -> (c o)").partition_broadcast(P)).then_inc(al, 16)
                sp.wait_ge(al, 16)
        general_project(nc, k, g, "pq", X, k.w0_ext.rearrange("c t o -> c (t o)"), [(p_tab, 0, C), (q_tab, CZ, CZ + C)])

        def combine(link, h, t0):
            link(nc.vector.tensor_tensor(g.wk[0:EP], g.ga[0:EP, h], g.gb[0:EP, h], ALU.add))
            link(nc.vector.scalar_tensor_tensor(out=g.wk2[0:EP], in0=g.wk[0:EP], scalar=ALPHA, in1=g.wk[0:EP],
                                                op0=ALU.mult, op1=ALU.max))
            link(nc.vector.tensor_tensor(g.wk[0:EP], g.wk2[0:EP],
                                         a_row[0:EP, :].unsqueeze(1).to_broadcast([EP, G, C]), ALU.mult))
            return nc.vector.tensor_reduce(e[0:EP, bass.ds(t0, G)], g.wk[0:EP], AX.X, ALU.add)

        general_scores(nc, k, g, p_tab, q_tab, C, combine, 3)
        general_denominators(nc, k, g, lambda q, t0, n: e[0:EP, bass.ds(t0, n)], 1,
                             lambda: nc.scalar.activation(e[0:EP, 0:g.T], e[0:EP, 0:g.T], ACT.Exp), den)
        scale_rows(nc, k, "g0_scale", X, den[:], R)
        with nc.Block() as block:
            @block.sync
            def _(sp):
                sp.dma_start(g.blocks(xs_tab), R[:]).then_inc(xs_st, 16)
                sp.wait_ge(xs_st, 16)

        def weigh(dest, rows, t0):
            return nc.vector.tensor_tensor(dest, rows, e[0:EP, bass.ds(t0, G)].unsqueeze(2).to_broadcast([EP, G, C]),
                                           ALU.mult)

        general_sums(nc, k, g, xs_tab, g.src, g.dst, weigh, S, R)


def general_layer1(nc, k, src, dst, X, S, R, den4):
    with Stage(nc) as ctx:
        k.S_zero = S
        g = General(nc, k, ctx, "g1", src, dst)
        h_tab, st_tab, r_tab = g.table(nc, "h_tab", C), g.table(nc, "st_tab", 2 * HEADS), g.table(nc, "r_tab", C)
        s1 = ctx.enter_context(nc.sbuf_tensor("g1_s1", [P, g.T, HEADS], F32))
        den = ctx.enter_context(nc.sbuf_tensor("g1_den", [P, HEADS * k.NI], F32))
        top = ctx.enter_context(nc.sbuf_tensor("g1_top", [P, 2], F32))
        mx, rl = ctx.semaphore("g1_max"), ctx.semaphore("g1_residual")
        HW = C + 2 * HEADS
        general_project(nc, k, g, "h", X, k.w1_all[:], [(h_tab, 0, C), (st_tab, C, HW), (r_tab, HW, HW + C)])

        def combine(link, h, t0):
            w = g.wk[0:EP, :, 0:HEADS]
            link(nc.vector.tensor_tensor(w, g.ga[0:EP, h, :, 0:HEADS], g.gb[0:EP, h, :, HEADS:2 * HEADS], ALU.add))
            return nc.vector.scalar_tensor_tensor(out=s1[0:EP, bass.ds(t0, G), :], in0=w, scalar=ALPHA, in1=w,
                                                  op0=ALU.mult, op1=ALU.max)

        general_scores(nc, k, g, st_tab, st_tab, 2 * HEADS, combine, 1)
        flat = s1[0:EP].rearrange("p t h -> p (t h)")
        with nc.Block() as block:
            @block.vector
            def _(dve):
                nc.vector.tensor_reduce(top[0:EP, 0:1], flat, AX.X, ALU.max).then_inc(mx, 1)
                dve.wait_ge(mx, 2)
                nc.vector.tensor_scalar(top[0:EP, 1:2], top[0:EP, 1:2], -1.0, None, ALU.mult)

            @block.gpsimd
            def _(pool):
                pool.wait_ge(mx, 1)
                nc.gpsimd.partition_all_reduce(top[0:EP, 1:2], top[0:EP, 0:1], EP, RMAX).then_inc(mx, 1)
        general_denominators(nc, k, g, lambda q, t0, n: s1[0:EP, bass.ds(t0, n), q], HEADS,
                             lambda: nc.scalar.activation(flat, flat, ACT.Exp, bias=top[0:EP, 1:2]), den)

        def weigh(dest, rows, t0):
            w = s1[0:EP, bass.ds(t0, G), :].rearrange("p g h -> p (g h)").unsqueeze(2).to_broadcast([EP, G * HEADS, D])
            return nc.vector.tensor_tensor(dest.rearrange("p g (h d) -> p (g h) d", h=HEADS),
                                           rows.rearrange("p g (h d) -> p (g h) d", h=HEADS), w, ALU.mult)

        general_sums(nc, k, g, h_tab, g.dst, g.src, weigh, S, R)
        with nc.Block() as block:
            @block.sync
            def _(sp):
                sp.dma_start(R[:], g.blocks(r_tab)).then_inc(rl, 16)
                sp.wait_ge(rl, 16)

            @block.vector
            def _(dve):
                nc.vector.tensor_copy(den4[:], den[:].rearrange("p (e b) -> p b e", e=HEADS))


def either(nc, label, value, expected, first, second):
    nc.br_eq(value, expected, on_true=f"{label}_first", on_false=f"{label}_second", engines=ENGINES)
    for arm, steps in (("first", first), ("second", second)):
        with nc.body(f"{label}_{arm}", valid_engines=ENGINES):
            steps()
            nc.br(f"{label}_end", engines=ENGINES)
    nc.switch_bb(f"{label}_end")


def all_binned(nc, k, flag, edges):
    with Stage(nc) as ctx:
        has = ctx.enter_context(nc.sbuf_tensor("has_edge", [P, k.NI, k.NI], BF16))
        count = ctx.enter_context(nc.sbuf_tensor("lane_count", [P, 1], F32))
        psum = ctx.enter_context(nc.psum_tensor("lane_psum", [P, 512], F32))
        chain, counted, summed = (ctx.semaphore("lane_" + n) for n in ("chain", "counted", "summed"))
        with nc.Block() as block:
            @block.vector
            def _(dve):
                nc.vector.tensor_scalar(has[:], k.SLs[:, 0:k.NI], 0.0, None, ALU.is_ge).then_inc(chain, 1)
                dve.wait_ge(chain, 1)
                nc.vector.tensor_reduce(count[:], has[:].rearrange("p a b -> p (a b)"), AX.X, ALU.add).then_inc(counted, 1)
                dve.wait_ge(summed, 1)
                nc.vector.tensor_scalar(flag[:], psum[:, 0:1], float(edges), None, ALU.is_equal)

            @block.tensor
            def _(pe):
                pe.wait_ge(counted, 1)
                nc.tensor.matmul(psum[:, 0:1], k.ones[:], count[:], start=True, stop=True).then_inc(summed, 1)


class Shared:
    pass


def load_constants(nc, k, sb, X, x, w0, a0, w1, a_left, a_right, w_res):
    N = x.shape[0]
    NFULL, NREST = N // P, N % P
    iota_i, part_i, part = sb("iota_i", [P, P], I32), sb("part_i", [P, 1], I32), k.part
    w1_sb, wres_sb, w1_t = sb("w1_sb", [P, C]), sb("wres_sb", [P, C]), sb("w1_t", [P, C])
    a_diag, a_rows, w0_a, w0_dot = sb("a_diag", [P, P]), sb("a_rows", [P, C]), sb("w0_a", [P, 2, C]), sb("w0_dot", [P, 2])
    al_col, al_blk = sb("al_col", [P, 2]), sb("al_blk", [P, 2 * HEADS])
    hm_i, hm_f, headmask = sb("hm_i", [P, 1], I32), sb("hm_f", [P, 1]), sb("headmask", [P, HEADS])
    with Stage(nc) as ctx:
        psum = ctx.enter_context(nc.psum_tensor("const_psum", [P, 512], F32))
        ld, zeroed, io, cst, wt_ready, wt_sb, wa_ready = (ctx.semaphore("const_" + n) for n in (
            "loaded", "zeroed", "iota", "chain", "w_turned", "w_turned_in_sbuf", "w_attention"))
        with nc.Block() as block:
            @block.sync
            def _(sp):
                sp.dma_start(k.w0, w0.rearrange("(t c) o -> c t o", t=2)).then_inc(ld, 16)
                sp.dma_start(w1_sb[:], w1).then_inc(ld, 16)
                sp.dma_start(wres_sb[:], w_res).then_inc(ld, 16)
                sp.dma_start(k.a_col[:], a0).then_inc(ld, 16)
                sp.dma_start(al_col[:, 0:1], a_left.rearrange("h d o -> (h d) o")).then_inc(ld, 16)
                sp.dma_start(al_col[:, 1:2], a_right.rearrange("h d o -> (h d) o")).then_inc(ld, 16)
                sp.dma_start(X[:, 0:NFULL, :], x[0:NFULL * P].rearrange("(b p) c -> p b c", p=P)).then_inc(ld, 16)
                sp.wait_ge(zeroed, 1)
                sp.dma_start(X[0:NREST, NFULL, :], x[NFULL * P:N]).then_inc(ld, 16)
                sp.wait_ge(ld, 128)

            @block.gpsimd
            def _(pool):
                nc.gpsimd.iota(iota_i[:], [[1, P]], base=0, channel_multiplier=0).then_inc(io, 1)
                nc.gpsimd.iota(part_i[:], [[1, 1]], base=0, channel_multiplier=1).then_inc(io, 1)

            @block.vector
            def _(dve):
                ch = Chain(dve, cst)
                nc.vector.memset(X[:, NFULL:k.NI, :], 0.0).then_inc(zeroed, 1)
                nc.vector.memset(k.ones[:], 1.0)
                dve.wait_ge(io, 2)
                nc.vector.tensor_copy(k.iota[:], iota_i[:])
                nc.vector.tensor_copy(k.iota_x[:], iota_i[:].unsqueeze(2).to_broadcast([P, P, GT]))
                ch.link(nc.vector.tensor_copy(part[:], part_i[:]))
                nc.vector.tensor_scalar(k.ident[:], k.iota[:], part[:, 0:1], None, ALU.is_equal)
                nc.vector.tensor_scalar(k.ident_b[:], k.iota[:], part[:, 0:1], None, ALU.is_equal)
                nc.vector.tensor_scalar(k.above_b[:], k.iota[:], part[:, 0:1], None, ALU.is_gt)
                nc.vector.tensor_scalar(k.thr[:], k.iota[:, 0:k.NW], float(P), None, ALU.mult)
                ch.link(nc.vector.tensor_scalar(hm_i[:], part_i[:], D.bit_length() - 1, None, ALU.logical_shift_right))
                ch.link(nc.vector.tensor_copy(hm_f[:], hm_i[:]))
                ch.link(nc.vector.tensor_scalar(headmask[:], k.iota[:, 0:HEADS], hm_f[:, 0:1], None, ALU.is_equal))
                dve.wait_ge(ld, 128)
                nc.vector.tensor_scalar(al_blk[:, 0:HEADS], headmask[:], al_col[:, 0:1], None, ALU.mult)
                nc.vector.tensor_scalar(al_blk[:, HEADS:], headmask[:], al_col[:, 1:2], None, ALU.mult)
                nc.vector.tensor_scalar(a_diag[:], k.ident[:], k.a_col[:], None, ALU.mult)
                nc.vector.memset(k.a_pos[:, C:C + 1], 1.0)
                nc.vector.memset(k.a_pos[:, C + 1:CZ], -1.0)
                nc.vector.tensor_copy(k.w1_all[:, 0:C], w1_sb[:])
                ch.link(nc.vector.tensor_copy(k.w1_all[:, C + 2 * HEADS:], wres_sb[:]))
                dve.wait_ge(wt_ready, 1)
                ch.link(nc.vector.tensor_copy(a_rows[:], psum[:, 2 * C:3 * C]))
                nc.vector.tensor_copy(w1_t[:], psum[:, 0:C]).then_inc(wt_sb, 1)
                nc.vector.tensor_scalar(k.a_pos[:, 0:C], a_rows[:], 1.0 - ALPHA, None, ALU.mult)
                ch.link(nc.vector.tensor_tensor(w0_a[:], k.w0, a_rows[:].unsqueeze(1).to_broadcast([P, 2, C]), ALU.mult))
                ch.link(nc.vector.tensor_reduce(w0_dot[:], w0_a[:], AX.X, ALU.add))
                nc.vector.tensor_scalar(k.w0_ext[:, :, C:C + 1], w0_dot[:].unsqueeze(2), ALPHA, None, ALU.mult)
                nc.vector.tensor_scalar(k.w0_ext[:, :, C + 1:CZ], w0_dot[:].unsqueeze(2), -ALPHA, None, ALU.mult)
                dve.wait_ge(wa_ready, 1)
                nc.vector.tensor_copy(k.w1_all[:, C:C + 2 * HEADS], psum[:, 0:2 * HEADS])

            @block.tensor
            def _(pe):
                pe.wait_ge(cst, 5)
                nc.tensor.matmul(psum[:, 2 * C:3 * C], k.ones[:], a_diag[:], start=True, stop=True)
                nc.tensor.transpose(psum[:, 0:C], w1_sb[:], k.ident[:]).then_inc(wt_ready, 1)
                pe.wait_ge(wt_sb, 1)
                nc.tensor.matmul(psum[:, 0:2 * HEADS], w1_t[:], al_blk[:], start=True, stop=True).then_inc(wa_ready, 1)


def scale_rows(nc, k, tag, X, den, xs):
    NB = k.NI
    with Stage(nc) as ctx:
        scc = ctx.semaphore(f"{tag}_chain")
        rden = ctx.enter_context(nc.sbuf_tensor(f"{tag}_rden", [P, NB], F32))
        with nc.Block() as block:
            @block.vector
            def _(dve):
                ch = Chain(dve, scc)
                ch.link(nc.vector.tensor_scalar(den, den, 1.1754944e-38, None, ALU.max))
                ch.link(nc.vector.reciprocal(rden[:], den))
                nc.vector.tensor_tensor(xs[:], X[:], rden[:].unsqueeze(2).to_broadcast([P, NB, C]), ALU.mult)


def add_and_norm(nc, k, tag, X, S, R, before, out):
    NB = k.NI
    with Stage(nc) as ctx:
        stat = ctx.enter_context(nc.sbuf_tensor(f"{tag}_stat", [P, NB], F32))
        ask = ctx.enter_context(nc.sbuf_tensor(f"{tag}_ask", [P, 1], F32))
        chain, a_req, a_done, fin, st = (ctx.semaphore(f"{tag}_{n}") for n in (
            "chain", "act_asked", "act_done", "finished", "stored"))
        asked = []
        with nc.Block() as block:
            @block.vector
            def _(dve):
                ch = Chain(dve, chain)

                def on_act(emit):
                    asked.append(emit)
                    dve.sem_inc(a_req, 1)
                    dve.wait_ge(a_done, len(asked))

                before(ch.link, on_act)
                ch.link(nc.vector.tensor_tensor(X[:], X[:], S[:], ALU.add))
                ch.link(nc.vector.tensor_reduce(stat[:], X[:], AX.X, ALU.add))
                ch.link(nc.vector.tensor_scalar(stat[:], stat[:], 1.0 / C, None, ALU.mult))
                ch.link(nc.vector.tensor_tensor(X[:], X[:], stat[:].unsqueeze(2).to_broadcast([P, NB, C]), ALU.subtract))
                ch.link(nc.vector.tensor_tensor(S[:], X[:], X[:], ALU.mult))
                ch.link(nc.vector.tensor_reduce(stat[:], S[:], AX.X, ALU.add))
                ch.link(nc.vector.tensor_scalar(stat[:], stat[:], 1.0 / C, LN_EPS, ALU.mult, ALU.add))
                on_act(lambda: nc.scalar.activation(stat[:], stat[:], ACT.Sqrt))
                ch.link(nc.vector.reciprocal(stat[:], stat[:]))
                nc.vector.tensor_tensor(X[:], X[:], stat[:].unsqueeze(2).to_broadcast([P, NB, C]), ALU.mult
                                        ).then_inc(fin, 1)

            @block.scalar
            def _(act):
                for n, emit in enumerate(asked):
                    act.wait_ge(a_req, n + 1)
                    emit().then_inc(a_done, 1)

            @block.sync
            def _(sp):
                if out is not None:
                    N = out.shape[0]
                    NFULL, NREST = N // P, N % P
                    sp.wait_ge(fin, 1)
                    sp.dma_start(out[0:NFULL * P].rearrange("(b p) c -> p b c", p=P), X[:, 0:NFULL, :]).then_inc(st, 16)
                    sp.dma_start(out[NFULL * P:N], X[0:NREST, NFULL, :]).then_inc(st, 16)
                    sp.wait_ge(st, 32)


def gnn_program(nc, x, src, dst, w0, a0, w1, a_left, a_right, w_res, out):
    N, E = x.shape[0], src.shape[0]
    k = Shared()
    k.NI = 2 * (-(-N // (2 * P)))
    k.NW = k.NI + 1
    assert (k.NI - 1) * P >= N and E % (EP * STEP) == 0
    with Stage(nc) as ctx:
        def sb(name, shape, dt=F32):
            return ctx.enter_context(nc.sbuf_tensor(name, shape, dt))

        X = sb("X", [P, k.NI, C])
        k.iota = sb("iota", [P, P])
        k.iota_x = sb("iota_x", [P, P, GT], BF16)
        k.ident, k.ident_b, k.above_b = sb("ident", [P, P]), sb("ident_b", [P, P], BF16), sb("above_b", [P, P], BF16)
        k.part = sb("part", [P, 1])
        k.ones, k.thr = sb("one_mat", [P, P]), sb("thr", [P, k.NW])
        w0x = sb("w0_ext", [P, 2, CZ])
        k.w0_ext, k.w0 = w0x[:], w0x[:, :, 0:C]
        k.a_pos = sb("a_pos", [P, CZ])
        k.w1_all = sb("w1_all", [P, 2 * C + 2 * HEADS])
        k.a_col = sb("a_col", [P, 1])
        k.SLs, k.SLd = sb("SLs", [P, k.NW, k.NI], BF16), sb("SLd", [P, k.NW, k.NI], BF16)
        den = sb("den", [P, k.NI])
        with ExitStack() as scope:
            load_constants(nc, k, lambda n, s, d=F32: scope.enter_context(nc.sbuf_tensor(n, s, d)), X, x, w0, a0, w1,
                           a_left, a_right, w_res)
        e0 = sb("e0", [P, k.NI, k.NI])
        with ExitStack() as scope:
            k.key, k.slo, k.dlo = (scope.enter_context(nc.sbuf_tensor(n, [P, k.NW, W_T], BF16))
                                   for n in ("win_key", "win_slo", "win_dlo"))
            place_windows(nc, k, src, dst)
            pq = scope.enter_context(nc.sbuf_tensor("pq", [P, k.NI, 3, 2 * CZ], BF16))
            project_parts(nc, k, "proj0", X, k.w0_ext.rearrange("c t o -> c (t o)"), 2 * CZ, k.NI, pq, None)
            bin_and_score(nc, k, pq, e0, den)
        flag = sb("flag", [P, 1], I32)
        all_binned(nc, k, flag, E)
        binned = nc.values_load(flag[0:1, 0:1], min_val=0, max_val=1)
        S, R, den4 = sb("S", [P, k.NI, C]), sb("R", [P, k.NI, C]), sb("den4", [P, k.NI, HEADS])

        def binned_layer0():
            scale_rows(nc, k, "scale", X, den[:], R)
            layer0_sums(nc, k, R, e0, S)

        def binned_layer1():
            with ExitStack() as scope:
                hp = scope.enter_context(nc.sbuf_tensor("hp", [P, k.NW, 3, C + 2 * HEADS], BF16))
                s1 = scope.enter_context(nc.sbuf_tensor("s1", [P, k.NI, k.NI, HEADS], F32))
                project_parts(nc, k, "proj1", X, k.w1_all[:], C + 2 * HEADS, k.NI, hp, R)
                layer1_scores(nc, k, hp, s1)
                with nc.sbuf_tensor("penalty", [P, k.NI, k.NI], F32) as pen:
                    layer1_weights(nc, k, s1, pen)
                layer1_sums(nc, k, hp, s1, S, den4)

        either(nc, "layer0", binned, 1, binned_layer0,
               lambda: general_layer0(nc, k, src, dst, X, a0, S, R, e0))
        add_and_norm(nc, k, "norm0", X, S, R, lambda link, on_act: None, None)
        either(nc, "layer1", binned, 1, binned_layer1,
               lambda: general_layer1(nc, k, src, dst, X, S, R, den4))

        def finish(link, on_act):
            link(nc.vector.tensor_scalar(den4[:], den4[:], SM_EPS, None, ALU.add))
            link(nc.vector.reciprocal(den4[:], den4[:]))
            v = S[:].rearrange("p b (e d) -> p (b e) d", e=HEADS)
            link(nc.vector.tensor_tensor(v, v, den4[:].rearrange("p b e -> p (b e)").unsqueeze(2)
                                         .to_broadcast([P, k.NI * HEADS, D]), ALU.mult))
            link(nc.vector.tensor_tensor(S[:], S[:], R[:], ALU.add))
            link(nc.vector.tensor_scalar(R[:], S[:], 0.0, None, ALU.min))
            on_act(lambda: nc.scalar.activation(R[:], R[:], ACT.Exp))
            link(nc.vector.tensor_scalar(R[:], R[:], -1.0, None, ALU.add))
            link(nc.vector.scalar_tensor_tensor(out=S[:], in0=S[:], scalar=0.0, in1=R[:], op0=ALU.max, op1=ALU.add))

        add_and_norm(nc, k, "norm1", X, S, R, finish, out)


_INS = ["x", "src", "dst", "L0_gnn_w", "L0_gnn_a", "L1_gnn_W", "L1_gnn_A_left", "L1_gnn_A_right",
        "L1_gnn_residual_projection"]


def kernel(**inputs):
    import numpy as _np
    import concourse.bacc as _bacc
    from concourse import mybir as _mybir
    from concourse.bass_utils import run_bass_kernel_spmd as _run

    nc = _bacc.Bacc("TRN2", target_bir_lowering=False, num_devices=1)
    arrays, args = {}, []
    for name in _INS:
        a = _np.ascontiguousarray(inputs[name])
        arrays[f"in_{name}_dram"] = a
        args.append(nc.dram_tensor(f"in_{name}_dram", a.shape, _mybir.dt.from_np(a.dtype), kind="ExternalInput").ap())
    n, c = inputs["x"].shape
    args.append(nc.dram_tensor("out_0_dram", (n, c), _mybir.dt.float32, kind="ExternalOutput").ap())
    gnn_program(nc, *args)
    r = _run(nc, [arrays], core_ids=[0])
    return r.results[0]["out_0_dram"]
```

```python
from contextlib import ExitStack

import concourse.bass as bass
from concourse import mybir

F32 = mybir.dt.float32
BF16 = mybir.dt.bfloat16
I32 = mybir.dt.int32
U32 = mybir.dt.uint32
ALU = mybir.AluOpType
ACT = mybir.ActivationFunctionType
AX = mybir.AxisListType
RMAX = bass.bass_isa.ReduceOp.max

P = 128
C = 128
HEADS = 4
D = C // HEADS
ALPHA = 0.2
LN_EPS = 1e-5
SM_EPS = 1e-8
NEVER = -1e30
ENGINES = mybir.ALL_ENGINES
EP = 125



CZ = C + 2
W_T = 36
WIN = P * W_T
GT = 4
STEP = 16


class Stage(ExitStack):

    def __init__(self, nc):
        super().__init__()
        self.nc, self.semaphores = nc, []

    def semaphore(self, name):
        self.semaphores.append(self.nc.alloc_semaphore(name))
        return self.semaphores[-1]

    def __exit__(self, *error):
        closed = super().__exit__(*error)
        if error[0] is None and self.semaphores:
            self.nc.clear_and_free_semaphores(self.semaphores)
            self.nc.all_engine_barrier()
        return closed


def groups_of(n):
    return [(a, min(GT, n - a)) for a in range(0, n, GT)]


class Chain:

    def __init__(self, eng, sem, per=0):
        self.eng, self.sem, self.per, self.n, self.base, self.it = eng, sem, per, 0, 0, None

    def enter(self, it):
        self.base, self.n, self.it = self.n, 0, it

    def leave(self, iters):
        assert self.n == self.per, (self.n, self.per)
        self.n, self.it, self.base = self.base + self.per * iters, None, 0

    def mark(self, ins):
        self.n += 1
        ins.then_inc(self.sem, 1)
        return self.n

    def wait(self, n):
        self.eng.wait_ge(self.sem, n if self.it is None else self.it * self.per + (self.base + n))

    def link(self, ins):
        self.wait(self.mark(ins))


def split3(nc, chain, value, hi, mid, lo, rest):
    chain.link(nc.vector.tensor_copy(hi, value))
    chain.link(nc.vector.tensor_tensor(rest, value, hi, ALU.subtract))
    chain.link(nc.vector.tensor_copy(mid, rest))
    return nc.vector.tensor_tensor(lo, rest, mid, ALU.subtract)


def place_windows(nc, k, src, dst):
    E = dst.shape[0]
    T, NS = E // EP, E // EP // STEP
    NW = k.NW
    with Stage(nc) as ctx:
        def sb(name, shape, dt=F32):
            return ctx.enter_context(nc.sbuf_tensor(name, shape, dt))

        dst_i = sb("win_dst_all", [P, T], I32)
        dst_f = sb("win_dst_sample", [P, NS])
        less = sb("win_less", [P, k.NW, NS], BF16)
        count = sb("win_count", [P, k.NW])
        thr = k.thr
        off_f = sb("win_off_f", [P, NW])
        off_i = sb("win_off_i", [P, NW], I32)
        ws = sb("win_src", [P, NW, W_T], I32)
        wd = sb("win_dst", [P, NW, W_T], I32)
        wi = sb("win_int", [P, NW, W_T], I32)
        f1 = sb("win_f1", [P, NW, W_T])
        f2 = sb("win_f2", [P, NW, W_T])
        f3 = sb("win_f3", [P, NW, W_T])
        psum = ctx.enter_context(nc.psum_tensor("win_psum", [P, NW], F32))
        s = {n: ctx.semaphore("win_" + n) for n in
             ("loaded", "chain", "counted", "summed", "offsets", "src_read", "dst_read", "padded")}
        with nc.Block() as block:
            @block.sync
            def _(sp):
                sp.dma_start(dst_i[0:EP, :], dst.rearrange("(p t) -> p t", p=EP)).then_inc(s["loaded"], 16)
                sp.wait_ge(s["offsets"], 1)
                sp.wait_ge(s["padded"], 1)
                with sp.Fori(0, k.NI) as j:
                    o = sp.value_load(off_i[0:1, bass.ds(j, 1)], min_val=0, max_val=E - WIN)
                    sp.dma_start(ws[:, bass.ds(j, 1), :], src[bass.ds(o, WIN)].rearrange("(p a t) -> p a t", p=P, a=1)
                                 ).then_inc(s["src_read"], 16)
                sp.wait_ge(s["src_read"], 16 * k.NI)

            @block.scalar
            def _(act):
                act.wait_ge(s["offsets"], 1)
                act.wait_ge(s["padded"], 1)
                with act.Fori(0, k.NI) as j:
                    o = act.value_load(off_i[0:1, bass.ds(j, 1)], min_val=0, max_val=E - WIN)
                    act.dma_start(wd[:, bass.ds(j, 1), :], dst[bass.ds(o, WIN)].rearrange("(p a t) -> p a t", p=P, a=1)
                                  ).then_inc(s["dst_read"], 16)
                act.wait_ge(s["dst_read"], 16 * k.NI)

            @block.tensor
            def _(pe):
                pe.wait_ge(s["counted"], 1)
                nc.tensor.matmul(psum[:], k.ones[0:EP, :], count[0:EP, :], start=True, stop=True).then_inc(s["summed"], 1)

            @block.vector
            def _(dve):
                ch = Chain(dve, s["chain"])
                nc.vector.memset(ws[:, k.NI:NW, :], 0)
                nc.vector.memset(wd[:, k.NI:NW, :], 0).then_inc(s["padded"], 1)
                dve.wait_ge(s["loaded"], 16)
                ch.link(nc.vector.tensor_copy(dst_f[0:EP], dst_i[0:EP, 0:T:STEP]))
                ch.link(nc.vector.tensor_tensor(less[0:EP], dst_f[0:EP].unsqueeze(1).to_broadcast([EP, NW, NS]),
                                                thr[0:EP].unsqueeze(2).to_broadcast([EP, NW, NS]), ALU.is_lt))
                nc.vector.tensor_reduce(count[0:EP], less[0:EP], AX.X, ALU.add).then_inc(s["counted"], 1)
                dve.wait_ge(s["summed"], 1)
                ch.link(nc.vector.tensor_scalar(off_f[:], psum[:], float(STEP), -float(STEP), ALU.mult, ALU.add))
                ch.link(nc.vector.tensor_scalar(off_f[:], off_f[:], 0.0, float(E - WIN), ALU.max, ALU.min))
                nc.vector.tensor_copy(off_i[:], off_f[:]).then_inc(s["offsets"], 1)
                dve.wait_ge(s["src_read"], 16 * k.NI)
                dve.wait_ge(s["dst_read"], 16 * k.NI)
                ch.link(nc.vector.tensor_copy(f1[:], wd[:]))
                ch.link(nc.vector.tensor_tensor(f1[:], f1[:], thr[:].unsqueeze(2).to_broadcast([P, NW, W_T]),
                                                ALU.subtract))
                nc.vector.tensor_scalar(k.dlo[:], f1[:], 1.0, None, ALU.add)
                ch.link(nc.vector.tensor_scalar(f2[:], f1[:], 0.0, None, ALU.is_ge))
                ch.link(nc.vector.tensor_scalar(f3[:], f1[:], float(P), None, ALU.is_lt))
                ch.link(nc.vector.tensor_tensor(f2[:], f2[:], f3[:], ALU.mult))
                ch.link(nc.vector.tensor_scalar(f2[:], f2[:], -200.0, 200.0, ALU.mult, ALU.add))
                ch.link(nc.vector.tensor_scalar(wi[:], ws[:], P - 1, None, ALU.bitwise_and))
                ch.link(nc.vector.tensor_copy(f3[:], wi[:]))
                nc.vector.tensor_scalar(k.slo[:], f3[:], 1.0, None, ALU.add)
                ch.link(nc.vector.tensor_scalar(wi[:], ws[:], 7, None, ALU.logical_shift_right))
                ch.link(nc.vector.tensor_copy(f1[:], wi[:]))
                nc.vector.tensor_tensor(k.key[:], f1[:], f2[:], ALU.add)


def project_parts(nc, k, tag, X, weights, cols, NB, parts, plain):
    width = weights.shape[1]
    with Stage(nc) as ctx:
        def sb(name, shape, dt=F32):
            return ctx.enter_context(nc.sbuf_tensor(f"{tag}_{name}", shape, dt))

        def pair(name):
            return [ctx.semaphore(f"{tag}_{name}{h}") for h in range(2)]

        xb, xt, rest = sb("block", [P, 2, C]), sb("turned", [P, 2, C]), sb("rest", [P, 2, cols])
        tps = ctx.enter_context(nc.psum_tensor(f"{tag}_tps", [P, 2, 512], F32))
        prod = ctx.enter_context(nc.psum_tensor(f"{tag}_prod", [P, 2, 512], F32))
        picked, turned, xt_ok, mul, hi_ok, rest_ok, mid_ok, lo_ok = (
            pair(n) for n in ("picked", "turned", "turned_in_sbuf", "product", "hi", "rest", "mid", "lo"))

        def rows(m, h):
            n = m * 2 + h
            return slice(n, n + 1) if isinstance(n, int) else bass.ds(n, 1)

        def block_of(blocks, m, h):
            return blocks[:, rows(m, h), :]

        def part(m, h, q):
            return parts[:, rows(m, h), q, :]

        LAST = NB // 2 - 1

        def pick(dve, m):
            for h in range(2):
                if not (isinstance(m, int) and m == 0):
                    dve.wait_ge(turned[h], m)
                nc.vector.tensor_copy(xb[:, h:h + 1, :], block_of(X, m, h)).then_inc(picked[h], 1)

        def split(dve, m):
            for h in range(2):
                dve.wait_ge(hi_ok[h], m + 1)
                nc.vector.tensor_tensor(rest[:, h:h + 1, :], prod[:, h:h + 1, 0:cols], part(m, h, 0),
                                        ALU.subtract).then_inc(rest_ok[h], 1)
            for h in range(2):
                dve.wait_ge(mid_ok[h], m + 1)
                nc.vector.tensor_tensor(part(m, h, 2), rest[:, h:h + 1, :], part(m, h, 1),
                                        ALU.subtract).then_inc(lo_ok[h], 1)
                dve.wait_ge(lo_ok[h], m + 1)

        def turn(pe, m, h):
            pe.wait_ge(picked[h], m + 1)
            if not (isinstance(m, int) and m == 0):
                pe.wait_ge(xt_ok[h], m)
            nc.tensor.transpose(tps[:, h, 0:C], xb[:, h, :], k.ident[:]).then_inc(turned[h], 1)

        def multiply(pe, m, h):
            pe.wait_ge(xt_ok[h], m + 1)
            pe.wait_ge(rest_ok[h], m + 1)
            nc.tensor.matmul(prod[:, h, 0:width], xt[:, h, :], weights, start=True, stop=True).then_inc(mul[h], 1)

        def take_turned(act, m, h):
            act.wait_ge(turned[h], m + 1)
            nc.scalar.copy(xt[:, h, :], tps[:, h, 0:C]).then_inc(xt_ok[h], 1)

        def take_high(act, m, h):
            if plain is not None:
                nc.scalar.copy(block_of(plain, m, h), prod[:, h:h + 1, cols:width])
            nc.scalar.copy(part(m, h, 0), prod[:, h:h + 1, 0:cols]).then_inc(hi_ok[h], 1)

        def take_middle(act, m, h):
            act.wait_ge(rest_ok[h], m + 2)
            nc.scalar.copy(part(m, h, 1), rest[:, h:h + 1, :]).then_inc(mid_ok[h], 1)

        with nc.Block() as block:
            @block.vector
            def _(dve):
                for h in range(2):
                    dve.sem_inc(rest_ok[h], 1)
                pick(dve, 0)
                with dve.Fori(0, LAST) as m:
                    pick(dve, m + 1)
                    split(dve, m)
                split(dve, LAST)

            @block.tensor
            def _(pe):
                for h in range(2):
                    turn(pe, 0, h)
                with pe.Fori(0, LAST) as m:
                    for h in range(2):
                        multiply(pe, m, h)
                        turn(pe, m + 1, h)
                for h in range(2):
                    multiply(pe, LAST, h)

            @block.scalar
            def _(act):
                for h in range(2):
                    take_turned(act, 0, h)
                with act.Fori(0, LAST) as m:
                    for h in range(2):
                        act.wait_ge(mul[h], m + 1)
                        take_high(act, m, h)
                        take_turned(act, m + 1, h)
                    for h in range(2):
                        take_middle(act, m, h)
                for h in range(2):
                    act.wait_ge(mul[h], LAST + 1)
                    take_high(act, LAST, h)
                for h in range(2):
                    take_middle(act, LAST, h)


def one(ap):
    return ap.squeeze(1)


def bin_and_score(nc, k, pq, e0, den_out):
    NI, NW = k.NI - 1, k.NW
    grp = groups_of(NI)
    NG = len(grp)
    K2 = 2 * NG
    PER = K2 // 2
    L = k.NI // 2
    W2 = W_T + 2
    with Stage(nc) as ctx:
        def sb(name, shape, dt=F32):
            return ctx.enter_context(nc.sbuf_tensor(f"p1_{name}", shape, dt))

        def ps(name, shape, dt=F32):
            return ctx.enter_context(nc.psum_tensor(f"p1_{name}", shape, dt))

        def sem(name):
            return ctx.semaphore(f"p1_{name}")

        def pair(name):
            return [sem(f"{name}{h}") for h in range(2)]

        binrow = sb("binrow", [P, NI, W_T], BF16)
        keep = sb("keep", [P, NI, W2], BF16)
        ohb = sb("ohb", [P, NI, W2], BF16)
        scan = sb("scan", [P, NI, W2], BF16)
        rank = sb("rank", [P, W_T])
        rank_b = sb("rank_b", [P, W_T], BF16)
        lanes = sb("lanes", [P, P, W_T], BF16)
        pay = sb("pay", [P, 2, NI, W_T], BF16)
        picked = pay[:, 0]
        slot = sb("slot", [P, 2, 2, NI], BF16)
        ohs = sb("ohs", [P, 2, NG, P, GT], BF16)
        ohd = sb("ohd", [P, 2, P, GT], BF16)
        oht = sb("oht", [P, 2, 2, GT, P], BF16)
        qst = sb("qst", [P, 2, 3, CZ], BF16)
        rz = sb("rz", [P, 2, GT, CZ])
        score = sb("score", [P, 2, NI])
        rest = sb("rest", [P, NI])
        ep = sb("ep", [P, 2, NI, 3], BF16)
        zeros = keep[:, :, 0:1].to_broadcast([P, NI, 3])

        tp = ps("tp", [P, 2, 2, GT * P], BF16)
        z = ps("z", [P, 2, 2, 512])
        base_slots = ps("base_slots", [P, 512])
        base, slots = base_slots[:, 0:NI], base_slots[:, 256:256 + 2 * NI]
        dps = ps("dps", [P, 512])

        gen, tr, ev, zz, rl, dt = (pair(n) for n in ("onehot", "turned", "turned_in_sbuf", "z", "relu", "scored"))
        qs, ex, pt, dn = (pair(n) for n in ("q_block", "exp", "exp_parts", "den"))
        b_oh, b_base, b_scan, b_pick, b_rank, b_lane, b_pay, b_slot = (sem(n) for n in (
            "bin_onehot", "bin_base", "bin_scan", "bin_picked", "bin_rank", "bin_lanes", "bin_payload", "bin_slots"))
        b_init, opened, closed, chain = sem("const"), sem("opened"), sem("closed"), sem("chain")

        def bins_of(banks, w):
            pairs = banks[:, :, 0:2 * CZ].rearrange("p b (i c) -> p b i c", c=CZ)
            return pairs if w == GT else pairs[:, 0, 0:w]

        def key_at(arr, n):
            return one(arr[:, bass.ds(n, 1), :]) if not isinstance(n, int) else arr[:, n, :]

        oh_part = ohb[:, :, 2:W2]

        LANE_PIECES = (4, 5, 7, 8)

        def dve_bin(ch, dve, piece, n, m, h):
            first = isinstance(m, int) and m == 0
            if piece == 0:
                if not first:
                    dve.wait_ge(b_base, m)
                    dve.wait_ge(b_slot, m)
                nc.vector.tensor_tensor(oh_part, binrow[:], key_at(k.key, n).unsqueeze(1).to_broadcast([P, NI, W_T]),
                                        ALU.is_equal).then_inc(b_oh, 1)
            if piece == 1:
                dve.wait_ge(b_base, m + 1)
                ch.link(nc.vector.tensor_scalar(ohb[:, :, 1], base, 200.0, None, ALU.min))
                nc.vector.tensor_tensor_scan(scan[:].rearrange("p b t -> p (b t)"), keep[:].rearrange("p b t -> p (b t)"),
                                             ohb[:].rearrange("p b t -> p (b t)"), 0.0, ALU.mult, ALU.add
                                             ).then_inc(b_scan, 1)
            if piece == 3:
                dve.wait_ge(b_pick, m + 1)
                nc.vector.tensor_reduce(rank[:], picked.rearrange("p b t -> p t b"), AX.X, ALU.add).then_inc(b_rank, 1)
                dve.wait_ge(b_rank, m + 1)
                ch.link(nc.vector.tensor_scalar(rank_b[:], rank[:], -1.0, None, ALU.add))
            if piece in LANE_PIECES:
                part = LANE_PIECES.index(piece)
                a, b = part * P // 4, (part + 1) * P // 4
                by4 = [P, b - a, W_T // GT, GT]
                ins = nc.vector.tensor_tensor(
                    lanes[:, a:b, :].rearrange("p n (u v) -> p n u v", v=GT), k.iota_x[:, a:b, :].unsqueeze(2).to_broadcast(by4),
                    rank_b[:].rearrange("p (u v) -> p u v", v=GT).unsqueeze(1).to_broadcast(by4), ALU.is_equal)
                if part == 3:
                    ins.then_inc(b_lane, 1)
            if piece == 6:
                dve.wait_ge(b_slot, m + 1)
                ch.link(nc.vector.tensor_scalar(slot[:, h].rearrange("p a b -> p (a b)"), slots, -1.0, None, ALU.add))
                for a, arr in ((0, k.SLs), (1, k.SLd)):
                    out = arr[:, slice(n, n + 1) if first else bass.ds(n, 1), 0:NI]
                    ins = nc.vector.tensor_copy(out, slot[:, h, a].unsqueeze(1))
                ch.link(ins)

        def pe_base(pe, m):
            pe.wait_ge(b_oh, m + 1)
            for t in range(W_T):
                ins = nc.tensor.matmul(base, k.above_b[:], ohb[:, :, 2 + t], start=(t == 0), stop=(t == W_T - 1))
            ins.then_inc(b_base, 1)

        def pe_slots(pe, m):
            pe.wait_ge(b_lane, m + 1)
            pe.wait_ge(b_pay, m + 1)
            for t in range(W_T):
                ins = nc.tensor.matmul(slots.rearrange("p (a b) -> p a b", a=2), lanes[:, :, t], pay[:, :, :, t],
                                       start=(t == 0), stop=(t == W_T - 1))
            ins.then_inc(b_slot, 1)

        def pool_bin(pool, n, m):
            if not isinstance(n, int):
                pool.wait_ge(b_slot, m)
            pool.wait_ge(b_scan, m + 1)
            nc.gpsimd.tensor_tensor(picked, oh_part, scan[:, :, 2:W2], ALU.mult).then_inc(b_pick, 1)
            pool.wait_ge(b_rank, m + 1)
            for q, arr in enumerate((k.slo, k.dlo)):
                ins = nc.gpsimd.tensor_tensor(pay[:, q], oh_part, key_at(arr, n).unsqueeze(1).to_broadcast([P, NI, W_T]),
                                              ALU.mult)
            ins.then_inc(b_pay, 1)

        PIECES = {2: 3, 3: 4, 4: 5, 5: 7, 6: 8, 9: 6, 10: 0, 12: 1}
        CH = 2 * (1 + 1 + 2) + 2 * 3

        def of(it, r):
            h, g = divmod(r % K2, NG)
            return h, g, *grp[g], r % 2, it * PER + (r // 2 + 1)

        def make(dve, it, r):
            h, g, i0, w, gp, c = of(it, r)
            if g == 0:
                dve.wait_ge(dn[h], it + (r // K2 + 1))
            dve.wait_ge(tr[gp], c)
            nc.vector.tensor_tensor(ohs[:, h, g, :, 0:w], k.iota_x[:, :, 0:w],
                                    slot[:, h, 0, i0:i0 + w].unsqueeze(1).to_broadcast([P, P, w]), ALU.is_equal)
            nc.vector.tensor_tensor(ohd[:, gp, :, 0:w], k.iota_x[:, :, 0:w],
                                    slot[:, h, 1, i0:i0 + w].unsqueeze(1).to_broadcast([P, P, w]),
                                    ALU.is_equal).then_inc(gen[gp], 1)

        def turn(pe, it, r):
            h, g, i0, w, gp, c = of(it, r)
            pe.wait_ge(gen[gp], c + 1)
            pe.wait_ge(ev[gp], c)
            for q in range(w):
                nc.tensor.transpose(tp[:, gp, 0, q * P:(q + 1) * P], ohs[:, h, g, :, q], k.ident_b[:])
                ins = nc.tensor.transpose(tp[:, gp, 1, q * P:(q + 1) * P], ohd[:, gp, :, q], k.ident_b[:])
            ins.then_inc(tr[gp], 1)

        def take_turned(act, it, r):
            h, g, i0, w, gp, c = of(it, r)
            if g == 0:
                act.wait_ge(dn[h], it + (r // K2 + 1))
                n = (it * 2 + 2) % k.NI if r == K2 else it * 2 + h
                row = slice(n, n + 1) if isinstance(n, int) else bass.ds(n, 1)
                nc.scalar.copy(qst[:, h], one(pq[:, row, :, CZ:2 * CZ])).then_inc(qs[h], 1)
            act.wait_ge(tr[gp], c + 1)
            act.wait_ge(zz[gp], c)
            nc.scalar.copy(oht[:, gp, :, 0:w, :].rearrange("p a w n -> p a (w n)"), tp[:, gp, :, 0:w * P]
                           ).then_inc(ev[gp], 1)

        def gather(pe, it, r):
            h, g, i0, w, gp, c = of(it, r)
            pe.wait_ge(ev[gp], c + 1)
            pe.wait_ge(rl[gp], c)
            if g == 0:
                pe.wait_ge(qs[h], it + (r // K2 + 2))
            for i in range(w):
                at = z[:, gp, i // 2, i % 2 * CZ:(i % 2 + 1) * CZ]
                for q in range(3):
                    nc.tensor.matmul(at, oht[:, gp, 1, i, :], qst[:, h, q, :], start=(q == 0), stop=False)
                for q in range(3):
                    ins = nc.tensor.matmul(at, oht[:, gp, 0, i, :], pq[:, i0 + i, q, 0:CZ], start=False, stop=(q == 2))
            ins.then_inc(zz[gp], 1)

        def take_relu(act, it, r):
            h, g, i0, w, gp, c = of(it, r)
            act.wait_ge(zz[gp], c + 1)
            act.wait_ge(dt[gp], c)
            out = rz[:, gp].rearrange("p (b i) c -> p b i c", b=2) if w == GT else rz[:, gp, 0:w]
            nc.scalar.activation(out, bins_of(z[:, gp], w), ACT.Relu).then_inc(rl[gp], 1)

        def weigh(dve, it, r):
            h, g, i0, w, gp, c = of(it, r)
            if g == 0:
                dve.wait_ge(ex[h], it + 1)
            dve.wait_ge(rl[gp], c + 1)
            for i in range(w):
                ins = nc.vector.tensor_tensor_reduce(
                    out=rz[:, gp, i, :], in0=rz[:, gp, i, :], in1=k.a_pos[:], scale=1.0, scalar=0.0,
                    op0=ALU.mult, op1=ALU.add, accum_out=score[:, h, i0 + i:i0 + i + 1])
            ins.then_inc(dt[gp], 1)

        def take_exp(act, it, h):
            r = (h + 1) * NG - 1
            act.wait_ge(dt[r % 2], it * PER + (r // 2 + 2))
            nc.scalar.activation(one(e0[:, bass.ds(it * 2 + h, 1), 0:NI]), score[:, h, :], ACT.Exp).then_inc(ex[h], 1)

        def split_exp(dve, ch, it, h):
            dve.wait_ge(ex[h], it + 2)
            dve.wait_ge(dn[h], it + 1)
            split3(nc, ch, one(e0[:, bass.ds(it * 2 + h, 1), 0:NI]), ep[:, h, :, 0], ep[:, h, :, 1],
                   ep[:, h, :, 2], rest[:]).then_inc(pt[h], 1)

        def sum_exp(pe, it, h):
            pe.wait_ge(pt[h], it + 1)
            for i in range(NI):
                ins = nc.tensor.matmul(dps[:, 3 * i:3 * i + 3], ohs[:, h, i // GT, :, i % GT], ep[:, h, i, :],
                                       start=False, stop=False, skip_group_check=True)
            ins.then_inc(dn[h], 1)

        with nc.Block() as block:
            @block.vector
            def _(dve):
                ch = Chain(dve, chain, CH)
                nc.vector.tensor_copy(binrow[:], k.iota[:, 0:NI].unsqueeze(2).to_broadcast([P, NI, W_T]))
                ch.link(nc.vector.memset(keep[:], 1.0))
                nc.vector.memset(keep[:, :, 0:1], 0.0)
                nc.vector.memset(ohb[:, :, 0:2], 0.0)
                nc.vector.memset(k.SLs[:], -1.0)
                nc.vector.memset(k.SLd[:], -1.0)
                nc.vector.memset(e0[:], 0.0)
                nc.vector.memset(den_out[:, NI:], 1.0).then_inc(b_init, 1)
                dve.wait_ge(b_init, 1)
                for piece in (0, 1, 3, 4, 5, 7, 8, 6):
                    dve_bin(ch, dve, piece, 0, 0, 0)
                for piece in (0, 1):
                    dve_bin(ch, dve, piece, 1, 1, 1)
                for h in range(2):
                    dve.sem_inc(gen[h], 1)
                    dve.sem_inc(dt[h], 1)
                for r in range(3):
                    make(dve, 0, r)
                with dve.Fori(0, L) as it:
                    ch.enter(it)
                    for s in range(K2):
                        h, g = divmod(s, NG)
                        make(dve, it, s + 3)
                        if g in PIECES:
                            m = it * 2 + (h + 1 + (PIECES[g] < 2))
                            n = m % k.NW if h == 1 and PIECES[g] < 2 else m
                            dve_bin(ch, dve, PIECES[g], n, m, 1 - h)
                        weigh(dve, it, s)
                        if s == NG + 2:
                            split_exp(dve, ch, it, 0)
                        if s == K2 - 1:
                            split_exp(dve, ch, it, 1)
                    ch.leave(L)
                dve.wait_ge(closed, 1)
                nc.vector.tensor_reduce(den_out[:, 0:NI], dps[:, 0:3 * NI].rearrange("p (i q) -> p i q", q=3), AX.X, ALU.add)

            @block.tensor
            def _(pe):
                pe.wait_ge(b_init, 1)
                nc.tensor.matmul(dps[:, 0:3 * NI].rearrange("p (i q) -> p i q", q=3), k.ident_b[:], zeros, start=True, stop=False).then_inc(opened, 1)
                pe_base(pe, 0)
                pe_slots(pe, 0)
                pe_base(pe, 1)
                for h in range(2):
                    pe.sem_inc(tr[h], 1)
                    pe.sem_inc(dn[h], 1)
                    pe.sem_inc(zz[h], 1)
                turn(pe, 0, 0)
                turn(pe, 0, 1)
                gather(pe, 0, 0)
                turn(pe, 0, 2)
                gather(pe, 0, 1)
                with pe.Fori(0, L) as it:
                    for s in range(K2):
                        h, g = divmod(s, NG)
                        turn(pe, it, s + 3)
                        gather(pe, it, s + 2)
                        if g == 10:
                            pe_base(pe, it * 2 + (h + 2))
                        if g == 7:
                            pe_slots(pe, it * 2 + (h + 1))
                        if s == NG + 3:
                            sum_exp(pe, it, 0)
                        if s == K2 - 1:
                            sum_exp(pe, it, 1)
                nc.tensor.matmul(dps[:, 0:3 * NI].rearrange("p (i q) -> p i q", q=3), k.ident_b[:], zeros, start=False, stop=True).then_inc(closed, 1)

            @block.scalar
            def _(act):
                for h in range(2):
                    act.sem_inc(ev[h], 1)
                    act.sem_inc(rl[h], 1)
                    act.sem_inc(ex[h], 1)
                    act.sem_inc(qs[h], 1)
                take_turned(act, 0, 0)
                take_turned(act, 0, 1)
                take_relu(act, 0, 0)
                take_turned(act, 0, 2)
                take_relu(act, 0, 1)
                with act.Fori(0, L) as it:
                    for s in range(K2):
                        take_turned(act, it, s + 3)
                        take_relu(act, it, s + 2)
                        if s == NG:
                            take_exp(act, it, 0)
                        if s == K2 - 1:
                            take_exp(act, it, 1)

            @block.gpsimd
            def _(pool):
                pool_bin(pool, 0, 0)
                with pool.Fori(0, L) as it:
                    for h in range(2):
                        pool_bin(pool, it * 2 + (h + 1), it * 2 + (h + 1))


STAGE = {0: 0, 8: 1}


def layer0_sums(nc, k, xs, e0, S):
    NI = k.NI - 1
    grp = groups_of(NI)
    NG = len(grp)
    K2, PER, L = 2 * NG, NG, k.NI // 2
    with Stage(nc) as ctx:
        def sb(name, shape, dt=F32):
            return ctx.enter_context(nc.sbuf_tensor(f"p2_{name}", shape, dt))

        def ps(name, shape, dt=F32):
            return ctx.enter_context(nc.psum_tensor(f"p2_{name}", shape, dt))

        def pair(name):
            return [ctx.semaphore(f"p2_{name}{h}") for h in range(2)]

        win = sb("window", [P, 2, 3, NI])
        ohs = sb("ohs", [P, 2, GT, P])
        ohd = sb("ohd", [P, 2, GT, P])
        wsb = sb("wsb", [P, 2, GT, P])
        wps = ps("wps", [P, 2, GT * P])
        acc = ps("acc", [P, 2, 512])
        staged, gen, wm, wc, used, kept = (pair(n) for n in (
            "staged", "onehot", "weights", "weights_in_sbuf", "weights_used", "kept"))
        with nc.Block() as block:
            @block.vector
            def _(dve):
                for h in range(2):
                    dve.sem_inc(gen[h], 1)
                with dve.Fori(0, L) as it:
                    for s in range(K2):
                        if s < K2:
                            h, g = divmod(s, NG)
                            i0, w = grp[g]
                            gp, c = s % 2, it * PER + (s // 2 + 1)
                            if g == 0:
                                dve.wait_ge(staged[h], it + 1)
                            dve.wait_ge(wm[gp], c)
                            nc.vector.tensor_tensor(ohs[:, gp, 0:w, :], k.iota[:].unsqueeze(1).to_broadcast([P, w, P]),
                                                    win[:, h, 0, i0:i0 + w].unsqueeze(2).to_broadcast([P, w, P]),
                                                    ALU.is_equal)
                            for i in range(w):
                                ins = nc.vector.tensor_scalar(ohd[:, gp, i, :], k.iota[:], win[:, h, 1, i0 + i:i0 + i + 1],
                                                              win[:, h, 2, i0 + i:i0 + i + 1], ALU.is_equal, ALU.mult)
                            ins.then_inc(gen[gp], 1)

            @block.tensor
            def _(pe):
                for h in range(2):
                    pe.sem_inc(wm[h], 1)
                    pe.sem_inc(used[h], 1)
                with pe.Fori(0, L) as it:
                    for s in range(K2 + 1):
                        if s < K2:
                            w = grp[s % NG][1]
                            gp, c = s % 2, it * PER + (s // 2 + 1)
                            pe.wait_ge(gen[gp], c + 1)
                            pe.wait_ge(wc[gp], c)
                            for i in range(w):
                                ins = nc.tensor.matmul(wps[:, gp, i * P:(i + 1) * P], ohs[:, gp, i, :], ohd[:, gp, i, :],
                                                       start=True, stop=True)
                            ins.then_inc(wm[gp], 1)
                        if s >= 1:
                            r = s - 1
                            h, g = divmod(r, NG)
                            i0, w = grp[g]
                            gp, c = r % 2, it * PER + (r // 2 + 1)
                            pe.wait_ge(wc[gp], c + 1)
                            if g == 0:
                                pe.wait_ge(kept[h], it + 1)
                            for i in range(w):
                                ins = nc.tensor.matmul(acc[:, h, 0:C], wsb[:, gp, i, :], xs[:, i0 + i, :],
                                                       start=(i0 + i == 0), stop=(i0 + i == NI - 1))
                            ins.then_inc(used[gp], 1)

            @block.scalar
            def _(act):
                def stage(n, v):
                    row = slice(n, n + 1) if isinstance(n, int) else bass.ds(n, 1)
                    nc.scalar.copy(win[:, v, 0, :], one(k.SLs[:, row, 0:NI]))
                    nc.scalar.copy(win[:, v, 1, :], one(k.SLd[:, row, 0:NI]))
                    nc.scalar.copy(win[:, v, 2, :], one(e0[:, row, 0:NI])).then_inc(staged[v], 1)

                for h in range(2):
                    act.sem_inc(wc[h], 1)
                    act.sem_inc(kept[h], 1)
                stage(0, 0)
                with act.Fori(0, L) as it:
                    for q in range(2):
                        act.wait_ge(gen[q], it * PER + 1)
                    stage(it * 2 + 1, 1)
                    for s in range(K2 + 1):
                        if s < K2:
                            w = grp[s % NG][1] * P
                            gp, c = s % 2, it * PER + (s // 2 + 1)
                            act.wait_ge(wm[gp], c + 1)
                            act.wait_ge(used[gp], c)
                            nc.scalar.copy(wsb[:, gp].rearrange("p a b -> p (a b)")[:, 0:w], wps[:, gp, 0:w]
                                           ).then_inc(wc[gp], 1)
                        if s == NG + 1:
                            for r in (NG - 2, NG - 1):
                                act.wait_ge(gen[r % 2], it * PER + (r // 2 + 2))
                            stage((it * 2 + 2) % k.NI, 0)
                        if s == NG or s == K2:
                            h = 0 if s == NG else 1
                            r = (h + 1) * NG - 1
                            act.wait_ge(used[r % 2], it * PER + (r // 2 + 2))
                            nc.scalar.copy(S[:, bass.ds(it * 2 + h, 1), :], acc[:, h, 0:C].unsqueeze(1)
                                           ).then_inc(kept[h], 1)


def layer1_scores(nc, k, hp, s1):
    NI = k.NI - 1
    grp = groups_of(NI)
    NG = len(grp)
    K2, PER, L = 2 * NG, NG, k.NI // 2
    HP = 3 * HEADS
    with Stage(nc) as ctx:
        def sb(name, shape, dt=F32):
            return ctx.enter_context(nc.sbuf_tensor(f"p3_{name}", shape, dt))

        def ps(name, shape, dt=F32):
            return ctx.enter_context(nc.psum_tensor(f"p3_{name}", shape, dt))

        def sem(name):
            return ctx.semaphore(f"p3_{name}")

        def pair(name):
            return [sem(f"{name}{h}") for h in range(2)]

        win = sb("window", [P, 2, 2, NI], BF16)
        htw = sb("htw", [P, 2, 3, HEADS], BF16)
        oht = sb("oht", [P, 2, 2, GT, P], BF16)
        sm = sb("sm", [P, NI, HEADS])
        tp = ps("tp", [P, 2, 2, GT * P], BF16)
        FIRST = 40
        sp_ = ps("scores", [P, 2, 2, 512])
        staged, tr, ev, gt, kept = (pair(n) for n in ("staged", "turned", "onehot", "gathered", "kept"))
        chain = sem("chain")

        def of(it, r):
            h, g = divmod(r % K2, NG)
            return h, g, *grp[g], r % 2, it * PER + (r // 2 + 1)

        def turn(pe, it, r):
            h, g, i0, w, gp, c = of(it, r)
            if g == 0:
                pe.wait_ge(staged[h], it + (r // K2 + 1))
            pe.wait_ge(ev[gp], c)
            for a in range(2):
                for q in range(w):
                    ins = nc.tensor.transpose(tp[:, gp, a, q * P:(q + 1) * P],
                                              win[:, h, a, i0 + q:i0 + q + 1].to_broadcast([P, P]), k.ident_b[:])
            ins.then_inc(tr[gp], 1)

        def compare(dve, it, r):
            h, g, i0, w, gp, c = of(it, r)
            dve.wait_ge(tr[gp], c + 1)
            dve.wait_ge(gt[gp], c)
            nc.vector.tensor_scalar(oht[:, gp, :, 0:w, :].rearrange("p a w n -> p a (w n)"),
                                    tp[:, gp, :, 0:w * P], k.part[:, 0:1], None, ALU.is_equal).then_inc(ev[gp], 1)

        def gather(pe, it, r):
            h, g, i0, w, gp, c = of(it, r)
            pe.wait_ge(ev[gp], c + 1)
            if g == 0:
                pe.wait_ge(kept[h], it + 1)
            for i in range(i0, i0 + w):
                bank, at = (0, i) if i < FIRST else (1, i - FIRST)
                o = sp_[:, h, bank, at * HP:(at + 1) * HP]
                nc.tensor.matmul(o, oht[:, gp, 0, i - i0, :], hp[:, i, :, C:C + HEADS], start=True, stop=False)
                ins = nc.tensor.matmul(o, oht[:, gp, 1, i - i0, :], htw[:, h], start=False, stop=True)
            ins.then_inc(gt[gp], 1)

        def keep_scores(dve, ch, it, h):
            r = (h + 1) * NG - 1
            dve.wait_ge(gt[r % 2], it * PER + (r // 2 + 2))
            for bank, a, b in ((0, 0, FIRST), (1, FIRST, NI)):
                ins = nc.vector.tensor_reduce(
                    sm[:, a:b, :], sp_[:, h, bank, 0:(b - a) * HP].rearrange(
                        "p (i q e) -> p i e q", q=3, e=HEADS), AX.X, ALU.add)
            ch.link(ins)
            dve.sem_inc(kept[h], 1)
            ch.link(nc.vector.scalar_tensor_tensor(
                out=s1[:, bass.ds(it * 2 + h, 1), 0:NI, :].rearrange("p a i e -> p (a i e)"),
                in0=sm[:].rearrange("p i e -> p (i e)"), scalar=ALPHA,
                in1=sm[:].rearrange("p i e -> p (i e)"), op0=ALU.mult, op1=ALU.max))

        def stage(n, v):
            row = slice(n, n + 1) if isinstance(n, int) else bass.ds(n, 1)
            nc.scalar.copy(win[:, v, 0, :], one(k.SLs[:, row, 0:NI]))
            nc.scalar.copy(win[:, v, 1, :], one(k.SLd[:, row, 0:NI]))
            nc.scalar.copy(htw[:, v], one(hp[:, row, :, C + HEADS:C + 2 * HEADS])).then_inc(staged[v], 1)

        with nc.Block() as block:
            @block.vector
            def _(dve):
                ch = Chain(dve, chain, 2 * 2)
                nc.vector.memset(s1[:, :, NI:, :], 0.0)
                for h in range(2):
                    dve.sem_inc(ev[h], 1)
                    dve.sem_inc(kept[h], 1)
                compare(dve, 0, 0)
                with dve.Fori(0, L) as it:
                    ch.enter(it)
                    for s in range(K2):
                        compare(dve, it, s + 1)
                        if s == NG:
                            keep_scores(dve, ch, it, 0)
                        if s == K2 - 1:
                            keep_scores(dve, ch, it, 1)
                    ch.leave(L)

            @block.tensor
            def _(pe):
                for h in range(2):
                    pe.sem_inc(gt[h], 1)
                    pe.sem_inc(tr[h], 1)
                turn(pe, 0, 0)
                turn(pe, 0, 1)
                with pe.Fori(0, L) as it:
                    for s in range(K2):
                        turn(pe, it, s + 2)
                        gather(pe, it, s)

            @block.scalar
            def _(act):
                stage(0, 0)
                with act.Fori(0, L) as it:
                    for q in range(2):
                        act.wait_ge(tr[q], it * PER + 1)
                        act.wait_ge(gt[q], it * PER + 1)
                    stage(it * 2 + 1, 1)
                    for r in (NG - 2, NG - 1):
                        act.wait_ge(tr[r % 2], it * PER + (r // 2 + 2))
                        act.wait_ge(gt[r % 2], it * PER + (r // 2 + 2))
                    stage((it * 2 + 2) % k.NI, 0)


def layer1_weights(nc, k, s1, pen):
    with Stage(nc) as ctx:
        s = {n: ctx.semaphore("p3b_" + n) for n in ("chain", "top", "all", "neg")}
        top = ctx.enter_context(nc.sbuf_tensor("p3b_top", [P, 2], F32))
        A = k.NI
        flat = s1[:, 0:A].rearrange("p a i e -> p (a i e)")
        with nc.Block() as block:
            @block.vector
            def _(dve):
                ch = Chain(dve, s["chain"])
                ch.link(nc.vector.tensor_scalar(pen[:, 0:A], k.SLs[:, 0:A], 0.0, NEVER, ALU.is_lt, ALU.mult))
                v = s1[:, 0:A].rearrange("p a i e -> p (a i) e")
                ch.link(nc.vector.tensor_tensor(v, v, pen[:, 0:A].rearrange("p a i -> p (a i)").unsqueeze(2)
                                                .to_broadcast([P, A * k.NI, HEADS]), ALU.add))
                nc.vector.tensor_reduce(top[:, 0:1], flat, AX.X, ALU.max).then_inc(s["top"], 1)
                dve.wait_ge(s["all"], 1)
                nc.vector.tensor_scalar(top[:, 1:2], top[:, 1:2], -1.0, None, ALU.mult).then_inc(s["neg"], 1)

            @block.gpsimd
            def _(pool):
                pool.wait_ge(s["top"], 1)
                nc.gpsimd.partition_all_reduce(top[:, 1:2], top[:, 0:1], P, RMAX).then_inc(s["all"], 1)

            @block.scalar
            def _(act):
                act.wait_ge(s["neg"], 1)
                nc.scalar.activation(flat, flat, ACT.Exp, bias=top[:, 1:2])


def layer1_sums(nc, k, hp, s1, S, den4):
    NI = k.NI - 1
    grp = groups_of(NI)
    NG = len(grp)
    K2, PER, L = 2 * NG, NG, k.NI // 2
    CW = C + HEADS
    with Stage(nc) as ctx:
        def sb(name, shape, dt=F32):
            return ctx.enter_context(nc.sbuf_tensor(f"p4_{name}", shape, dt))

        def ps(name, shape, dt=F32):
            return ctx.enter_context(nc.psum_tensor(f"p4_{name}", shape, dt))

        def pair(name):
            return [ctx.semaphore(f"p4_{name}{h}") for h in range(2)]

        win = sb("window", [P, 2, 2, NI], BF16)
        wgt = sb("weights", [P, 2, NI, HEADS])
        ohd = sb("ohd", [P, 2, P, GT], BF16)
        oht = sb("oht", [P, 2, GT, P], BF16)
        ohs = sb("ohs", [P, 2, GT, P])
        msg = sb("msg", [P, 2, GT, CW])
        tp = ps("tp", [P, 2, 2 * GT * P], BF16)
        gps = ps("gathered", [P, 2, GT * P])
        acc = ps("acc", [P, 2, 512])
        staged, gen, tr, ev, gt, ms, ag, kept = (pair(n) for n in (
            "staged", "onehot", "turned", "turned_in_sbuf", "gathered", "messages", "added", "kept"))
        wcp = pair("weights_copied")

        def of(it, r):
            h, g = divmod(r % K2, NG)
            return h, g, *grp[g], r % 2, it * PER + (r // 2 + 1)

        def make(dve, it, r):
            h, g, i0, w, gp, c = of(it, r)
            if g == 0:
                dve.wait_ge(staged[h], it + (r // K2 + 1))
            dve.wait_ge(tr[gp], c)
            nc.vector.tensor_tensor(ohd[:, gp, :, 0:w], k.iota_x[:, :, 0:w],
                                    win[:, h, 1, i0:i0 + w].unsqueeze(1).to_broadcast([P, P, w]),
                                    ALU.is_equal).then_inc(gen[gp], 1)

        def turn(pe, it, r):
            h, g, i0, w, gp, c = of(it, r)
            pe.wait_ge(gen[gp], c + 1)
            pe.wait_ge(ev[gp], c)
            for q in range(w):
                ins = nc.tensor.transpose(tp[:, gp, q * P:(q + 1) * P], ohd[:, gp, :, q], k.ident_b[:])
            ins.then_inc(tr[gp], 1)

        def take_turned(act, it, r):
            h, g, i0, w, gp, c = of(it, r)
            act.wait_ge(tr[gp], c + 1)
            act.wait_ge(gt[gp], c)
            nc.scalar.copy(oht[:, gp].rearrange("p a b -> p (a b)")[:, 0:w * P], tp[:, gp, 0:w * P]
                           ).then_inc(ev[gp], 1)

        def gather(pe, it, r):
            h, g, i0, w, gp, c = of(it, r)
            pe.wait_ge(ev[gp], c + 1)
            pe.wait_ge(ms[gp], c)
            for i in range(w):
                for q in range(3):
                    ins = nc.tensor.matmul(gps[:, gp, i * P:(i + 1) * P], oht[:, gp, i, :],
                                           hp[:, i0 + i, q, 0:C], start=(q == 0), stop=(q == 2))
            ins.then_inc(gt[gp], 1)

        def copy_weights(act, it, r):
            h, g, i0, w, gp, c = of(it, r)
            act.wait_ge(ag[gp], c)
            nc.scalar.copy(msg[:, gp, 0:w, C:CW], wgt[:, h, i0:i0 + w, :]).then_inc(wcp[gp], 1)

        def weigh(dve, it, r):
            h, g, i0, w, gp, c = of(it, r)
            dve.wait_ge(gt[gp], c + 1)
            dve.wait_ge(ag[gp], c)
            nc.vector.tensor_tensor(ohs[:, gp, 0:w, :], k.iota[:].unsqueeze(1).to_broadcast([P, w, P]),
                                    win[:, h, 0, i0:i0 + w].unsqueeze(2).to_broadcast([P, w, P]), ALU.is_equal)
            nc.vector.tensor_tensor(
                msg[:, gp, 0:w, 0:C].rearrange("p w (e d) -> p w e d", e=HEADS),
                gps[:, gp, 0:w * P].rearrange("p (w e d) -> p w e d", w=w, e=HEADS),
                wgt[:, h, i0:i0 + w, :].unsqueeze(3).to_broadcast([P, w, HEADS, D]), ALU.mult).then_inc(ms[gp], 1)

        def add_up(pe, it, r):
            h, g, i0, w, gp, c = of(it, r)
            pe.wait_ge(ms[gp], c + 1)
            pe.wait_ge(wcp[gp], c)
            if g == 0:
                pe.wait_ge(kept[h], it + 1)
            for i in range(w):
                ins = nc.tensor.matmul(acc[:, h, 0:CW], ohs[:, gp, i, :], msg[:, gp, i, :],
                                       start=(i0 + i == 0), stop=(i0 + i == NI - 1))
            ins.then_inc(ag[gp], 1)

        def stage(n, v):
            col = slice(n, n + 1) if isinstance(n, int) else bass.ds(n, 1)
            nc.scalar.copy(win[:, v, 0, :], k.SLs[:, 0:NI, col].rearrange("p a b -> p (a b)"))
            nc.scalar.copy(win[:, v, 1, :], k.SLd[:, 0:NI, col].rearrange("p a b -> p (a b)"))
            nc.scalar.copy(wgt[:, v], s1[:, 0:NI, col, :].rearrange("p a b e -> p a (b e)")).then_inc(staged[v], 1)

        with nc.Block() as block:
            @block.vector
            def _(dve):
                for h in range(2):
                    dve.sem_inc(gen[h], 1)
                    dve.sem_inc(ms[h], 1)
                make(dve, 0, 0)
                make(dve, 0, 1)
                with dve.Fori(0, L) as it:
                    for s in range(K2):
                        make(dve, it, s + 2)
                        weigh(dve, it, s)

            @block.tensor
            def _(pe):
                for h in range(2):
                    pe.sem_inc(tr[h], 1)
                    pe.sem_inc(gt[h], 1)
                    pe.sem_inc(ag[h], 1)
                turn(pe, 0, 0)
                turn(pe, 0, 1)
                gather(pe, 0, 0)
                with pe.Fori(0, L) as it:
                    for s in range(K2):
                        turn(pe, it, s + 2)
                        gather(pe, it, s + 1)
                        add_up(pe, it, s)

            @block.scalar
            def _(act):
                for h in range(2):
                    act.sem_inc(ev[h], 1)
                    act.sem_inc(kept[h], 1)
                stage(0, 0)
                take_turned(act, 0, 0)
                copy_weights(act, 0, 0)
                take_turned(act, 0, 1)
                with act.Fori(0, L) as it:
                    for s in range(K2):
                        if s == 0:
                            for q in range(2):
                                act.wait_ge(ms[q], it * PER + 1)
                            stage(it * 2 + 1, 1)
                        if s == NG + 1:
                            for r in (NG - 2, NG - 1):
                                act.wait_ge(ms[r % 2], it * PER + (r // 2 + 2))
                            stage((it * 2 + 2) % k.NI, 0)
                        take_turned(act, it, s + 2)
                        copy_weights(act, it, s + 1)
                        if s == NG or s == K2 - 1:
                            h = 0 if s == NG else 1
                            r = (h + 1) * NG - 1
                            act.wait_ge(ag[r % 2], it * PER + (r // 2 + 2))
                            nc.scalar.copy(S[:, bass.ds(it * 2 + h, 1), :], acc[:, h, 0:C].unsqueeze(1))
                            nc.scalar.copy(den4[:, bass.ds(it * 2 + h, 1), :], acc[:, h, C:CW].unsqueeze(1)
                                           ).then_inc(kept[h], 1)



G = 8
COPIES = 4


class General:

    def __init__(self, nc, k, ctx, tag, src, dst):
        self.tag = tag
        self.T = src.shape[0] // EP
        self.ITERS = self.T // (2 * G)
        assert self.ITERS * 2 * G == self.T
        self.NP = k.NI * P

        def sb(name, shape, dt=F32):
            return ctx.enter_context(nc.sbuf_tensor(f"{tag}_{name}", shape, dt))

        self.src, self.dst = sb("src", [P, self.T], I32), sb("dst", [P, self.T], I32)
        self.below = sb("below", [P, P])
        self.dummy = sb("own_row", [P, 1])
        self.idx_a, self.idx_b = sb("idx_a", [P, 2, G], U32), sb("idx_b", [P, 2, G], U32)
        self.ga, self.gb = sb("rows_a", [P, 2, G, C]), sb("rows_b", [P, 2, G, C])
        self.wk, self.wk2, self.wk3 = (sb(n, [P, G, C]) for n in ("work1", "work2", "work3"))
        self.bank_a = ctx.enter_context(nc.psum_tensor(f"{tag}_bank_a", [P, 2, 512], F32))
        self.bank_b = ctx.enter_context(nc.psum_tensor(f"{tag}_bank_b", [P, 2, 512], F32))
        self.bank_c = ctx.enter_context(nc.psum_tensor(f"{tag}_bank_c", [P, 512], F32))
        self.turns = ctx.semaphore(f"{tag}_pool_turns")
        self.accs = [nc.dram_tensor(f"{tag}_acc{c}", (self.NP + P, C), F32, kind="Internal").ap()
                     for c in range(COPIES)]
        self.prepare(nc, k, ctx, src, dst)

    def table(self, nc, name, width):
        return nc.dram_tensor(f"{self.tag}_{name}", (self.NP, width), F32, kind="Internal").ap()

    def blocks(self, table):
        return table[0:self.NP].rearrange("(b p) c -> p b c", p=P)

    def prepare(self, nc, k, ctx, src, dst):
        tag = self.tag
        zero = k.S_zero
        ld, zs, ready, io, chain = (ctx.semaphore(f"{tag}_{n}") for n in (
            "loaded", "cleared", "zeros_ready", "part_ready", "part_chain"))
        part_i = ctx.enter_context(nc.sbuf_tensor(f"{tag}_part_i", [P, 1], I32))
        part = ctx.enter_context(nc.sbuf_tensor(f"{tag}_part", [P, 1], F32))
        with nc.Block() as block:
            @block.sync
            def _(sp):
                sp.dma_start(self.src[0:EP, :], src.rearrange("(p t) -> p t", p=EP)).then_inc(ld, 16)
                sp.dma_start(self.dst[0:EP, :], dst.rearrange("(p t) -> p t", p=EP)).then_inc(ld, 16)
                sp.wait_ge(ld, 32)

            @block.scalar
            def _(act):
                act.wait_ge(ready, 1)
                for acc in self.accs:
                    act.dma_start(self.blocks(acc), zero[:]).then_inc(zs, 16)
                act.wait_ge(zs, 16 * COPIES)

            @block.gpsimd
            def _(pool):
                nc.gpsimd.iota(part_i[:], [[1, 1]], base=0, channel_multiplier=1).then_inc(io, 1)

            @block.vector
            def _(dve):
                nc.vector.memset(zero[:], 0.0).then_inc(ready, 1)
                dve.wait_ge(io, 1)
                nc.vector.tensor_copy(part[:], part_i[:]).then_inc(chain, 1)
                dve.wait_ge(chain, 1)
                nc.vector.tensor_scalar(self.dummy[:], part[:], float(self.NP), None, ALU.add)
                nc.vector.tensor_scalar(self.below[:], k.iota[:], part[:, 0:1], None, ALU.is_lt)


def general_project(nc, k, g, name, X, weights, stores):
    width = weights.shape[1]
    tag = f"{g.tag}_{name}"
    with Stage(nc) as ctx:
        def pair(n):
            return [ctx.semaphore(f"{tag}_{n}{h}") for h in range(2)]

        xb, xt = (ctx.enter_context(nc.sbuf_tensor(f"{tag}_{n}", [P, 2, C], F32)) for n in ("block", "turned"))
        stage = ctx.enter_context(nc.sbuf_tensor(f"{tag}_stage", [P, 2, width], F32))
        picked, turned, xt_ok, mul, staged, stored = (pair(n) for n in (
            "picked", "turned_ok", "turned_in_sbuf", "product", "staged", "stored"))
        PER = 16 * len(stores)
        with nc.Block() as block:
            @block.vector
            def _(dve):
                with dve.Fori(0, k.NI // 2) as it:
                    for h in range(2):
                        dve.wait_ge(turned[h], it + 1)
                        nc.vector.tensor_copy(xb[:, h:h + 1, :], X[:, bass.ds(it * 2 + h, 1), :]
                                              ).then_inc(picked[h], 1)

            @block.tensor
            def _(pe):
                for h in range(2):
                    pe.sem_inc(turned[h], 1)
                    pe.sem_inc(mul[h], 1)
                with pe.Fori(0, k.NI // 2) as it:
                    for h in range(2):
                        pe.wait_ge(picked[h], it + 1)
                        pe.wait_ge(xt_ok[h], it + 1)
                        nc.tensor.transpose(g.bank_a[:, h, 0:C], xb[:, h, :], k.ident[:]).then_inc(turned[h], 1)
                        pe.wait_ge(xt_ok[h], it + 2)
                        pe.wait_ge(staged[h], it + 1)
                        nc.tensor.matmul(g.bank_b[:, h, 0:width], xt[:, h, :], weights, start=True, stop=True
                                         ).then_inc(mul[h], 1)

            @block.scalar
            def _(act):
                for h in range(2):
                    act.sem_inc(xt_ok[h], 1)
                    act.sem_inc(staged[h], 1)
                with act.Fori(0, k.NI // 2) as it:
                    for h in range(2):
                        act.wait_ge(turned[h], it + 2)
                        act.wait_ge(mul[h], it + 1)
                        nc.scalar.copy(xt[:, h, :], g.bank_a[:, h, 0:C]).then_inc(xt_ok[h], 1)
                        act.wait_ge(mul[h], it + 2)
                        nc.scalar.copy(stage[:, h, :], g.bank_b[:, h, 0:width]).then_inc(staged[h], 1)
                        act.wait_ge(staged[h], it + 2)
                        for tab, a, b in stores:
                            act.dma_start(tab[bass.ds((it * 2 + h) * P, P)], stage[:, h, a:b]).then_inc(stored[h], 16)
                        act.wait_ge(stored[h], (it + 1) * PER)


def general_scores(nc, k, g, tab_a, tab_b, width, combine, steps):
    with Stage(nc) as ctx:
        def pair(n):
            return [ctx.semaphore(f"{g.tag}_score_{n}{h}") for h in range(2)]

        idx_ready, gathered, used = (pair(n) for n in ("indices", "gathered", "used"))
        chain = ctx.semaphore(f"{g.tag}_score_chain")
        PER = 16 * 2 * G
        with nc.Block() as block:
            @block.scalar
            def _(act):
                with act.Fori(0, g.ITERS) as it:
                    for h in range(2):
                        act.wait_ge(used[h], it + 1)
                        for idx, edges in ((g.idx_a, g.src), (g.idx_b, g.dst)):
                            nc.scalar.copy(idx[0:EP, h, :], edges[0:EP, bass.ds(it * (2 * G) + h * G, G)]
                                           ).then_inc(idx_ready[h], 1)

            @block.gpsimd
            def _(pool):
                with pool.Fori(0, g.ITERS) as it:
                    for h in range(2):
                        pool.wait_ge(idx_ready[h], it * 2 + 2)
                        pool.wait_ge(used[h], it + 1)
                        pool.sem_inc(g.turns, 1)
                        for q in range(G):
                            for rows, idx, tab in ((g.ga, g.idx_a, tab_a), (g.gb, g.idx_b, tab_b)):
                                pool.indirect_dma_start(
                                    out=rows[0:EP, h, q, 0:width], out_offset=None, in_=tab,
                                    in_offset=bass.IndirectOffsetOnAxis(ap=idx[0:EP, h, q:q + 1], axis=0),
                                ).then_inc(gathered[h], 16)

            @block.vector
            def _(dve):
                ch = Chain(dve, chain, 2 * steps)
                for h in range(2):
                    dve.sem_inc(used[h], 1)
                with dve.Fori(0, g.ITERS) as it:
                    ch.enter(it)
                    for h in range(2):
                        dve.wait_ge(gathered[h], (it + 1) * PER)
                        dve.wait_ge(used[1 - h], it + h + 1)
                        combine(ch.link, h, it * (2 * G) + h * G).then_inc(used[h], 1)
                    ch.leave(g.ITERS)


def general_denominators(nc, k, g, weight, heads, prepare_weights, den):
    HI, K = k.NI, 4
    L, W = g.T // (2 * K), heads * HI
    with Stage(nc) as ctx:
        def sb(name, shape, dt=F32):
            return ctx.enter_context(nc.sbuf_tensor(f"{g.tag}_den_{name}", shape, dt))

        def sem(name):
            return ctx.semaphore(f"{g.tag}_den_{name}")

        part_i, lo_f, hi_f = sb("part_i", [P, g.T], I32), sb("lo", [P, g.T]), sb("hi", [P, g.T])
        oh, ohw = sb("oh", [P, 2, K, P]), sb("ohw", [P, 2, K, heads * HI])
        zero = sb("zero", [P, W])
        ready, chain, opened, closed, zeros = (sem(n) for n in ("weights", "chain", "opened", "closed", "zeros"))
        hot, taken = ([sem(f"{n}{h}") for h in range(2)] for n in ("onehot", "taken"))
        with nc.Block() as block:
            @block.scalar
            def _(act):
                prepare_weights().then_inc(ready, 1)

            @block.vector
            def _(dve):
                ch = Chain(dve, chain, 2)
                nc.vector.memset(zero[:], 0.0).then_inc(zeros, 1)
                ch.link(nc.vector.tensor_scalar(part_i[0:EP], g.src[0:EP], P - 1, None, ALU.bitwise_and))
                ch.link(nc.vector.tensor_copy(lo_f[0:EP], part_i[0:EP]))
                ch.link(nc.vector.tensor_scalar(part_i[0:EP], g.src[0:EP], 7, None, ALU.logical_shift_right))
                ch.link(nc.vector.tensor_copy(hi_f[0:EP], part_i[0:EP]))
                dve.wait_ge(ready, 1)
                for h in range(2):
                    dve.sem_inc(hot[h], 1)
                with dve.Fori(0, L) as it:
                    ch.enter(it)
                    for h in range(2):
                        t0 = it * (2 * K) + h * K
                        dve.wait_ge(taken[h], it + 1)
                        dve.wait_ge(hot[1 - h], it + h + 1)
                        nc.vector.tensor_tensor(
                            oh[0:EP, h], k.iota[0:EP].unsqueeze(1).to_broadcast([EP, K, P]),
                            lo_f[0:EP, bass.ds(t0, K)].unsqueeze(2).to_broadcast([EP, K, P]), ALU.is_equal)
                        v = g.wk[0:EP].rearrange("p g c -> p (g c)")[:, 0:K * HI].rearrange("p (k n) -> p k n", k=K)
                        ch.link(nc.vector.tensor_tensor(
                            v, k.iota[0:EP, 0:HI].unsqueeze(1).to_broadcast([EP, K, HI]),
                            hi_f[0:EP, bass.ds(t0, K)].unsqueeze(2).to_broadcast([EP, K, HI]), ALU.is_equal))
                        for q in range(heads):
                            ins = nc.vector.tensor_tensor(
                                ohw[0:EP, h, :, q * HI:(q + 1) * HI], v,
                                weight(q, t0, K).unsqueeze(2).to_broadcast([EP, K, HI]), ALU.mult)
                        ins.then_inc(hot[h], 1)
                    ch.leave(L)
                dve.wait_ge(closed, 1)
                nc.vector.tensor_copy(den[:, 0:W], g.bank_c[:, 0:W])

            @block.tensor
            def _(pe):
                pe.wait_ge(zeros, 1)
                nc.tensor.matmul(g.bank_c[:, 0:W], k.ones[:], zero[:], start=True, stop=False).then_inc(opened, 1)
                for h in range(2):
                    pe.sem_inc(taken[h], 1)
                with pe.Fori(0, L) as it:
                    for h in range(2):
                        pe.wait_ge(hot[h], it + 2)
                        for q in range(K):
                            ins = nc.tensor.matmul(g.bank_c[:, 0:W], oh[0:EP, h, q, :], ohw[0:EP, h, q, 0:W],
                                                   start=False, stop=False)
                        ins.then_inc(taken[h], 1)
                nc.tensor.matmul(g.bank_c[:, 0:W], k.ones[:], zero[:], start=False, stop=True).then_inc(closed, 1)


def general_sums(nc, k, g, table, pick, key, weigh, S, R):
    with Stage(nc) as ctx:
        def sb(name, shape, dt=F32):
            return ctx.enter_context(nc.sbuf_tensor(f"{g.tag}_sum_{name}", shape, dt))

        def sem(name):
            return ctx.semaphore(f"{g.tag}_sum_{name}")

        def pair(name):
            return [sem(f"{name}{h}") for h in range(2)]

        key_f, dup, dmy = sb("key", [P, G]), sb("dup", [P, G]), sb("target", [P, G])
        idx_ready, gathered, msg_ready, diag_ready, rows_ready, same_ready, summed, out_ready = (pair(n) for n in (
            "indices", "gathered", "messages", "diagonals", "key_rows", "targets", "tile_sums", "sums_in_sbuf"))
        scattered = [sem(f"scattered{c}") for c in range(COPIES)]
        chain = sem("chain")
        PER, STEPS = 16 * G, 7
        SPI = 2 * G // COPIES
        key_rows = g.bank_a[0:EP].rearrange("p b n -> p (b n)").rearrange("p (k n) -> p k n", k=G)[:, :, 0:EP]
        sums = g.bank_b[0:EP].rearrange("p b n -> p (b n)").rearrange("p (k n) -> p k n", k=G)

        with nc.Block() as block:
            @block.scalar
            def _(act):
                for h in range(2):
                    act.sem_inc(out_ready[h], 1)
                with act.Fori(0, g.ITERS) as it:
                    for h in range(2):
                        act.wait_ge(msg_ready[h], it + 1)
                        nc.scalar.copy(g.idx_a[0:EP, h, :], pick[0:EP, bass.ds(it * (2 * G) + h * G, G)]
                                       ).then_inc(idx_ready[h], 1)
                    for h in range(2):
                        act.wait_ge(summed[h], it + 2)
                        for c in range(COPIES):
                            act.wait_ge(scattered[c], it * (16 * SPI) + 16)
                        nc.scalar.copy(g.gb[0:EP, h], sums).then_inc(out_ready[h], 1)

            @block.gpsimd
            def _(pool):
                for c in range(COPIES):
                    pool.dma_start(g.accs[c][g.NP:g.NP + P], k.S_zero[:, 0, :]).then_inc(scattered[c], 16)
                with pool.Fori(0, g.ITERS) as it:
                    for h in range(2):
                        pool.wait_ge(idx_ready[h], it + 1)
                        pool.wait_ge(msg_ready[h], it + 1)
                        pool.sem_inc(g.turns, 1)
                        for q in range(G):
                            pool.indirect_dma_start(
                                out=g.ga[0:EP, h, q, :], out_offset=None, in_=table,
                                in_offset=bass.IndirectOffsetOnAxis(ap=g.idx_a[0:EP, h, q:q + 1], axis=0),
                            ).then_inc(gathered[h], 16)
                    for h in range(2):
                        pool.wait_ge(same_ready[h], it + 2)
                        pool.wait_ge(out_ready[h], it + 2)
                        pool.sem_inc(g.turns, 1)
                        for q in range(G):
                            c, n = q % COPIES, (h * G + q) // COPIES
                            pool.wait_ge(scattered[c], it * (16 * SPI) + 16 * (n + 1))
                            pool.sem_inc(g.turns, 1)
                            pool.indirect_dma_start(
                                out=g.accs[c], out_offset=bass.IndirectOffsetOnAxis(ap=g.idx_b[0:EP, h, q:q + 1], axis=0),
                                in_=g.gb[0:EP, h, q, :], in_offset=None, compute_op=ALU.add,
                            ).then_inc(scattered[c], 16)
                for c in range(COPIES):
                    pool.wait_ge(scattered[c], 16 * (SPI * g.ITERS + 1))

            @block.vector
            def _(dve):
                ch = Chain(dve, chain, 2 * STEPS - 2)
                for h in range(2):
                    dve.sem_inc(msg_ready[h], 1)
                    dve.sem_inc(same_ready[h], 1)
                with dve.Fori(0, g.ITERS) as it:
                    ch.enter(it)
                    for h in range(2):
                        t0 = it * (2 * G) + h * G
                        dve.wait_ge(same_ready[1 - h], it + h + 1)
                        ch.link(nc.vector.tensor_copy(key_f[0:EP], key[0:EP, bass.ds(t0, G)]))
                        keys = key_f[0:EP].unsqueeze(2).to_broadcast([EP, G, EP])
                        nc.vector.tensor_tensor(
                            g.wk[0:EP, :, 0:EP], k.ident[0:EP, 0:EP].unsqueeze(1).to_broadcast([EP, G, EP]), keys,
                            ALU.mult).then_inc(diag_ready[h], 1)
                        dve.wait_ge(rows_ready[h], it + 1)
                        dve.wait_ge(summed[1 - h], it + h + 1)
                        ch.link(nc.vector.tensor_tensor(g.wk2[0:EP, :, 0:EP], key_rows, keys, ALU.is_equal))
                        ch.link(nc.vector.tensor_tensor(
                            g.wk[0:EP, :, 0:EP], g.wk2[0:EP, :, 0:EP],
                            g.below[0:EP, 0:EP].unsqueeze(1).to_broadcast([EP, G, EP]), ALU.mult))
                        ch.link(nc.vector.tensor_reduce(dup[0:EP], g.wk[0:EP, :, 0:EP], AX.X, ALU.add))
                        ch.link(nc.vector.tensor_scalar(dmy[0:EP], key_f[0:EP], -1.0, g.dummy[0:EP, 0:1], ALU.mult,
                                                        ALU.add))
                        ch.link(nc.vector.scalar_tensor_tensor(out=dmy[0:EP], in0=dup[0:EP], scalar=1.0, in1=dmy[0:EP],
                                                               op0=ALU.min, op1=ALU.mult))
                        for c in range(COPIES):
                            dve.wait_ge(scattered[c], it * (16 * SPI) + 16)
                        nc.vector.tensor_tensor(g.idx_b[0:EP, h, :], dmy[0:EP], key_f[0:EP], ALU.add
                                                ).then_inc(same_ready[h], 1)
                        dve.wait_ge(gathered[h], (it + 1) * PER)
                        weigh(g.wk3[0:EP], g.ga[0:EP, h], t0).then_inc(msg_ready[h], 1)
                    ch.leave(g.ITERS)

            @block.tensor
            def _(pe):
                for h in range(2):
                    pe.sem_inc(summed[h], 1)
                with pe.Fori(0, g.ITERS) as it:
                    for h in range(2):
                        pe.wait_ge(diag_ready[h], it + 1)
                        half = G // 2
                        for b in range(2):
                            ins = nc.tensor.matmul(
                                g.bank_a[0:EP, b, :].rearrange("p (k n) -> p k n", k=half)[:, :, 0:EP],
                                k.ones[0:EP, 0:EP], g.wk[0:EP, b * half:(b + 1) * half, 0:EP],
                                start=True, stop=True)
                        ins.then_inc(rows_ready[h], 1)
                        pe.wait_ge(msg_ready[h], it + 2)
                        pe.wait_ge(out_ready[1 - h], it + h + 1)
                        for q in range(G):
                            ins = nc.tensor.matmul(sums[:, q, :], g.wk2[0:EP, q, 0:EP], g.wk3[0:EP, q, :],
                                                   start=True, stop=True)
                        ins.then_inc(summed[h], 1)

        first, others, added = sem("first_loaded"), sem("others_loaded"), sem("added")
        with nc.Block() as block:
            @block.sync
            def _(sp):
                sp.dma_start(S[:], g.blocks(g.accs[0])).then_inc(first, 16)
                for c in range(1, COPIES):
                    if c > 1:
                        sp.wait_ge(added, c - 1)
                    sp.dma_start(R[:], g.blocks(g.accs[c])).then_inc(others, 16)
                sp.wait_ge(others, 16 * (COPIES - 1))

            @block.vector
            def _(dve):
                dve.wait_ge(first, 16)
                for c in range(1, COPIES):
                    dve.wait_ge(others, 16 * c)
                    nc.vector.tensor_tensor(S[:], S[:], R[:], ALU.add).then_inc(added, 1)
                    dve.wait_ge(added, c)


def general_layer0(nc, k, src, dst, X, a0, S, R, e0):
    e = e0[:].rearrange("p a b -> p (a b)")
    with Stage(nc) as ctx:
        k.S_zero = S
        g = General(nc, k, ctx, "g0", src, dst)
        p_tab, q_tab, xs_tab = (g.table(nc, n, C) for n in ("p_tab", "q_tab", "xs_tab"))
        a_row = ctx.enter_context(nc.sbuf_tensor("g0_a_row", [P, C], F32))
        den = ctx.enter_context(nc.sbuf_tensor("g0_den", [P, k.NI], F32))
        al, xs_st = ctx.semaphore("g0_a_loaded"), ctx.semaphore("g0_xs_stored")
        with nc.Block() as block:
            @block.sync
            def _(sp):
                sp.dma_start(a_row[:], a0.rearrange("c o -> (c o)").partition_broadcast(P)).then_inc(al, 16)
                sp.wait_ge(al, 16)
        general_project(nc, k, g, "pq", X, k.w0_ext.rearrange("c t o -> c (t o)"), [(p_tab, 0, C), (q_tab, CZ, CZ + C)])

        def combine(link, h, t0):
            link(nc.vector.tensor_tensor(g.wk[0:EP], g.ga[0:EP, h], g.gb[0:EP, h], ALU.add))
            link(nc.vector.scalar_tensor_tensor(out=g.wk2[0:EP], in0=g.wk[0:EP], scalar=ALPHA, in1=g.wk[0:EP],
                                                op0=ALU.mult, op1=ALU.max))
            link(nc.vector.tensor_tensor(g.wk[0:EP], g.wk2[0:EP],
                                         a_row[0:EP, :].unsqueeze(1).to_broadcast([EP, G, C]), ALU.mult))
            return nc.vector.tensor_reduce(e[0:EP, bass.ds(t0, G)], g.wk[0:EP], AX.X, ALU.add)

        general_scores(nc, k, g, p_tab, q_tab, C, combine, 3)
        general_denominators(nc, k, g, lambda q, t0, n: e[0:EP, bass.ds(t0, n)], 1,
                             lambda: nc.scalar.activation(e[0:EP, 0:g.T], e[0:EP, 0:g.T], ACT.Exp), den)
        scale_rows(nc, k, "g0_scale", X, den[:], R)
        with nc.Block() as block:
            @block.sync
            def _(sp):
                sp.dma_start(g.blocks(xs_tab), R[:]).then_inc(xs_st, 16)
                sp.wait_ge(xs_st, 16)

        def weigh(dest, rows, t0):
            return nc.vector.tensor_tensor(dest, rows, e[0:EP, bass.ds(t0, G)].unsqueeze(2).to_broadcast([EP, G, C]),
                                           ALU.mult)

        general_sums(nc, k, g, xs_tab, g.src, g.dst, weigh, S, R)


def general_layer1(nc, k, src, dst, X, S, R, den4):
    with Stage(nc) as ctx:
        k.S_zero = S
        g = General(nc, k, ctx, "g1", src, dst)
        h_tab, st_tab, r_tab = g.table(nc, "h_tab", C), g.table(nc, "st_tab", 2 * HEADS), g.table(nc, "r_tab", C)
        s1 = ctx.enter_context(nc.sbuf_tensor("g1_s1", [P, g.T, HEADS], F32))
        den = ctx.enter_context(nc.sbuf_tensor("g1_den", [P, HEADS * k.NI], F32))
        top = ctx.enter_context(nc.sbuf_tensor("g1_top", [P, 2], F32))
        mx, rl = ctx.semaphore("g1_max"), ctx.semaphore("g1_residual")
        HW = C + 2 * HEADS
        general_project(nc, k, g, "h", X, k.w1_all[:], [(h_tab, 0, C), (st_tab, C, HW), (r_tab, HW, HW + C)])

        def combine(link, h, t0):
            w = g.wk[0:EP, :, 0:HEADS]
            link(nc.vector.tensor_tensor(w, g.ga[0:EP, h, :, 0:HEADS], g.gb[0:EP, h, :, HEADS:2 * HEADS], ALU.add))
            return nc.vector.scalar_tensor_tensor(out=s1[0:EP, bass.ds(t0, G), :], in0=w, scalar=ALPHA, in1=w,
                                                  op0=ALU.mult, op1=ALU.max)

        general_scores(nc, k, g, st_tab, st_tab, 2 * HEADS, combine, 1)
        flat = s1[0:EP].rearrange("p t h -> p (t h)")
        with nc.Block() as block:
            @block.vector
            def _(dve):
                nc.vector.tensor_reduce(top[0:EP, 0:1], flat, AX.X, ALU.max).then_inc(mx, 1)
                dve.wait_ge(mx, 2)
                nc.vector.tensor_scalar(top[0:EP, 1:2], top[0:EP, 1:2], -1.0, None, ALU.mult)

            @block.gpsimd
            def _(pool):
                pool.wait_ge(mx, 1)
                nc.gpsimd.partition_all_reduce(top[0:EP, 1:2], top[0:EP, 0:1], EP, RMAX).then_inc(mx, 1)
        general_denominators(nc, k, g, lambda q, t0, n: s1[0:EP, bass.ds(t0, n), q], HEADS,
                             lambda: nc.scalar.activation(flat, flat, ACT.Exp, bias=top[0:EP, 1:2]), den)

        def weigh(dest, rows, t0):
            w = s1[0:EP, bass.ds(t0, G), :].rearrange("p g h -> p (g h)").unsqueeze(2).to_broadcast([EP, G * HEADS, D])
            return nc.vector.tensor_tensor(dest.rearrange("p g (h d) -> p (g h) d", h=HEADS),
                                           rows.rearrange("p g (h d) -> p (g h) d", h=HEADS), w, ALU.mult)

        general_sums(nc, k, g, h_tab, g.dst, g.src, weigh, S, R)
        with nc.Block() as block:
            @block.sync
            def _(sp):
                sp.dma_start(R[:], g.blocks(r_tab)).then_inc(rl, 16)
                sp.wait_ge(rl, 16)

            @block.vector
            def _(dve):
                nc.vector.tensor_copy(den4[:], den[:].rearrange("p (e b) -> p b e", e=HEADS))


def either(nc, label, value, expected, first, second):
    nc.br_eq(value, expected, on_true=f"{label}_first", on_false=f"{label}_second", engines=ENGINES)
    for arm, steps in (("first", first), ("second", second)):
        with nc.body(f"{label}_{arm}", valid_engines=ENGINES):
            steps()
            nc.br(f"{label}_end", engines=ENGINES)
    nc.switch_bb(f"{label}_end")


def all_binned(nc, k, flag, edges):
    with Stage(nc) as ctx:
        has = ctx.enter_context(nc.sbuf_tensor("has_edge", [P, k.NI, k.NI], BF16))
        count = ctx.enter_context(nc.sbuf_tensor("lane_count", [P, 1], F32))
        psum = ctx.enter_context(nc.psum_tensor("lane_psum", [P, 512], F32))
        chain, counted, summed = (ctx.semaphore("lane_" + n) for n in ("chain", "counted", "summed"))
        with nc.Block() as block:
            @block.vector
            def _(dve):
                nc.vector.tensor_scalar(has[:], k.SLs[:, 0:k.NI], 0.0, None, ALU.is_ge).then_inc(chain, 1)
                dve.wait_ge(chain, 1)
                nc.vector.tensor_reduce(count[:], has[:].rearrange("p a b -> p (a b)"), AX.X, ALU.add).then_inc(counted, 1)
                dve.wait_ge(summed, 1)
                nc.vector.tensor_scalar(flag[:], psum[:, 0:1], float(edges), None, ALU.is_equal)

            @block.tensor
            def _(pe):
                pe.wait_ge(counted, 1)
                nc.tensor.matmul(psum[:, 0:1], k.ones[:], count[:], start=True, stop=True).then_inc(summed, 1)


class Shared:
    pass


def load_constants(nc, k, sb, X, x, w0, a0, w1, a_left, a_right, w_res):
    N = x.shape[0]
    NFULL, NREST = N // P, N % P
    iota_i, part_i, part = sb("iota_i", [P, P], I32), sb("part_i", [P, 1], I32), k.part
    w1_sb, wres_sb, w1_t = sb("w1_sb", [P, C]), sb("wres_sb", [P, C]), sb("w1_t", [P, C])
    a_diag, a_rows, w0_a, w0_dot = sb("a_diag", [P, P]), sb("a_rows", [P, C]), sb("w0_a", [P, 2, C]), sb("w0_dot", [P, 2])
    al_col, al_blk = sb("al_col", [P, 2]), sb("al_blk", [P, 2 * HEADS])
    hm_i, hm_f, headmask = sb("hm_i", [P, 1], I32), sb("hm_f", [P, 1]), sb("headmask", [P, HEADS])
    with Stage(nc) as ctx:
        psum = ctx.enter_context(nc.psum_tensor("const_psum", [P, 512], F32))
        ld, zeroed, io, cst, wt_ready, wt_sb, wa_ready = (ctx.semaphore("const_" + n) for n in (
            "loaded", "zeroed", "iota", "chain", "w_turned", "w_turned_in_sbuf", "w_attention"))
        with nc.Block() as block:
            @block.sync
            def _(sp):
                sp.dma_start(k.w0, w0.rearrange("(t c) o -> c t o", t=2)).then_inc(ld, 16)
                sp.dma_start(w1_sb[:], w1).then_inc(ld, 16)
                sp.dma_start(wres_sb[:], w_res).then_inc(ld, 16)
                sp.dma_start(k.a_col[:], a0).then_inc(ld, 16)
                sp.dma_start(al_col[:, 0:1], a_left.rearrange("h d o -> (h d) o")).then_inc(ld, 16)
                sp.dma_start(al_col[:, 1:2], a_right.rearrange("h d o -> (h d) o")).then_inc(ld, 16)
                sp.dma_start(X[:, 0:NFULL, :], x[0:NFULL * P].rearrange("(b p) c -> p b c", p=P)).then_inc(ld, 16)
                sp.wait_ge(zeroed, 1)
                sp.dma_start(X[0:NREST, NFULL, :], x[NFULL * P:N]).then_inc(ld, 16)
                sp.wait_ge(ld, 128)

            @block.gpsimd
            def _(pool):
                nc.gpsimd.iota(iota_i[:], [[1, P]], base=0, channel_multiplier=0).then_inc(io, 1)
                nc.gpsimd.iota(part_i[:], [[1, 1]], base=0, channel_multiplier=1).then_inc(io, 1)

            @block.vector
            def _(dve):
                ch = Chain(dve, cst)
                nc.vector.memset(X[:, NFULL:k.NI, :], 0.0).then_inc(zeroed, 1)
                nc.vector.memset(k.ones[:], 1.0)
                dve.wait_ge(io, 2)
                nc.vector.tensor_copy(k.iota[:], iota_i[:])
                nc.vector.tensor_copy(k.iota_x[:], iota_i[:].unsqueeze(2).to_broadcast([P, P, GT]))
                ch.link(nc.vector.tensor_copy(part[:], part_i[:]))
                nc.vector.tensor_scalar(k.ident[:], k.iota[:], part[:, 0:1], None, ALU.is_equal)
                nc.vector.tensor_scalar(k.ident_b[:], k.iota[:], part[:, 0:1], None, ALU.is_equal)
                nc.vector.tensor_scalar(k.above_b[:], k.iota[:], part[:, 0:1], None, ALU.is_gt)
                nc.vector.tensor_scalar(k.thr[:], k.iota[:, 0:k.NW], float(P), None, ALU.mult)
                ch.link(nc.vector.tensor_scalar(hm_i[:], part_i[:], D.bit_length() - 1, None, ALU.logical_shift_right))
                ch.link(nc.vector.tensor_copy(hm_f[:], hm_i[:]))
                ch.link(nc.vector.tensor_scalar(headmask[:], k.iota[:, 0:HEADS], hm_f[:, 0:1], None, ALU.is_equal))
                dve.wait_ge(ld, 128)
                nc.vector.tensor_scalar(al_blk[:, 0:HEADS], headmask[:], al_col[:, 0:1], None, ALU.mult)
                nc.vector.tensor_scalar(al_blk[:, HEADS:], headmask[:], al_col[:, 1:2], None, ALU.mult)
                nc.vector.tensor_scalar(a_diag[:], k.ident[:], k.a_col[:], None, ALU.mult)
                nc.vector.memset(k.a_pos[:, C:C + 1], 1.0)
                nc.vector.memset(k.a_pos[:, C + 1:CZ], -1.0)
                nc.vector.tensor_copy(k.w1_all[:, 0:C], w1_sb[:])
                ch.link(nc.vector.tensor_copy(k.w1_all[:, C + 2 * HEADS:], wres_sb[:]))
                dve.wait_ge(wt_ready, 1)
                ch.link(nc.vector.tensor_copy(a_rows[:], psum[:, 2 * C:3 * C]))
                nc.vector.tensor_copy(w1_t[:], psum[:, 0:C]).then_inc(wt_sb, 1)
                nc.vector.tensor_scalar(k.a_pos[:, 0:C], a_rows[:], 1.0 - ALPHA, None, ALU.mult)
                ch.link(nc.vector.tensor_tensor(w0_a[:], k.w0, a_rows[:].unsqueeze(1).to_broadcast([P, 2, C]), ALU.mult))
                ch.link(nc.vector.tensor_reduce(w0_dot[:], w0_a[:], AX.X, ALU.add))
                nc.vector.tensor_scalar(k.w0_ext[:, :, C:C + 1], w0_dot[:].unsqueeze(2), ALPHA, None, ALU.mult)
                nc.vector.tensor_scalar(k.w0_ext[:, :, C + 1:CZ], w0_dot[:].unsqueeze(2), -ALPHA, None, ALU.mult)
                dve.wait_ge(wa_ready, 1)
                nc.vector.tensor_copy(k.w1_all[:, C:C + 2 * HEADS], psum[:, 0:2 * HEADS])

            @block.tensor
            def _(pe):
                pe.wait_ge(cst, 5)
                nc.tensor.matmul(psum[:, 2 * C:3 * C], k.ones[:], a_diag[:], start=True, stop=True)
                nc.tensor.transpose(psum[:, 0:C], w1_sb[:], k.ident[:]).then_inc(wt_ready, 1)
                pe.wait_ge(wt_sb, 1)
                nc.tensor.matmul(psum[:, 0:2 * HEADS], w1_t[:], al_blk[:], start=True, stop=True).then_inc(wa_ready, 1)


def scale_rows(nc, k, tag, X, den, xs):
    NB = k.NI
    with Stage(nc) as ctx:
        scc = ctx.semaphore(f"{tag}_chain")
        rden = ctx.enter_context(nc.sbuf_tensor(f"{tag}_rden", [P, NB], F32))
        with nc.Block() as block:
            @block.vector
            def _(dve):
                ch = Chain(dve, scc)
                ch.link(nc.vector.tensor_scalar(den, den, 1.1754944e-38, None, ALU.max))
                ch.link(nc.vector.reciprocal(rden[:], den))
                nc.vector.tensor_tensor(xs[:], X[:], rden[:].unsqueeze(2).to_broadcast([P, NB, C]), ALU.mult)


def add_and_norm(nc, k, tag, X, S, R, before, out):
    NB = k.NI
    with Stage(nc) as ctx:
        stat = ctx.enter_context(nc.sbuf_tensor(f"{tag}_stat", [P, NB], F32))
        ask = ctx.enter_context(nc.sbuf_tensor(f"{tag}_ask", [P, 1], F32))
        chain, a_req, a_done, fin, st = (ctx.semaphore(f"{tag}_{n}") for n in (
            "chain", "act_asked", "act_done", "finished", "stored"))
        asked = []
        with nc.Block() as block:
            @block.vector
            def _(dve):
                ch = Chain(dve, chain)

                def on_act(emit):
                    asked.append(emit)
                    dve.sem_inc(a_req, 1)
                    dve.wait_ge(a_done, len(asked))

                before(ch.link, on_act)
                ch.link(nc.vector.tensor_tensor(X[:], X[:], S[:], ALU.add))
                ch.link(nc.vector.tensor_reduce(stat[:], X[:], AX.X, ALU.add))
                ch.link(nc.vector.tensor_scalar(stat[:], stat[:], 1.0 / C, None, ALU.mult))
                ch.link(nc.vector.tensor_tensor(X[:], X[:], stat[:].unsqueeze(2).to_broadcast([P, NB, C]), ALU.subtract))
                ch.link(nc.vector.tensor_tensor(S[:], X[:], X[:], ALU.mult))
                ch.link(nc.vector.tensor_reduce(stat[:], S[:], AX.X, ALU.add))
                ch.link(nc.vector.tensor_scalar(stat[:], stat[:], 1.0 / C, LN_EPS, ALU.mult, ALU.add))
                on_act(lambda: nc.scalar.activation(stat[:], stat[:], ACT.Sqrt))
                ch.link(nc.vector.reciprocal(stat[:], stat[:]))
                nc.vector.tensor_tensor(X[:], X[:], stat[:].unsqueeze(2).to_broadcast([P, NB, C]), ALU.mult
                                        ).then_inc(fin, 1)

            @block.scalar
            def _(act):
                for n, emit in enumerate(asked):
                    act.wait_ge(a_req, n + 1)
                    emit().then_inc(a_done, 1)

            @block.sync
            def _(sp):
                if out is not None:
                    N = out.shape[0]
                    NFULL, NREST = N // P, N % P
                    sp.wait_ge(fin, 1)
                    sp.dma_start(out[0:NFULL * P].rearrange("(b p) c -> p b c", p=P), X[:, 0:NFULL, :]).then_inc(st, 16)
                    sp.dma_start(out[NFULL * P:N], X[0:NREST, NFULL, :]).then_inc(st, 16)
                    sp.wait_ge(st, 32)


def gnn_program(nc, x, src, dst, w0, a0, w1, a_left, a_right, w_res, out):
    N, E = x.shape[0], src.shape[0]
    k = Shared()
    k.NI = 2 * (-(-N // (2 * P)))
    k.NW = k.NI + 1
    assert (k.NI - 1) * P >= N and E % (EP * STEP) == 0
    with Stage(nc) as ctx:
        def sb(name, shape, dt=F32):
            return ctx.enter_context(nc.sbuf_tensor(name, shape, dt))

        X = sb("X", [P, k.NI, C])
        k.iota = sb("iota", [P, P])
        k.iota_x = sb("iota_x", [P, P, GT], BF16)
        k.ident, k.ident_b, k.above_b = sb("ident", [P, P]), sb("ident_b", [P, P], BF16), sb("above_b", [P, P], BF16)
        k.part = sb("part", [P, 1])
        k.ones, k.thr = sb("one_mat", [P, P]), sb("thr", [P, k.NW])
        w0x = sb("w0_ext", [P, 2, CZ])
        k.w0_ext, k.w0 = w0x[:], w0x[:, :, 0:C]
        k.a_pos = sb("a_pos", [P, CZ])
        k.w1_all = sb("w1_all", [P, 2 * C + 2 * HEADS])
        k.a_col = sb("a_col", [P, 1])
        k.SLs, k.SLd = sb("SLs", [P, k.NW, k.NI], BF16), sb("SLd", [P, k.NW, k.NI], BF16)
        den = sb("den", [P, k.NI])
        with ExitStack() as scope:
            load_constants(nc, k, lambda n, s, d=F32: scope.enter_context(nc.sbuf_tensor(n, s, d)), X, x, w0, a0, w1,
                           a_left, a_right, w_res)
        e0 = sb("e0", [P, k.NI, k.NI])
        with ExitStack() as scope:
            k.key, k.slo, k.dlo = (scope.enter_context(nc.sbuf_tensor(n, [P, k.NW, W_T], BF16))
                                   for n in ("win_key", "win_slo", "win_dlo"))
            place_windows(nc, k, src, dst)
            pq = scope.enter_context(nc.sbuf_tensor("pq", [P, k.NI, 3, 2 * CZ], BF16))
            project_parts(nc, k, "proj0", X, k.w0_ext.rearrange("c t o -> c (t o)"), 2 * CZ, k.NI, pq, None)
            bin_and_score(nc, k, pq, e0, den)
        flag = sb("flag", [P, 1], I32)
        all_binned(nc, k, flag, E)
        binned = nc.values_load(flag[0:1, 0:1], min_val=0, max_val=1)
        S, R, den4 = sb("S", [P, k.NI, C]), sb("R", [P, k.NI, C]), sb("den4", [P, k.NI, HEADS])

        def binned_layer0():
            scale_rows(nc, k, "scale", X, den[:], R)
            layer0_sums(nc, k, R, e0, S)

        def binned_layer1():
            with ExitStack() as scope:
                hp = scope.enter_context(nc.sbuf_tensor("hp", [P, k.NI, 3, C + 2 * HEADS], BF16))
                s1 = scope.enter_context(nc.sbuf_tensor("s1", [P, k.NI, k.NI, HEADS], F32))
                project_parts(nc, k, "proj1", X, k.w1_all[:], C + 2 * HEADS, k.NI, hp, R)
                layer1_scores(nc, k, hp, s1)
                with nc.sbuf_tensor("penalty", [P, k.NI, k.NI], F32) as pen:
                    layer1_weights(nc, k, s1, pen)
                layer1_sums(nc, k, hp, s1, S, den4)

        either(nc, "layer0", binned, 1, binned_layer0,
               lambda: general_layer0(nc, k, src, dst, X, a0, S, R, e0))
        add_and_norm(nc, k, "norm0", X, S, R, lambda link, on_act: None, None)
        either(nc, "layer1", binned, 1, binned_layer1,
               lambda: general_layer1(nc, k, src, dst, X, S, R, den4))

        def finish(link, on_act):
            link(nc.vector.tensor_scalar(den4[:], den4[:], SM_EPS, None, ALU.add))
            link(nc.vector.reciprocal(den4[:], den4[:]))
            v = S[:].rearrange("p b (e d) -> p (b e) d", e=HEADS)
            link(nc.vector.tensor_tensor(v, v, den4[:].rearrange("p b e -> p (b e)").unsqueeze(2)
                                         .to_broadcast([P, k.NI * HEADS, D]), ALU.mult))
            link(nc.vector.tensor_tensor(S[:], S[:], R[:], ALU.add))
            link(nc.vector.tensor_scalar(R[:], S[:], 0.0, None, ALU.min))
            on_act(lambda: nc.scalar.activation(R[:], R[:], ACT.Exp))
            link(nc.vector.tensor_scalar(R[:], R[:], -1.0, None, ALU.add))
            link(nc.vector.scalar_tensor_tensor(out=S[:], in0=S[:], scalar=0.0, in1=R[:], op0=ALU.max, op1=ALU.add))

        add_and_norm(nc, k, "norm1", X, S, R, finish, out)


_INS = ["x", "src", "dst", "L0_gnn_w", "L0_gnn_a", "L1_gnn_W", "L1_gnn_A_left", "L1_gnn_A_right",
        "L1_gnn_residual_projection"]


def kernel(**inputs):
    import numpy as _np
    import concourse.bacc as _bacc
    from concourse import mybir as _mybir
    from concourse.bass_utils import run_bass_kernel_spmd as _run

    nc = _bacc.Bacc("TRN2", target_bir_lowering=False, num_devices=1)
    arrays, args = {}, []
    for name in _INS:
        a = _np.ascontiguousarray(inputs[name])
        arrays[f"in_{name}_dram"] = a
        args.append(nc.dram_tensor(f"in_{name}_dram", a.shape, _mybir.dt.from_np(a.dtype), kind="ExternalInput").ap())
    n, c = inputs["x"].shape
    args.append(nc.dram_tensor("out_0_dram", (n, c), _mybir.dt.float32, kind="ExternalOutput").ap())
    gnn_program(nc, *args)
    r = _run(nc, [arrays], core_ids=[0])
    return r.results[0]["out_0_dram"]
```
